# Optimizing a Trainium2 kernel written in Bass

```python
import numpy as np
import jax
import jax.numpy as jnp

def _softmax(x, axis=-1):
    return jax.nn.softmax(x, axis=axis)

def _gelu(x):
    return jax.nn.gelu(x, approximate=True)

def _silu(x):
    return jax.nn.silu(x)

def _sigmoid(x):
    return jax.nn.sigmoid(x)

def _layernorm(x, axis=-1, eps=1e-05):
    m = jnp.mean(x, axis=axis, keepdims=True)
    v = jnp.var(x, axis=axis, keepdims=True)
    return (x - m) / jnp.sqrt(v + eps)

def _scatter_add(tgt, idx, src, axis=0):
    return tgt.at[idx].add(src)

def _segment_sum(src, seg, n):
    return jax.ops.segment_sum(src, seg, n)
kernel_name = 'mk_hybrid_d1_jaxref_r8_4c74a6'

def setup_inputs(seed: int=0):
    np.random.seed(seed)
    _w = jnp.asarray

    def _L0_attn_a_setup():
        import jax, jax.numpy as jnp
        import numpy as np
        NUM_HEADS = 16
        EMB = 128
        DH = 64
        B, S = (4, 256)
        key = jax.random.key(seed)
        ks = jax.random.split(key, 9)
        sc = lambda fan_in: 1.0 / np.sqrt(fan_in)
        Wq = jax.random.uniform(ks[0], (NUM_HEADS, EMB, DH), minval=-sc(EMB), maxval=sc(EMB))
        Wk = jax.random.uniform(ks[1], (NUM_HEADS, EMB, DH), minval=-sc(EMB), maxval=sc(EMB))
        Wv = jax.random.uniform(ks[2], (NUM_HEADS, EMB, DH), minval=-sc(EMB), maxval=sc(EMB))
        bq = jax.random.uniform(ks[3], (NUM_HEADS, DH), minval=-sc(EMB), maxval=sc(EMB))
        bk = jax.random.uniform(ks[4], (NUM_HEADS, DH), minval=-sc(EMB), maxval=sc(EMB))
        bv = jax.random.uniform(ks[5], (NUM_HEADS, DH), minval=-sc(EMB), maxval=sc(EMB))
        Wo = jax.random.uniform(ks[6], (NUM_HEADS * DH, EMB), minval=-sc(NUM_HEADS * DH), maxval=sc(NUM_HEADS * DH))
        bo = jax.random.uniform(ks[7], (EMB,), minval=-sc(NUM_HEADS * DH), maxval=sc(NUM_HEADS * DH))
        x = jax.random.normal(ks[8], (B, S, EMB), dtype=jnp.float32)
        return {'x': x, 'Wq': Wq, 'Wk': Wk, 'Wv': Wv, 'bq': bq, 'bk': bk, 'bv': bv, 'Wo': Wo, 'bo': bo}
    _L0_attn_a_in = _L0_attn_a_setup()

    def _L0_attn_b_setup():
        import jax, jax.numpy as jnp
        import numpy as np
        B, S, D = (4, 256, 128)
        SCALE = 1.0 / np.sqrt(D)
        key = jax.random.key(seed)
        k1, k2, k3 = jax.random.split(key, 3)
        x = jax.random.normal(k1, (B, S, D), dtype=jnp.float32)
        bound = 1.0 / np.sqrt(D)
        W_qk = jax.random.uniform(k2, (D, D), minval=-bound, maxval=bound, dtype=jnp.float32)
        W_v = jax.random.uniform(k3, (D, D), minval=-bound, maxval=bound, dtype=jnp.float32)
        alibi_slope = jnp.full((1,), 0.5, dtype=jnp.float32)
        return {'x': x, 'W_qk': W_qk, 'W_v': W_v, 'alibi_slope': alibi_slope}
    _L0_attn_b_in = _L0_attn_b_setup()

    def _L0_ffn_setup():
        import jax, jax.numpy as jnp
        import numpy as np
        B, S, D = (4, 256, 128)
        N_EXPERTS, EXPERT_SIZE = (16, 32)
        WIDTH = N_EXPERTS * EXPERT_SIZE
        key = jax.random.key(seed)
        k_x, k_w1, k_w2, k_g = jax.random.split(key, 4)
        x = jax.random.normal(k_x, (B, S, D), dtype=jnp.float32)
        w1 = jax.random.normal(k_w1, (D, WIDTH), dtype=jnp.float32) / np.sqrt(D).astype(np.float32)
        b1 = jnp.zeros((WIDTH,), dtype=jnp.float32)
        w2 = jax.random.normal(k_w2, (WIDTH, D), dtype=jnp.float32) / np.sqrt(WIDTH).astype(np.float32)
        b2 = jnp.zeros((D,), dtype=jnp.float32)
        return {'x': x, 'w1': w1, 'b1': b1, 'w2': w2, 'b2': b2}
    _L0_ffn_in = _L0_ffn_setup()
    _d = {'L0_attn_a_x': _L0_attn_a_in['x'], 'L0_attn_a_Wq': _L0_attn_a_in['Wq'], 'L0_attn_a_Wk': _L0_attn_a_in['Wk'], 'L0_attn_a_Wv': _L0_attn_a_in['Wv'], 'L0_attn_a_bq': _L0_attn_a_in['bq'], 'L0_attn_a_bk': _L0_attn_a_in['bk'], 'L0_attn_a_bv': _L0_attn_a_in['bv'], 'L0_attn_a_Wo': _L0_attn_a_in['Wo'], 'L0_attn_a_bo': _L0_attn_a_in['bo'], 'L0_attn_b_W_qk': _L0_attn_b_in['W_qk'], 'L0_attn_b_W_v': _L0_attn_b_in['W_v'], 'L0_attn_b_alibi_slope': _L0_attn_b_in['alibi_slope'], 'L0_ffn_w1': _L0_ffn_in['w1'], 'L0_ffn_b1': _L0_ffn_in['b1'], 'L0_ffn_w2': _L0_ffn_in['w2'], 'L0_ffn_b2': _L0_ffn_in['b2']}
    _x0 = _d['L0_attn_a_x']
    _d['L0_attn_a_x'] = jax.random.normal(jax.random.fold_in(jax.random.key(seed), 1), (2, 1024, 128), dtype=_x0.dtype)
    del _x0
    return _d

def reference(L0_attn_a_x, L0_attn_a_Wq, L0_attn_a_Wk, L0_attn_a_Wv, L0_attn_a_bq, L0_attn_a_bk, L0_attn_a_bv, L0_attn_a_Wo, L0_attn_a_bo, L0_attn_b_W_qk, L0_attn_b_W_v, L0_attn_b_alibi_slope, L0_ffn_w1, L0_ffn_b1, L0_ffn_w2, L0_ffn_b2):

    def _L0_attn_a_ref(x, Wq, Wk, Wv, bq, bk, bv, Wo, bo):
        import jax, jax.numpy as jnp
        import numpy as np
        NUM_HEADS = 16
        EMB = 128
        DH = 64
        B, S = (4, 256)
        seq_len = x.shape[1]
        q = jnp.einsum('bse,hed->bhsd', x, Wq) + bq[None, :, None, :]
        k = jnp.einsum('bse,hed->bhsd', x, Wk) + bk[None, :, None, :]
        v = jnp.einsum('bse,hed->bhsd', x, Wv) + bv[None, :, None, :]
        scores = jnp.einsum('bhsd,bhtd->bhst', q, k) / jnp.sqrt(jnp.float32(DH))
        causal = jnp.tril(jnp.ones((seq_len, seq_len), dtype=bool))
        scores = jnp.where(causal[None, None, :, :], scores, -jnp.inf)
        attn = jax.nn.softmax(scores, axis=-1)
        out = jnp.einsum('bhst,bhtd->bhsd', attn, v)
        out = out.transpose(0, 2, 1, 3).reshape(x.shape[0], seq_len, NUM_HEADS * DH)
        return out @ Wo + bo

    def _L0_attn_b_ref(x, W_qk, W_v, alibi_slope):
        import jax, jax.numpy as jnp
        import numpy as np
        B, S, D = (4, 256, 128)
        SCALE = 1.0 / np.sqrt(D)
        seq_len = x.shape[1]
        scores = jnp.einsum('bqe,bke->bqk', x @ W_qk, x) * SCALE
        kpos = jnp.arange(seq_len, dtype=x.dtype)[None, :]
        qpos = jnp.arange(seq_len, dtype=x.dtype)[:, None]
        scores = scores + (kpos - qpos) * alibi_slope[0]
        causal = qpos >= kpos
        scores = jnp.where(causal, scores, -jnp.inf)
        attn = jax.nn.softmax(scores, axis=-1)
        v = x @ W_v.T
        return jnp.einsum('bqk,bkd->bqd', attn, v)

    def _L0_ffn_ref(x, w1, b1, w2, b2):
        import jax, jax.numpy as jnp
        import numpy as np
        B, S, D = (4, 256, 128)
        N_EXPERTS, EXPERT_SIZE = (16, 32)
        WIDTH = N_EXPERTS * EXPERT_SIZE
        h = jax.nn.relu(jnp.einsum('bsd,dw->bsw', x, w1) + b1)
        return jnp.einsum('bsw,wd->bsd', h, w2) + b2
    x = L0_attn_a_x
    x = x + _L0_attn_a_ref(_layernorm(x, axis=-1), L0_attn_a_Wq, L0_attn_a_Wk, L0_attn_a_Wv, L0_attn_a_bq, L0_attn_a_bk, L0_attn_a_bv, L0_attn_a_Wo, L0_attn_a_bo)
    x = x + _L0_ffn_ref(_layernorm(x, axis=-1), L0_ffn_w1, L0_ffn_b1, L0_ffn_w2, L0_ffn_b2)
    x = x + _L0_attn_b_ref(_layernorm(x, axis=-1), L0_attn_b_W_qk, L0_attn_b_W_v, L0_attn_b_alibi_slope)
    x = x + _L0_ffn_ref(_layernorm(x, axis=-1), L0_ffn_w1, L0_ffn_b1, L0_ffn_w2, L0_ffn_b2)
    return x

_drawn_inputs = setup_inputs


def setup_inputs(seed=0):
    import zlib

    import numpy as np

    out = dict(_drawn_inputs(seed))
    spreads = {'L0_ffn_b1': (0.0, 0.1), 'L0_ffn_b2': (0.0, 0.1)}
    factors = {'L0_attn_a_Wq': 4.363,
     'L0_attn_a_Wk': 4.354,
     'L0_attn_a_bq': 8.0,
     'L0_attn_a_bk': 8.0,
     'L0_attn_a_bo': 2.818}
    for name, (base, spread) in spreads.items():
        noise = np.random.default_rng([zlib.crc32(name.encode()), seed]).standard_normal(out[name].shape)
        drawn = base * np.exp(spread * noise) if base else spread * noise
        out[name] = jnp.asarray(drawn.astype(out[name].dtype))
    for name, factor in factors.items():
        out[name] = (out[name] * factor).astype(out[name].dtype)
    return out
```

```python
from contextlib import ExitStack

import concourse.bass as bass
from concourse import mybir

F32 = mybir.dt.float32
F32R = mybir.dt.float32r
F16 = mybir.dt.float16
BF16 = mybir.dt.bfloat16
ALU = mybir.AluOpType
ACT = mybir.ActivationFunctionType
AX_X = mybir.AxisListType.X

P = 128
BANK = 512
NEG = -1.0e30
EPS = 1.0e-5
TINY = 1.0e-30
F16_TOP = 4096.0


def hybrid_block(nc, x, Wq, Wk, Wv, bq, bk, bv, Wo, bo, Wqk, Wv2, slope, w1, b1, w2, b2, out):
    B, S, E = x.shape
    H, _, DH = Wq.shape
    F = w1.shape[1]
    T = B * S
    TILES = T // P
    QT = S // P
    CHUNKS = T // BANK
    CT = BANK // P
    HEADS = B * H
    PAIRS = HEADS // 2
    PP = H // 2
    FW = F // P
    OB = H * DH // P
    VP = 2 * DH + 2
    VW = VP - 1
    V2P = 2 * E + 2
    V2W = V2P - 1
    SCALE_A = float(DH) ** -0.5
    SCALE_B = float(E) ** -0.5
    assert E == P and DH * 2 == P and QT == 8 and F % P == 0 and HEADS == 32

    units, at, units_of = [], [], []
    for i in range(QT):
        at.append(sum(S - P * a for a in range(i)))
        units_of.append([])
        q0 = P * i
        while q0 < S:
            n = BANK - q0 % BANK
            units_of[i].append(len(units))
            units.append((i, q0, n))
            q0 += n
    NU = len(units)
    PCOLS = at[-1] + P
    need_units = [1 + max(r for r, (i, q0, n) in enumerate(units) if i <= j and q0 <= P * j < q0 + n)
                  for j in range(QT)]
    PV_GROUPS = [(0, 1, 2), (3, 4, 5), (6, 7)]
    NG = len(PV_GROUPS)
    GROUP_OF = {j: (g, js.index(j)) for g, js in enumerate(PV_GROUPS) for j in js}
    MAX_AT = [(7,), (6,), (5,), (4,), (3, 2), (1, 0), (), ()]
    MAX_ORDER = [j for js in MAX_AT for j in js]
    PIECE_STEPS = (0, 3)
    MROW_STEP = 6
    RING = 4
    ST_RING = 3

    v_dram = nc.dram_tensor("v_scratch", [HEADS, P, QT * VP], F16, kind="Internal").ap()
    o_dram = nc.dram_tensor("o_scratch", [PAIRS, P, QT, P], F32, kind="Internal").ap()
    x_tok = x.rearrange("b (t p) e -> p (b t) e", p=P)
    out_tok = out.rearrange("b (t p) e -> p (b t) e", p=P)

    start = (nc.sbuf_base + 31) // 32 * 32
    end = nc.sbuf_usable_end
    SIZE = {F32: 4, F32R: 4, F16: 2, BF16: 2}
    places = [start]

    def sb(name, shape, dt):
        n = SIZE[dt]
        for s in shape[1:]:
            n *= s
        offset = places[0]
        places[0] = offset + (n + 31) // 32 * 32
        assert places[0] <= end, (name, places[0], end)
        return nc.alloc_sbuf_tensor_at(name, shape, dt, offset=offset)

    x_sb = sb("x_sb", [P, TILES, E], F32)
    xT_hi = sb("xT_hi", [P, T], F32R)
    xT_lo = sb("xT_lo", [P, T], F32R)
    xn = sb("xn", [P, 2, CT, E], F32)
    stats = sb("stats", [P, TILES, 6], F32)
    mean_var = sb("mean_var", [P, TILES, 2], F32)
    var_eps = sb("var_eps", [P, TILES], F32)
    rstd = sb("rstd", [P, TILES], F32)
    minus_half = sb("minus_half", [P, CT], F32)
    ident = sb("ident", [P, P], F32)
    ident_b = sb("ident_b", [P, P], BF16)
    ones = sb("ones", [P, P], F32)
    wo_hi = sb("wo_hi", [P, OB, E], F32R)
    wo_lo = sb("wo_lo", [P, OB, E], F32R)
    w1_hi = sb("w1_hi", [P, F], F32R)
    w1_lo = sb("w1_lo", [P, F], F32R)
    w2_hi = sb("w2_hi", [P, FW, E], F32R)
    w2_lo = sb("w2_lo", [P, FW, E], F32R)
    b1_sb = sb("b1_sb", [P, FW], F32)
    b2_sb = sb("b2_sb", [P, 1], F32)
    bo_sb = sb("bo_sb", [P, 1], F32)
    bv_sb = sb("bv_sb", [P, OB], F32)
    bo_all = sb("bo_all", [P, 1], F32)
    l1_rows = sb("l1_rows", [P, OB], F32)
    shared = places[0]

    k_hh = sb("k_hh", [P, 4, S], F32R)
    q_hl = sb("q_hl", [P, 4, S], F32R)
    k_l1 = sb("k_l1", [P, 4, S], F32R)
    q_hm = sb("q_hm", [P, 4, S], F32R)
    st_hi = sb("st_hi", [P, 2, S], F32R)
    st_lo = sb("st_lo", [P, 2, S], F32R)
    w_raw = sb("w_raw", [P, 2, P], F32)
    w_hi = sb("w_hi", [P, 2, 2, P], F32R)
    w_lo = sb("w_lo", [P, 2, 2, P], F32R)
    w_b = sb("w_b", [P, 2, 2], F32)
    p_hl = sb("p_hl", [P, 2, 2, PCOLS], F16)
    mask_s = sb("mask_s", [P, S], F32)
    mask_t = sb("mask_t", [P, P], BF16)
    maxima = sb("maxima", [P, 2, QT], F32)
    max_junk = sb("max_junk", [P, S], BF16)
    gate = sb("gate", [P, 1], F32)
    neg_diag = sb("neg_diag", [QT, QT], F32)
    before_slots = places[0]
    p32 = sb("p32", [P, RING, BANK], F32)
    v_sb = sb("v_sb", [P, 2, QT, VP], F16)
    o_sb = sb("o_sb", [P, 2, QT, P], F32)
    o_sum = sb("o_sum", [P, 2, 3, DH], F32)
    o_den = sb("o_den", [P, 2, 3], F32)

    VH = H // 2
    VN = VH * QT * VP
    p_flat = p_hl[:, :, :, :].rearrange("p a b n -> p (a b n)")
    v_stage = [p_flat[:, n * VN:(n + 1) * VN].rearrange("p (h t c) -> p h t c", h=VH, t=QT) for n in range(2)]

    places[0] = before_slots
    wv_raw = sb("wv_raw", [P, H * DH], F32)
    wv_abs = sb("wv_abs", [P, H * DH], F32)
    wv_gain = sb("wv_gain", [P, H * DH], F32)
    wv_hi = sb("wv_hi", [P, H * DH], F32R)
    wv_lo = sb("wv_lo", [P, H * DH], F32R)
    wo_raw = sb("wo_raw", [P, OB, E], F32)
    w1_raw = sb("w1_raw", [P, F], F32)
    w2_raw = sb("w2_raw", [P, FW, E], F32)

    places[0] = shared
    o_in = sb("o_in", [P, 2, OB, CT, P], F32)
    oT_hi = sb("oT_hi", [P, 2, BANK], F32R)
    oT_lo = sb("oT_lo", [P, 2, BANK], F32R)
    h32 = sb("h32", [P, 2, BANK], F32)
    h_hi = sb("h_hi", [P, 2, BANK], F32R)
    h_lo = sb("h_lo", [P, 2, BANK], F32R)
    yT = sb("yT", [P, 2, BANK], F32)
    qb_hi = sb("qb_hi", [P, T], F32R)
    qb_lo = sb("qb_lo", [P, T], F32R)
    v2_sb = sb("v2_sb", [P, TILES, V2P], F16)
    qm_b = sb("qm_b", [P, B, S], F32R)
    k_one = sb("k_one", [P, P], F32R)
    s32 = sb("s32", [P, 3, BANK], F32)
    p32b = sb("p32b", [P, RING, BANK], F32)
    p_hlb = sb("p_hlb", [P, 2, PCOLS], F16)
    bias_s = sb("bias_s", [P, S], F32)
    bias_t = sb("bias_t", [P, S], F32)
    junk_b = sb("junk_b", [P, S], BF16)
    max_b = sb("max_b", [P, B, QT], F32)
    neg_diag_b = sb("neg_diag_b", [QT, QT], F32)
    slope_sb = sb("slope_sb", [P, 1], F32)
    wqk_raw = sb("wqk_raw", [P, E], F32)
    wqk_hi = sb("wqk_hi", [P, E], F32R)
    wqk_lo = sb("wqk_lo", [P, E], F32R)
    wv2_raw = sb("wv2_raw", [P, E], F32)
    wv2_abs = sb("wv2_abs", [P, E], F32)
    wv2_hi = sb("wv2_hi", [P, E], F32R)
    wv2_lo = sb("wv2_lo", [P, E], F32R)
    l1_b = sb("l1_b", [P, 3], F32)
    diag_b = sb("diag_b", [P, E], F32)
    l1_cols = sb("l1_cols", [P, E], F32)
    ob_sum = sb("ob_sum", [P, 2, E], F32)
    ob_den = sb("ob_den", [P, 2], F32)
    ob_out = sb("ob_out", [P, 2, E], F32)

    ctx = ExitStack()
    with ctx:
        psum = ctx.enter_context(nc.psum_tensor("psum", [P, 8 * BANK], F32))

        def bank(n, cols=BANK):
            return psum[:, n * BANK:n * BANK + cols]

        MAXB, PVB, MISC = 3, 5, 7

        def sem(name):
            return ctx.enter_context(nc.semaphore(name))

        x_in = [sem(f"x_in{g}") for g in range(CHUNKS)]
        wv_in, wo_in, ffn_in, bias_in = sem("wv_in"), sem("wo_in"), sem("ffn_in"), sem("bias_in")
        pair_in, attn_b_in = sem("pair_in"), sem("attn_b_in")
        v_in = [sem("v_in0"), sem("v_in1")]
        o_back = [sem("o_back0"), sem("o_back1")]
        scratch_out = [sem("scratch_out0"), sem("scratch_out1")]
        result_out = sem("result_out")
        zeroed, ident_ready, half_ready, ones_ready = sem("zeroed"), sem("ident_ready"), sem("half_ready"), sem("ones_ready")
        tri_ready, diag_ready, rows_ready = sem("tri_ready"), sem("diag_ready"), sem("rows_ready")
        bn_done, aggr_done, eps_done, rstd_done = sem("bn_done"), sem("aggr_done"), sem("eps_done"), sem("rstd_done")
        xn_ready, xt_full, xt_hi_done, xt_lo_done = sem("xn_ready"), sem("xt_full"), sem("xt_hi_done"), sem("xt_lo_done")
        abs_done, l1_full, gain_sum, gain_done = sem("abs_done"), sem("l1_full"), sem("gain_sum"), sem("gain_done")
        wv_scaled, wv_hi_done, wv_lo_done = sem("wv_scaled"), sem("wv_hi_done"), sem("wv_lo_done")
        l1r_full, l1r_done, wo_scaled = sem("l1r_full"), sem("l1r_done"), sem("wo_scaled")
        bo_full, wts_hi_done, wts_lo_done = sem("bo_full"), sem("wts_hi_done"), sem("wts_lo_done")
        v_full, v_hi_done, v_lo_done, v_one = sem("v_full"), sem("v_hi_done"), sem("v_lo_done"), sem("v_one")
        split_hi, split_lo = sem("split_hi"), sem("split_lo")
        piece_full, piece_hi, piece_lo = sem("piece_full"), sem("piece_hi"), sem("piece_lo")
        k_moved = [sem("k_moved0"), sem("k_moved1")]
        q_moved = [sem("q_moved0"), sem("q_moved1")]
        max_full, max_done, mt_full, mrow_done = sem("max_full"), sem("max_done"), sem("mt_full"), sem("mrow_done")
        st_full, exp_done, phi_done, plo_done = sem("st_full"), sem("exp_done"), sem("phi_done"), sem("plo_done")
        pv_done, o_summed, o_read, o_ready = sem("pv_done"), sem("o_summed"), sem("o_read"), sem("o_ready")
        ot_full, ot_hi_done, ot_lo_done, ot_used = sem("ot_full"), sem("ot_hi_done"), sem("ot_lo_done"), sem("ot_used")
        yT_ready, yt_full, res_done = sem("yT_ready"), sem("yt_full"), sem("res_done")
        h_full, h32_done, h_hi_done, h_lo_done, h_used = (
            sem("h_full"), sem("h32_done"), sem("h_hi_done"), sem("h_lo_done"), sem("h_used"))
        steps_b, bias_made, bias_ready, rows_b = sem("steps_b"), sem("bias_made"), sem("bias_ready"), sem("rows_b")
        wqk_hi_done, wqk_split = sem("wqk_hi_done"), sem("wqk_split")
        l1b_made, wv2_scaled, wv2_t, wv2_hi_done, wv2_split = (
            sem("l1b_made"), sem("wv2_scaled"), sem("wv2_t"), sem("wv2_hi_done"), sem("wv2_split"))
        diagb_made, l1c_full, l1c_done = sem("diagb_made"), sem("l1c_full"), sem("l1c_done")
        qb_full, qb_hi_done, qb_lo_done = sem("qb_full"), sem("qb_hi_done"), sem("qb_lo_done")
        v2_full, v2_hi_done, v2_lo_done, v2_one = sem("v2_full"), sem("v2_hi_done"), sem("v2_lo_done"), sem("v2_one")
        maxb_full, maxb_done, mtb_full, mrowb_done = sem("maxb_full"), sem("maxb_done"), sem("mtb_full"), sem("mrowb_done")
        sb_full, s32_done, expb_done, phib_done, plob_done = (
            sem("sb_full"), sem("s32_done"), sem("expb_done"), sem("phib_done"), sem("plob_done"))
        pvb_done, ob_steps, ob_read, resb_done = sem("pvb_done"), sem("ob_steps"), sem("ob_read"), sem("resb_done")

        LOOPS = (HEADS - 4) // 4
        LAST_SLOTS = range(1, 4)

        def pieces_after(t, k):
            if isinstance(t, int):
                return min(2 * (4 * t + k) + 8, 4 * PAIRS)
            return 8 * t + (2 * k + 8)

        def set_of(k, offset=0):
            return (k + offset) % 4

        block = ctx.enter_context(nc.Block())

        @block.sync
        def _(sp):
            wk_pair = Wk.rearrange("(q a) e d -> q e a d", a=2)
            wq_pair = Wq.rearrange("(q a) e d -> q e a d", a=2)
            bk_pair = bk.rearrange("(q a) d -> q (a d)", a=2)
            bq_pair = bq.rearrange("(q a) d -> q (a d)", a=2)

            def load_biases(q, par):
                for which, b in enumerate((bk_pair, bq_pair)):
                    sp.dma_start(w_b[:, par, which:which + 1], b[q].unsqueeze(1)).then_inc(pair_in, 16)

            def load_weights(q):
                for which, w in enumerate((wk_pair, wq_pair)):
                    sp.dma_start(w_raw[:, which, :].rearrange("p (a d) -> p a d", a=2), w[q]).then_inc(pair_in, 16)

            def move_k(par, s):
                rows = slice(DH * par, DH * par + DH)
                hi, lo = st_hi[rows, 0, :].bitcast(F32), st_lo[rows, 0, :].bitcast(F32)
                sp.dma_start(k_hh[0:DH, s, :].bitcast(F32), hi).then_inc(k_moved[par], 16)
                sp.dma_start(k_hh[DH:P, s, :].bitcast(F32), hi).then_inc(k_moved[par], 16)
                sp.dma_start(k_l1[0:DH, s, :].bitcast(F32), lo).then_inc(k_moved[par], 16)

            def move_q(par, s):
                rows = slice(DH * par, DH * par + DH)
                hi, lo = st_hi[rows, 1, :].bitcast(F32), st_lo[rows, 1, :].bitcast(F32)
                sp.dma_start(q_hl[0:DH, s, :].bitcast(F32), hi).then_inc(q_moved[par], 16)
                sp.dma_start(q_hl[DH:P, s, :].bitcast(F32), lo).then_inc(q_moved[par], 16)
                sp.dma_start(q_hm[0:DH, s, :].bitcast(F32), hi).then_inc(q_moved[par], 16)

            for g in range(CHUNKS):
                sp.dma_start(x_sb[:, CT * g:CT * (g + 1), :], x_tok[:, CT * g:CT * (g + 1), :]).then_inc(x_in[g], 16)
                if g == 0:
                    load_weights(0)
                    load_biases(0, 0)
            sp.wait_ge(rows_ready, 1)
            for pair in range(2):
                sp.wait_ge(split_lo, pair + 1)
                if pair == 1:
                    sp.wait_ge(piece_lo, 4)
                load_biases(pair + 1, (pair + 1) % 2)
                load_weights(pair + 1)
                sp.wait_ge(piece_lo, 4 * pair + 2)
                for par in range(2):
                    move_k(par, 2 * pair + par)
                sp.wait_ge(piece_lo, 4 * pair + 4)
                for par in range(2):
                    move_q(par, 2 * pair + par)
            sp.wait_ge(v_one, 1)
            for n in range(2 * B):
                sp.wait_ge(v_lo_done, QT * (n + 1))
                h0 = (n % B) * H + (n // B) * VH
                sp.dma_start(v_dram[h0:h0 + VH].rearrange("h p n -> p h n"),
                             v_stage[n % 2].rearrange("p h t c -> p h (t c)")).then_inc(scratch_out[n % 2], 16)
            for n in range(2):
                sp.wait_ge(scratch_out[n], 16 * B)
            sp.wait_ge(wts_lo_done, 3)

            def fixed(value):
                return value if isinstance(value, int) else sp.snap(value)

            def sp_slot(t, k, project):
                u = fixed(4 * t + k)
                scored, pair = fixed(NU * u), fixed(2 * t + (k + 5) // 2)
                earlier, index, projected = fixed(4 * (pair - 1)), fixed(pair % PP), fixed(pieces_after(t, k))
                stored, pair_out = fixed(NG * (4 * t + k)), fixed(2 * t + (k // 2 - 1))
                if k or not isinstance(t, int):
                    sp.wait_ge(st_full, scored)
                sp.dma_start(v_sb[:, k % 2, :, :].rearrange("p t c -> p (t c)"), v_dram[u]).then_inc(v_in[k % 2], 16)
                if project and k % 2 == 1:
                    sp.wait_ge(piece_lo, earlier)
                    load_biases(index, ((k + 5) // 2) % 2)
                    sp.wait_ge(split_lo, pair)
                    load_weights(index)
                    sp.wait_ge(piece_lo, projected)
                    move_k(0, set_of(k, 3))
                if project and k % 2 == 0 and k:
                    move_k(1, set_of(k, 3))
                    sp.wait_ge(piece_lo, projected)
                    move_q(0, set_of(k, 2))
                    move_q(1, set_of(k, 3))
                if k % 2 == 0 and k:
                    store_pair(k, stored, pair_out)

            def store_pair(k, stored, index):
                sp.wait_ge(o_ready, stored)
                par = (k // 2 - 1) % 2
                sp.dma_start(o_dram[index], o_sb[:, par, :, :]).then_inc(scratch_out[par], 16)

            sp_slot(0, 0, True)
            with sp.Fori(0, LOOPS) as t:
                for k in range(1, 5):
                    sp_slot(t, k, True)
            for k in LAST_SLOTS:
                sp_slot(LOOPS, k, False)
            store_pair(4, NG * HEADS, PAIRS - 1)

            for n in range(2):
                sp.wait_ge(scratch_out[n], 16 * (B + PAIRS // 2))
            sp.wait_ge(plo_done, NU * HEADS)
            sp.dma_start(wqk_raw[:, :], Wqk).then_inc(attn_b_in, 16)
            sp.dma_start(wv2_raw[:, :], Wv2).then_inc(attn_b_in, 16)
            sp.dma_start(slope_sb[:, :], slope.partition_broadcast(P)).then_inc(attn_b_in, 16)
            for c in range(CHUNKS):
                if c >= 2:
                    sp.wait_ge(ot_full, OB * (c - 1))
                b, t0 = c * CT // QT, c * CT % QT
                sp.dma_start(o_in[:, c % 2], o_dram[PP * b:PP * (b + 1), :, t0:t0 + CT, :].rearrange("h p t n -> p h t n"))\
                    .then_inc(o_back[c % 2], 16)
            for c in range(CHUNKS):
                sp.wait_ge(res_done, 2 * CHUNKS + c + 1)
                sp.dma_start(out_tok[:, CT * c:CT * (c + 1), :], x_sb[:, CT * c:CT * (c + 1), :]).then_inc(result_out, 16)
            sp.wait_ge(result_out, 16 * CHUNKS)

        @block.tensor
        def _(pe):
            def three(dst, hi, lo, m_hi, m_lo, start=True, stop=True):
                nc.tensor.matmul(dst, hi, m_hi, start=start, stop=False)
                nc.tensor.matmul(dst, lo, m_hi, start=False, stop=False)
                return nc.tensor.matmul(dst, hi, m_lo, start=False, stop=stop)

            def turn_chunk(n):
                pe.wait_ge(xn_ready, n + 1)
                if n >= 2:
                    pe.wait_ge(xt_lo_done, n - 1)
                for j in range(CT):
                    last = nc.tensor.transpose(bank(6 + n % 2)[:, P * j:P * (j + 1)], xn[:, n % 2, j, :], ident[:, :])
                last.then_inc(xt_full, 1)

            pe.wait_ge(ident_ready, 2)
            for c in range(CHUNKS):
                turn_chunk(c)
            pe.wait_ge(abs_done, 1)
            pe.wait_ge(ones_ready, 1)
            for n in range(2):
                last = nc.tensor.matmul(bank(MAXB + n), ones[:, :], wv_abs[:, BANK * n:BANK * (n + 1)], start=True, stop=True)
            last.then_inc(l1_full, 1)
            for k in range(OB):
                last = nc.tensor.matmul(bank(PVB)[:, k:k + 1], wv_abs[:, P * k:P * (k + 1)], ones[:, 0:1], start=True, stop=True)
            last.then_inc(l1r_full, 1)
            pe.wait_ge(wo_in, 16)
            pe.wait_ge(bias_in, 64)
            pe.wait_ge(xt_lo_done, CHUNKS)
            for k in range(OB):
                last = nc.tensor.matmul(bank(PVB + 1)[:, 0:1], wo_raw[:, k, :], bv_sb[:, k:k + 1], start=(k == 0), stop=(k == OB - 1))
            last.then_inc(bo_full, 1)

            def piece(n, pair, par, which, half, b):
                pe.wait_ge(piece_lo, n)
                pe.wait_ge(split_lo, pair + 1)
                cols = slice(S * b + BANK * half, S * b + BANK * (half + 1)) if isinstance(b, int) else bass.ds(b * S + BANK * half, BANK)
                three(bank(MISC), w_hi[:, par, which, :], w_lo[:, par, which, :], xT_hi[:, cols], xT_lo[:, cols]).then_inc(piece_full, 1)

            for n in range(8):
                if n == 0:
                    pe.wait_ge(split_lo, 1)
                    three(bank(MISC), w_hi[:, 0, 0, :], w_lo[:, 0, 0, :], xT_hi[:, 0:BANK], xT_lo[:, 0:BANK]).then_inc(piece_full, 1)
                else:
                    piece(n, n // 4, n // 4, n % 4 // 2, n % 2, 0)

            pe.wait_ge(wv_lo_done, 1)
            n = 0
            for half in range(2):
                cols = slice(BANK * half, BANK * (half + 1))
                for tile in range(TILES):
                    if n >= ST_RING:
                        pe.wait_ge(v_lo_done, n - ST_RING + 1)
                    rows = slice(P * tile, P * (tile + 1))
                    three(bank(n % ST_RING), xT_hi[:, rows], xT_lo[:, rows], wv_hi[:, cols], wv_lo[:, cols]).then_inc(v_full, 1)
                    n += 1

            def max_tile(v, n, s):
                j = MAX_ORDER[n]
                if not (isinstance(v, int) and v == 0 and n == 0):
                    pe.wait_ge(max_done, QT * v + n)
                cols = P * (j + 1)
                for c0 in range(0, cols, BANK):
                    c1 = min(c0 + BANK, cols)
                    last = nc.tensor.matmul(psum[:, MAXB * BANK + c0:MAXB * BANK + c1], q_hl[:, s, P * j:P * (j + 1)], k_hh[:, s, c0:c1],
                                            start=True, stop=True)
                last.then_inc(max_full, 1)

            def turn_maxima(v, par, pieces):
                pe.wait_ge(max_done, QT * (v + 1))
                pe.wait_ge(piece_lo, pieces)
                nc.tensor.transpose(bank(MISC)[0:QT, 0:P], maxima[:, par, :], ident[:, :]).then_inc(mt_full, 1)

            def outputs(w, k, j, uses):
                par = (k - 1) % 2
                g, r = GROUP_OF[j]
                if j == 0:
                    pe.wait_ge(v_in[par], 16 * (uses + 1))
                pe.wait_ge(plo_done, NU * w + need_units[j])
                if r == 0:
                    pe.wait_ge(o_read, NG * w + (g + 1))
                dst = bank(PVB + (par + g) % 2)[:, VW * r:VW * (r + 1)]
                for kt in range(j + 1):
                    cols = slice(at[kt] + P * (j - kt), at[kt] + P * (j - kt + 1))
                    nc.tensor.matmul(dst, p_hl[:, par, 0, cols], v_sb[:, par, kt, 0:VW], start=(kt == 0), stop=False)
                    last = nc.tensor.matmul(dst[:, DH:VW], p_hl[:, par, 1, cols], v_sb[:, par, kt, DH:VW], start=False, stop=(kt == j))
                last.then_inc(pv_done, 1)

            def scores(u, k, i, r):
                _, q0, n = units[r]
                s = set_of(k)
                if r >= ST_RING or not (isinstance(u, int) and u == 0):
                    pe.wait_ge(phi_done, NU * u + (r - ST_RING + 1))
                if r == 0:
                    pe.wait_ge(mrow_done, u + 1)
                keys = slice(P * i, P * (i + 1))
                dst = bank(r % ST_RING, n)
                diagonal = q0 == P * i
                nc.tensor.matmul(dst, k_hh[:, s, keys], q_hl[:, s, q0:q0 + n], start=True, stop=False)
                last = nc.tensor.matmul(dst, k_l1[:, s, keys], q_hm[:, s, q0:q0 + n], start=False, stop=not diagonal)
                if diagonal:
                    last = nc.tensor.matmul(dst[:, 0:P], ident_b[:, :], mask_t[:, :], start=False, stop=True)
                last.then_inc(st_full, 1)

            def pe_slot(t, k, project, maximum):
                u = 4 * t + k
                for i in range(QT):
                    if maximum:
                        if i == 0:
                            par, count = (k + 1) % 2, 2 * t + (k + 1) // 2 + 1
                            pe.wait_ge(k_moved[par], 48 * count)
                            pe.wait_ge(q_moved[par], 48 * count)
                        for j in MAX_AT[i]:
                            max_tile(u + 1, MAX_ORDER.index(j), set_of(k, 1))
                    if project and i in PIECE_STEPS:
                        half = PIECE_STEPS.index(i)
                        if half == 0:
                            pe.wait_ge(mrow_done, u + 1)
                        piece(2 * u + (6 + half), 2 * t + (k + 3) // 2, ((k + 3) // 2) % 2, (k + 1) % 2, half, (t + 1) // (PP // 2))
                    if not (isinstance(u, int) and u == 0):
                        outputs(u - 1, k, i, 2 * t + (k - 1) // 2)
                    for r in units_of[i]:
                        scores(u, k, i, r)
                    if maximum and i == MROW_STEP:
                        turn_maxima(u + 1, (k + 1) % 2, pieces_after(t, k))

            pe.wait_ge(gain_sum, 2)
            pe.wait_ge(k_moved[0], 48)
            pe.wait_ge(q_moved[0], 48)
            for n in range(QT):
                max_tile(0, n, 0)
            turn_maxima(0, 0, 8)
            pe.wait_ge(rows_ready, 1)
            pe.wait_ge(tri_ready, 2)
            pe.wait_ge(v_lo_done, 2 * TILES)

            pe_slot(0, 0, False, True)
            with pe.Fori(0, LOOPS) as t:
                for k in range(1, 5):
                    pe_slot(t, k, True, True)
            for k in LAST_SLOTS:
                pe_slot(LOOPS, k, False, k < 3)
            for j in range(QT):
                outputs(HEADS - 1, 4, j, PAIRS - 1)

            def turn_result(n):
                pe.wait_ge(yT_ready, n + 1)
                if n >= 2:
                    pe.wait_ge(res_done, n - 1)
                for j in range(CT):
                    last = nc.tensor.transpose(bank(4 + n % 2)[:, P * j:P * (j + 1)], yT[:, n % 2, P * j:P * (j + 1)], ident[:, :])
                last.then_inc(yt_full, 1)

            pe.wait_ge(o_read, 2 + NG * HEADS)
            pe.wait_ge(phi_done, NU * HEADS)
            for c in range(CHUNKS):
                pe.wait_ge(o_back[c % 2], 16 * (c // 2 + 1))
                for blk in range(OB + 1):
                    n = OB * c + blk
                    if blk < OB:
                        if n >= 2:
                            pe.wait_ge(ot_lo_done, n - 1)
                        for j in range(CT):
                            last = nc.tensor.transpose(bank(n % 2)[:, P * j:P * (j + 1)], o_in[:, c % 2, blk, j, :], ident[:, :])
                        last.then_inc(ot_full, 1)
                    if blk >= 1:
                        pe.wait_ge(ot_lo_done, n)
                        if blk == 1 and c >= 2:
                            pe.wait_ge(yT_ready, c - 1)
                        m = (n - 1) % 2
                        last = three(bank(2 + c % 2), wo_hi[:, blk - 1, :], wo_lo[:, blk - 1, :], oT_hi[:, m, :], oT_lo[:, m, :],
                                     start=(blk == 1), stop=(blk == OB))
                        last.then_inc(ot_used, 1)
                    if blk == 3 and c >= 1:
                        turn_result(c - 1)

            def feed_forward(layer, c):
                fc = CHUNKS * layer + c
                y = CHUNKS + fc
                cols = slice(BANK * c, BANK * (c + 1))
                pe.wait_ge(xt_lo_done, xt_of(layer, c) + 1)
                for m in range(FW + 1):
                    n = FW * fc + m
                    if m < FW:
                        if n >= 2:
                            pe.wait_ge(h_hi_done, n - 1)
                        blk = slice(P * m, P * (m + 1))
                        three(bank(n % 2), w1_hi[:, blk], w1_lo[:, blk], xT_hi[:, cols], xT_lo[:, cols]).then_inc(h_full, 1)
                    if m == 1 and turn_before(layer, c):
                        turn_result(y - 1)
                    if m >= 1:
                        pe.wait_ge(h_lo_done, n)
                        if m == 1:
                            pe.wait_ge(yT_ready, y - 1)
                        r = (n - 1) % 2
                        three(bank(2 + y % 2), w2_hi[:, m - 1, :], w2_lo[:, m - 1, :], h_hi[:, r, :], h_lo[:, r, :],
                              start=(m == 1), stop=(m == FW)).then_inc(h_used, 1)

            def xt_of(layer, c):
                return CHUNKS * (1 + 2 * layer) + c

            def turn_before(layer, c):
                return not (layer == 1 and c == 0)

            for c in range(CHUNKS):
                turn_chunk(CHUNKS + c)
                feed_forward(0, c)

            pe.wait_ge(wv2_scaled, 1)
            pe.wait_ge(h_hi_done, FW * CHUNKS)
            nc.tensor.transpose(bank(0)[:, 0:P], wv2_abs[:, :], ident[:, :]).then_inc(wv2_t, 1)
            pe.wait_ge(diagb_made, 1)
            nc.tensor.matmul(bank(1)[:, 0:P], ones[:, :], diag_b[:, :], start=True, stop=True).then_inc(l1c_full, 1)

            def max_tile_b(b, n):
                j = QT - 1 - n
                if b or n:
                    pe.wait_ge(maxb_done, QT * b + n)
                cols = P * (j + 1)
                for c0 in range(0, cols, BANK):
                    c1 = min(c0 + BANK, cols)
                    last = nc.tensor.matmul(psum[:, 2 * BANK + c0:2 * BANK + c1], qb_hi[:, S * b + P * j:S * b + P * (j + 1)],
                                            xT_hi[:, S * b + c0:S * b + c1], start=True, stop=True)
                last.then_inc(maxb_full, 1)

            def turn_maxima_b(b):
                pe.wait_ge(maxb_done, QT * (b + 1))
                if b == 0:
                    pe.wait_ge(v2_lo_done, CHUNKS)
                else:
                    pe.wait_ge(mrowb_done, 1)
                nc.tensor.transpose(bank(1)[0:QT, 0:P], max_b[:, b, :], ident[:, :]).then_inc(mtb_full, 1)

            pe.wait_ge(wqk_split, 1)
            pe.wait_ge(wv2_split, 1)
            pe.wait_ge(l1c_done, 1)
            for c in range(CHUNKS):
                cols = slice(BANK * c, BANK * (c + 1))
                turn_chunk(2 * CHUNKS + c)
                if c == 0:
                    turn_result(2 * CHUNKS - 1)
                pe.wait_ge(xt_lo_done, 2 * CHUNKS + c + 1)
                if c:
                    pe.wait_ge(qb_lo_done, c)
                three(bank(0), wqk_hi[:, :], wqk_lo[:, :], xT_hi[:, cols], xT_lo[:, cols]).then_inc(qb_full, 1)
                if c:
                    pe.wait_ge(v2_lo_done, c)
                for j in range(CT):
                    rows = slice(BANK * c + P * j, BANK * c + P * (j + 1))
                    last = three(bank(1)[:, P * j:P * (j + 1)], xT_hi[:, rows], xT_lo[:, rows], wv2_hi[:, :], wv2_lo[:, :])
                last.then_inc(v2_full, 1)
                if c == 2:
                    pe.wait_ge(yT_ready, 2 * CHUNKS)
                    pe.wait_ge(qb_lo_done, 2)
                if c >= 2:
                    for n in range(4 * (c - 2), 4 * (c - 1)):
                        max_tile_b(0, n)
            turn_maxima_b(0)
            pe.wait_ge(rows_b, 3)
            pe.wait_ge(res_done, 2 * CHUNKS)
            pe.wait_ge(xt_lo_done, 3 * CHUNKS)

            st_bank = (4, 5, 0)

            def scores_b(b, i, r):
                _, q0, n = units[r]
                m = NU * b + r
                if m >= ST_RING:
                    pe.wait_ge(s32_done, m - ST_RING + 1)
                if r == 0:
                    pe.wait_ge(mrowb_done, b + 1)
                    pe.wait_ge(qb_lo_done, CHUNKS)
                keys = slice(S * b + P * i, S * b + P * (i + 1))
                qs = slice(S * b + q0, S * b + q0 + n)
                dst = bank(st_bank[m % ST_RING], n)
                three(dst, xT_hi[:, keys], xT_lo[:, keys], qb_hi[:, qs], qb_lo[:, qs], stop=False)
                nc.tensor.matmul(dst, k_one[:, :], qm_b[:, b, q0:q0 + n], start=False, stop=True).then_inc(sb_full, 1)

            def outputs_b(b, j):
                pe.wait_ge(plob_done, NU * b + need_units[j])
                m = QT * b + j
                if m >= 2:
                    pe.wait_ge(ob_read, m - 1)
                if m == 0:
                    pe.wait_ge(v2_one, 1)
                dst = bank(6 + m % 2, V2W)
                for kt in range(j + 1):
                    cols = slice(at[kt] + P * (j - kt), at[kt] + P * (j - kt + 1))
                    tile = QT * b + kt
                    nc.tensor.matmul(dst, p_hlb[:, 0, cols], v2_sb[:, tile, 0:V2W], start=(kt == 0), stop=False)
                    last = nc.tensor.matmul(dst[:, E:V2W], p_hlb[:, 1, cols], v2_sb[:, tile, E:V2W], start=False, stop=(kt == j))
                last.then_inc(pvb_done, 1)

            for b in range(B):
                for i in range(QT + 2):
                    if i < QT:
                        for r in units_of[i]:
                            scores_b(b, i, r)
                        if b == 0:
                            max_tile_b(1, i)
                    if i >= 2:
                        outputs_b(b, i - 2)
                if b == 0:
                    turn_maxima_b(1)

            pe.wait_ge(s32_done, NU * B)
            pe.wait_ge(ob_read, QT * B)
            for c in range(CHUNKS):
                turn_chunk(3 * CHUNKS + c)
                feed_forward(1, c)
            turn_result(3 * CHUNKS - 1)

        @block.scalar
        def _(act):
            act.dma_start(wv_raw[:, :].rearrange("p (h d) -> p h d", h=H), Wv.rearrange("h e d -> e h d")).then_inc(wv_in, 16)
            act.dma_start(bv_sb[:, :], bv.rearrange("(q a) d -> (a d) q", a=2), allow_slow_non_contiguous=True).then_inc(bias_in, 16)
            act.dma_start(bo_sb[:, :], bo.unsqueeze(1)).then_inc(bias_in, 16)
            act.dma_start(b1_sb[:, :], b1.rearrange("(m p) -> p m", p=P), allow_slow_non_contiguous=True).then_inc(bias_in, 16)
            act.dma_start(b2_sb[:, :], b2.unsqueeze(1)).then_inc(bias_in, 16)
            act.dma_start(wo_raw[:, :, :], Wo.rearrange("(k p) e -> p k e", p=P)).then_inc(wo_in, 16)
            act.dma_start(w1_raw[:, :], w1).then_inc(ffn_in, 16)
            act.dma_start(w2_raw[:, :, :], w2.rearrange("(m p) e -> p m e", p=P)).then_inc(ffn_in, 16)

            def split_high(pair, par):
                act.wait_ge(pair_in, 64 * (pair + 1))
                nc.scalar.copy(w_hi[:, par, :, :], w_raw[:, :, :]).then_inc(split_hi, 1)

            def chunk_high(n):
                act.wait_ge(xt_full, n + 1)
                c = n % CHUNKS
                nc.scalar.copy(xT_hi[:, BANK * c:BANK * (c + 1)], bank(6 + n % 2)).then_inc(xt_hi_done, 1)

            def piece_high(n, pair, par, which, half):
                act.wait_ge(piece_full, n + 1)
                if half == 0 and not (isinstance(pair, int) and pair == 0):
                    moved = (k_moved, q_moved)[which]
                    act.wait_ge(moved[0], 48 * pair)
                    act.wait_ge(moved[1], 48 * pair)
                nc.scalar.activation(st_hi[:, which, BANK * half:BANK * (half + 1)], bank(MISC), ACT.Identity,
                                     bias=w_b[:, par, which:which + 1]).then_inc(piece_hi, 1)

            split_high(0, 0)
            act.wait_ge(wv_in, 16)
            nc.scalar.activation(wv_abs[:, :], wv_raw[:, :], ACT.Abs).then_inc(abs_done, 1)
            for c in range(CHUNKS):
                chunk_high(c)
            for n in range(8):
                if n == 2:
                    split_high(1, 1)
                piece_high(n, n // 4, n // 4, n % 4 // 2, n % 2)
            act.wait_ge(wv_scaled, 1)
            nc.scalar.copy(wv_hi[:, :], wv_raw[:, :]).then_inc(wv_hi_done, 1)
            act.wait_ge(wo_scaled, 1)
            nc.scalar.copy(wo_hi[:, :, :], wo_raw[:, :, :]).then_inc(wts_hi_done, 1)
            act.wait_ge(ffn_in, 32)
            nc.scalar.copy(w1_hi[:, :], w1_raw[:, :]).then_inc(wts_hi_done, 1)
            nc.scalar.copy(w2_hi[:, :, :], w2_raw[:, :, :]).then_inc(wts_hi_done, 1)
            for n in range(2 * TILES):
                act.wait_ge(v_full, n + 1)
                stage = n // QT
                if n % QT == 0 and stage >= 2:
                    act.wait_ge(scratch_out[stage % 2], 16)
                nc.scalar.copy(v_stage[stage % 2][:, :, n % QT, DH:2 * DH],
                               bank(n % ST_RING).rearrange("p (h d) -> p h d", d=DH)).then_inc(v_hi_done, 1)
            for n in range(2):
                act.wait_ge(scratch_out[n], 16 * B)
            act.wait_ge(wts_lo_done, 3)
            act.wait_ge(v_lo_done, 2 * TILES)

            def exponentials(u, k, r):
                i, q0, n = units[r]
                act.wait_ge(st_full, NU * u + (r + 1))
                if r >= RING or not (isinstance(u, int) and u == 0):
                    act.wait_ge(plo_done, NU * u + (r - RING + 1))
                src = bank(r % ST_RING, n)
                nc.scalar.activation(p32[:, r % RING, 0:n], src, ACT.Exp, scale=SCALE_A).then_inc(exp_done, 1)
                c0 = at[i] + q0 - P * i
                nc.scalar.activation(p_hl[:, k % 2, 0, c0:c0 + n], src, ACT.Exp, scale=SCALE_A).then_inc(phi_done, 1)

            def act_slot(t, k, project, split):
                u = 4 * t + k
                for i in range(QT):
                    if project and i in PIECE_STEPS:
                        half = PIECE_STEPS.index(i)
                        piece_high(2 * u + (6 + half), 2 * t + (k + 3) // 2, ((k + 3) // 2) % 2, (k + 1) % 2, half)
                    for r in units_of[i]:
                        exponentials(u, k, r)
                    if split and i == 1:
                        split_high(2 * t + (k + 4) // 2, ((k + 4) // 2) % 2)

            act_slot(0, 0, False, True)
            with act.Fori(0, LOOPS) as t:
                for k in range(1, 5):
                    act_slot(t, k, True, k % 2 == 0)
            for k in LAST_SLOTS:
                act_slot(LOOPS, k, False, False)

            def result_high(n, bias):
                if n >= 2:
                    act.wait_ge(yt_full, n - 1)
                nc.scalar.activation(yT[:, n % 2, :], bank(2 + n % 2), ACT.Identity, bias=bias).then_inc(yT_ready, 1)

            act.wait_ge(attn_b_in, 48)
            nc.scalar.activation(wv2_abs[:, :], wv2_raw[:, :], ACT.Abs, accum_out=l1_b[:, 0:1]).then_inc(l1b_made, 1)
            for c in range(CHUNKS):
                for blk in range(OB):
                    n = OB * c + blk
                    act.wait_ge(ot_full, n + 1)
                    if n >= 2:
                        act.wait_ge(ot_used, n - 1)
                    nc.scalar.copy(oT_hi[:, n % 2, :], bank(n % 2)).then_inc(ot_hi_done, 1)
                act.wait_ge(ot_used, OB * (c + 1))
                act.wait_ge(o_read, 2)
                result_high(c, bo_all[:, 0:1])

            def feed_forward(layer, c):
                fc = CHUNKS * layer + c
                chunk_high_of(layer, c)
                for m in range(FW):
                    n = FW * fc + m
                    act.wait_ge(h_full, n + 1)
                    if n >= 2:
                        act.wait_ge(h_lo_done, n - 1)
                        act.wait_ge(h_used, n - 1)
                    nc.scalar.activation(h32[:, n % 2, :], bank(n % 2), ACT.Relu, bias=b1_sb[:, m:m + 1]).then_inc(h32_done, 1)
                    nc.scalar.activation(h_hi[:, n % 2, :], bank(n % 2), ACT.Relu, bias=b1_sb[:, m:m + 1]).then_inc(h_hi_done, 1)
                act.wait_ge(h_used, FW * (fc + 1))
                result_high(CHUNKS + fc, b2_sb[:, 0:1])

            def chunk_high_of(layer, c):
                chunk_high(CHUNKS * (1 + 2 * layer) + c)

            for c in range(CHUNKS):
                feed_forward(0, c)
            act.wait_ge(attn_b_in, 48)
            nc.scalar.copy(wqk_hi[:, :], wqk_raw[:, :]).then_inc(wqk_hi_done, 1)
            act.wait_ge(wv2_t, 1)
            nc.scalar.copy(wv2_hi[:, :], bank(0)[:, 0:P]).then_inc(wv2_hi_done, 1)
            for c in range(CHUNKS):
                chunk_high(2 * CHUNKS + c)
                act.wait_ge(qb_full, c + 1)
                nc.scalar.mul(qb_hi[:, BANK * c:BANK * (c + 1)], bank(0), SCALE_B).then_inc(qb_hi_done, 1)
                act.wait_ge(v2_full, c + 1)
                nc.scalar.copy(v2_sb[:, CT * c:CT * (c + 1), E:2 * E], bank(1).rearrange("p (t e) -> p t e", e=E)).then_inc(v2_hi_done, 1)
            for m in range(NU * B):
                i, q0, n = units[m % NU]
                act.wait_ge(s32_done, m + 1)
                if m >= RING:
                    act.wait_ge(plob_done, m - RING + 1)
                if m == NU:
                    act.wait_ge(pvb_done, QT)
                src = s32[:, m % 3, 0:n]
                nc.scalar.activation(p32b[:, m % RING, 0:n], src, ACT.Exp).then_inc(expb_done, 1)
                c0 = at[i] + q0 - P * i
                nc.scalar.activation(p_hlb[:, 0, c0:c0 + n], src, ACT.Exp).then_inc(phib_done, 1)
            for c in range(CHUNKS):
                feed_forward(1, c)

        @block.vector
        def _(dve):
            def chunk_stats(n):
                c = n % CHUNKS
                for j in range(CT * c, CT * (c + 1)):
                    last = nc.vector.bn_stats(stats[:, j, :], x_sb[:, j, :])
                last.then_inc(bn_done, 1)
                dve.wait_ge(bn_done, n + 1)
                for j in range(CT * c, CT * (c + 1)):
                    last = nc.vector.bn_aggr(mean_var[:, j, :], stats[:, j, :])
                last.then_inc(aggr_done, 1)

            def chunk_norm(n):
                c = n % CHUNKS
                dve.wait_ge(rstd_done, n + 1)
                if n >= 2:
                    dve.wait_ge(xt_full, n - 1)
                for j in range(CT):
                    tile = CT * c + j
                    last = nc.vector.tensor_scalar(xn[:, n % 2, j, :], x_sb[:, tile, :], mean_var[:, tile, 0:1], rstd[:, tile:tile + 1],
                                                   ALU.subtract, ALU.mult)
                last.then_inc(xn_ready, 1)

            def chunk_low(n):
                dve.wait_ge(xt_hi_done, n + 1)
                c = n % CHUNKS
                cols = slice(BANK * c, BANK * (c + 1))
                nc.vector.tensor_tensor(xT_lo[:, cols], bank(6 + n % 2), xT_hi[:, cols], ALU.subtract).then_inc(xt_lo_done, 1)

            def piece_low(n, par, which, half):
                dve.wait_ge(piece_hi, n + 1)
                cols = slice(BANK * half, BANK * (half + 1))
                nc.vector.scalar_tensor_tensor(out=st_lo[:, which, cols], in0=bank(MISC), scalar=w_b[:, par, which:which + 1],
                                               in1=st_hi[:, which, cols], op0=ALU.add, op1=ALU.subtract).then_inc(piece_lo, 1)

            nc.vector.memset(minus_half[:, :], -0.5).then_inc(half_ready, 1)
            nc.vector.memset(ones[:, :], 1.0).then_inc(ones_ready, 1)
            for c in range(CHUNKS):
                dve.wait_ge(x_in[c], 16)
                chunk_stats(c)
            chunk_norm(0)
            chunk_norm(1)
            for c in range(CHUNKS):
                chunk_low(c)
                if c + 2 < CHUNKS:
                    chunk_norm(c + 2)
            dve.wait_ge(l1r_full, 1)
            nc.vector.tensor_scalar(l1_rows[:, :], bank(PVB)[:, 0:OB], TINY, 1.0 / F16_TOP, ALU.add, ALU.mult).then_inc(o_read, 1)
            dve.wait_ge(bo_full, 1)
            nc.vector.tensor_tensor(bo_all[:, :], bank(PVB + 1)[:, 0:1], bo_sb[:, :], ALU.add).then_inc(o_read, 1)
            dve.wait_ge(o_read, 2)
            nc.vector.tensor_tensor(wo_raw[:, :, :], wo_raw[:, :, :], l1_rows[:, :].unsqueeze(2).to_broadcast([P, OB, E]), ALU.mult)\
                .then_inc(wo_scaled, 1)
            for n in range(4):
                piece_low(n, 0, n // 2, n % 2)
            dve.wait_ge(l1_full, 1)
            for n in range(2):
                nc.vector.tensor_scalar(wv_gain[:, BANK * n:BANK * (n + 1)], bank(MAXB + n), TINY, None, ALU.add).then_inc(gain_sum, 1)
            dve.wait_ge(gain_sum, 2)
            nc.vector.reciprocal(wv_abs[:, :], wv_gain[:, :]).then_inc(gain_done, 1)
            dve.wait_ge(gain_done, 1)
            nc.vector.scalar_tensor_tensor(out=wv_raw[:, :], in0=wv_abs[:, :], scalar=F16_TOP, in1=wv_raw[:, :],
                                           op0=ALU.mult, op1=ALU.mult).then_inc(wv_scaled, 1)
            for n in range(4, 8):
                piece_low(n, 1, n % 4 // 2, n % 2)
            dve.wait_ge(wv_hi_done, 1)
            nc.vector.tensor_tensor(wv_lo[:, :], wv_raw[:, :], wv_hi[:, :], ALU.subtract).then_inc(wv_lo_done, 1)
            for n in range(2 * TILES):
                dve.wait_ge(v_hi_done, n + 1)
                stage = v_stage[n // QT % 2]
                nc.vector.tensor_tensor(stage[:, :, n % QT, 0:DH], bank(n % ST_RING).rearrange("p (h d) -> p h d", d=DH),
                                        stage[:, :, n % QT, DH:2 * DH], ALU.subtract).then_inc(v_lo_done, 1)

            def take_max(v, par, n):
                j = MAX_ORDER[n]
                cols = P * (j + 1)
                dve.wait_ge(max_full, QT * v + (n + 1))
                nc.vector.memset(gate[:, :], 0.0)
                nc.vector.tensor_tensor_reduce(out=max_junk[:, 0:cols], in0=psum[:, MAXB * BANK:MAXB * BANK + cols],
                                               in1=mask_s[:, S - cols:S], scale=1.0, scalar=-3.0e38, op0=ALU.add, op1=ALU.max,
                                               accum_out=maxima[:, par, j:j + 1]).then_inc(max_done, 1)

            def max_rows(v, s):
                dve.wait_ge(mt_full, v + 1)
                nc.vector.tensor_tensor(q_hm[DH:DH + QT, s, :].rearrange("p (j q) -> p j q", j=QT),
                                        bank(MISC)[0:QT, 0:P].unsqueeze(1).to_broadcast([QT, QT, P]),
                                        neg_diag[:, :].unsqueeze(2).to_broadcast([QT, QT, P]), ALU.mult).then_inc(mrow_done, 1)

            def outputs_out(w, k, g, pairs_before):
                js = PV_GROUPS[g]
                n = len(js)
                par = (k - 1) // 2 % 2
                m = (k - 1 + g) % 2
                src = bank(PVB + m, VW * n).rearrange("p (j c) -> p j c", c=VW)
                dve.wait_ge(pv_done, QT * w + js[-1] + 1)
                nc.vector.tensor_reduce(o_sum[:, m, 0:n, :], src[:, :, 0:2 * DH].rearrange("p j (a d) -> p j d a", a=2), AX_X, ALU.add)\
                    .then_inc(o_summed, 1)
                nc.vector.reciprocal(o_den[:, m, 0:n], src[:, :, 2 * DH]).then_inc(o_read, 1)
                if g == 0 and (k - 1) % 2 == 0:
                    dve.wait_ge(scratch_out[par], 16 * (B + pairs_before))
                dve.wait_ge(o_summed, NG * w + (g + 1))
                dve.wait_ge(o_read, NG * w + (g + 3))
                c0 = DH * ((k - 1) % 2)
                nc.vector.tensor_tensor(o_sb[:, par, js[0]:js[-1] + 1, c0:c0 + DH], o_sum[:, m, 0:n, :],
                                        o_den[:, m, 0:n].unsqueeze(2).to_broadcast([P, n, DH]), ALU.mult).then_inc(o_ready, 1)

            def dve_slot(t, k, project, maximum):
                u = 4 * t + k
                for i in range(QT):
                    if maximum:
                        for j in MAX_AT[i]:
                            take_max(u + 1, (k + 1) % 2, MAX_ORDER.index(j))
                    if project and i in PIECE_STEPS:
                        half = PIECE_STEPS.index(i)
                        piece_low(2 * u + (6 + half), ((k + 3) // 2) % 2, (k + 1) % 2, half)
                    if not (isinstance(u, int) and u == 0):
                        for g, js in enumerate(PV_GROUPS):
                            if js[-1] == i:
                                outputs_out(u - 1, k, g, t + (k - 1) // 4)
                    if maximum and i == MROW_STEP:
                        max_rows(u + 1, set_of(k, 1))

            dve.wait_ge(tri_ready, 2)
            for n in range(QT):
                take_max(0, 0, n)
            dve.wait_ge(diag_ready, 1)
            dve.wait_ge(rows_ready, 1)
            max_rows(0, 0)
            dve_slot(0, 0, False, True)
            with dve.Fori(0, LOOPS) as t:
                for k in range(1, 5):
                    dve_slot(t, k, True, True)
            for k in LAST_SLOTS:
                dve_slot(LOOPS, k, False, k < 3)
            for g in range(NG):
                outputs_out(HEADS - 1, 4, g, LOOPS)

            def add_result(n):
                c = n % CHUNKS
                dve.wait_ge(yt_full, n + 1)
                tiles = slice(CT * c, CT * (c + 1))
                nc.vector.tensor_tensor(x_sb[:, tiles, :], bank(4 + n % 2).rearrange("p (t e) -> p t e", e=E), x_sb[:, tiles, :], ALU.add)\
                    .then_inc(res_done, 1)

            dve.wait_ge(attn_b_in, 48)
            dve.wait_ge(l1b_made, 1)
            nc.vector.tensor_scalar(l1_b[:, 1:2], l1_b[:, 0:1], TINY, 1.0 / F16_TOP, ALU.add, ALU.mult).then_inc(l1b_made, 1)
            dve.wait_ge(l1b_made, 2)
            nc.vector.reciprocal(l1_b[:, 2:3], l1_b[:, 1:2]).then_inc(l1b_made, 1)
            nc.vector.tensor_scalar(diag_b[:, :], ident[:, :], l1_b[:, 1:2], None, ALU.mult).then_inc(diagb_made, 1)
            dve.wait_ge(l1b_made, 3)
            nc.vector.tensor_scalar(wv2_abs[:, :], wv2_raw[:, :], l1_b[:, 2:3], None, ALU.mult).then_inc(wv2_scaled, 1)

            for c in range(CHUNKS):
                for blk in range(OB):
                    n = OB * c + blk
                    dve.wait_ge(ot_hi_done, n + 1)
                    nc.vector.tensor_tensor(oT_lo[:, n % 2, :], bank(n % 2), oT_hi[:, n % 2, :], ALU.subtract).then_inc(ot_lo_done, 1)
                    if blk == 4 and c >= 1:
                        add_result(c - 1)
                        dve.wait_ge(res_done, c)
                        chunk_stats(CHUNKS + c - 1)
                    if blk == 6 and c == CHUNKS - 1:
                        chunk_norm(CHUNKS)

            dve.wait_ge(bias_made, 2)
            nc.vector.tensor_scalar(bias_s[:, :], bias_s[:, :], slope_sb[:, 0:1], None, ALU.mult).then_inc(steps_b, 1)
            nc.vector.tensor_scalar(bias_t[:, :], bias_t[:, :], slope_sb[:, 0:1], None, ALU.mult).then_inc(steps_b, 1)

            def feed_forward(layer, c):
                fc = CHUNKS * layer + c
                ln = CHUNKS * (1 + 2 * layer)
                chunk_low(ln + c)
                for m in range(FW):
                    n = FW * fc + m
                    dve.wait_ge(h32_done, n + 1)
                    dve.wait_ge(h_hi_done, n + 1)
                    nc.vector.tensor_tensor(h_lo[:, n % 2, :], h32[:, n % 2, :], h_hi[:, n % 2, :], ALU.subtract).then_inc(h_lo_done, 1)
                    if m == 1:
                        if not (layer == 1 and c == 0):
                            y = CHUNKS + fc - 1
                            add_result(y)
                            if c == 0 or layer == 0:
                                dve.wait_ge(res_done, y + 1)
                                chunk_stats(CHUNKS * (1 + 2 * layer) + 3 if c == 0 else CHUNKS * 2 + c - 1)
                    if m == 2 and c + 1 < CHUNKS:
                        chunk_norm(ln + c + 1)
                    if m == 3 and layer == 0 and c == CHUNKS - 1:
                        chunk_norm(2 * CHUNKS)

            for c in range(CHUNKS):
                feed_forward(0, c)
            dve.wait_ge(wqk_hi_done, 1)
            nc.vector.tensor_tensor(wqk_lo[:, :], wqk_raw[:, :], wqk_hi[:, :], ALU.subtract).then_inc(wqk_split, 1)
            dve.wait_ge(wv2_hi_done, 1)
            nc.vector.tensor_tensor(wv2_lo[:, :], bank(0)[:, 0:P], wv2_hi[:, :], ALU.subtract).then_inc(wv2_split, 1)
            dve.wait_ge(l1c_full, 1)
            nc.vector.tensor_copy(l1_cols[:, :], bank(1)[:, 0:P]).then_inc(l1c_done, 1)

            def take_max_b(b, n):
                j = QT - 1 - n
                cols = P * (j + 1)
                dve.wait_ge(maxb_full, QT * b + n + 1)
                nc.vector.tensor_tensor_reduce(out=junk_b[:, 0:cols], in0=psum[:, 2 * BANK:2 * BANK + cols], in1=bias_s[:, S - cols:S],
                                               scale=1.0, scalar=-3.0e38, op0=ALU.add, op1=ALU.max,
                                               accum_out=max_b[:, b, j:j + 1]).then_inc(maxb_done, 1)

            def max_rows_b(b):
                dve.wait_ge(mtb_full, b + 1)
                nc.vector.tensor_tensor(qm_b[0:QT, b, :].rearrange("p (j q) -> p j q", j=QT),
                                        bank(1)[0:QT, 0:P].unsqueeze(1).to_broadcast([QT, QT, P]),
                                        neg_diag_b[:, :].unsqueeze(2).to_broadcast([QT, QT, P]), ALU.mult).then_inc(mrowb_done, 1)

            for c in range(CHUNKS):
                chunk_low(2 * CHUNKS + c)
                if c == 0:
                    add_result(2 * CHUNKS - 1)
                    dve.wait_ge(res_done, 2 * CHUNKS)
                    chunk_stats(3 * CHUNKS - 1)
                if c + 1 < CHUNKS:
                    chunk_norm(2 * CHUNKS + c + 1)
                cols = slice(BANK * c, BANK * (c + 1))
                dve.wait_ge(qb_hi_done, c + 1)
                nc.vector.scalar_tensor_tensor(out=qb_lo[:, cols], in0=bank(0), scalar=SCALE_B, in1=qb_hi[:, cols],
                                               op0=ALU.mult, op1=ALU.subtract).then_inc(qb_lo_done, 1)
                dve.wait_ge(v2_hi_done, c + 1)
                tiles = slice(CT * c, CT * (c + 1))
                nc.vector.tensor_tensor(v2_sb[:, tiles, 0:E], bank(1).rearrange("p (t e) -> p t e", e=E), v2_sb[:, tiles, E:2 * E], ALU.subtract)\
                    .then_inc(v2_lo_done, 1)
                if c == 2:
                    dve.wait_ge(bias_ready, 2)
                if c >= 2:
                    for n in range(4 * (c - 2), 4 * (c - 1)):
                        take_max_b(0, n)
            dve.wait_ge(rows_b, 3)
            max_rows_b(0)

            def biased(b, r):
                i, q0, n = units[r]
                m = NU * b + r
                dve.wait_ge(sb_full, m + 1)
                if m >= 3:
                    dve.wait_ge(phib_done, m - 2)
                c0 = q0 - P * i
                nc.vector.tensor_tensor(s32[:, m % 3, 0:n], bank(st_bank[m % ST_RING], n), bias_t[:, c0:c0 + n], ALU.add).then_inc(s32_done, 1)

            st_bank = (4, 5, 0)

            def output_b(b, j):
                m = QT * b + j
                src = bank(6 + m % 2, V2W)
                dve.wait_ge(pvb_done, m + 1)
                nc.vector.tensor_reduce(ob_sum[:, m % 2, :], src[:, 0:2 * E].rearrange("p (a d) -> p d a", a=2), AX_X, ALU.add).then_inc(ob_steps, 1)
                nc.vector.reciprocal(ob_den[:, m % 2:m % 2 + 1], src[:, 2 * E:V2W]).then_inc(ob_read, 1)
                dve.wait_ge(ob_steps, 2 * m + 1)
                dve.wait_ge(ob_read, m + 1)
                nc.vector.scalar_tensor_tensor(out=ob_out[:, m % 2, :], in0=ob_sum[:, m % 2, :], scalar=ob_den[:, m % 2:m % 2 + 1],
                                               in1=l1_cols[:, :], op0=ALU.mult, op1=ALU.mult).then_inc(ob_steps, 1)
                dve.wait_ge(ob_steps, 2 * m + 2)
                nc.vector.tensor_tensor(x_sb[:, m, :], ob_out[:, m % 2, :], x_sb[:, m, :], ALU.add).then_inc(resb_done, 1)
                if m % CT == CT - 1:
                    dve.wait_ge(resb_done, m + 1)
                    chunk_stats(3 * CHUNKS + m // CT)

            for b in range(B):
                for i in range(QT + 2):
                    if i < QT:
                        for r in units_of[i]:
                            biased(b, r)
                        if b == 0:
                            take_max_b(1, i)
                    if b == 1 and i == QT - 1:
                        chunk_norm(3 * CHUNKS)
                    if i >= 2:
                        output_b(b, i - 2)
                if b == 0:
                    max_rows_b(1)
            for c in range(CHUNKS):
                feed_forward(1, c)
            add_result(3 * CHUNKS - 1)

        @block.gpsimd
        def _(pool):
            nc.gpsimd.memset(ident[:, :], 0.0).then_inc(zeroed, 1)
            nc.gpsimd.memset(ident_b[:, :], 0.0).then_inc(zeroed, 1)
            pool.wait_ge(zeroed, 2)
            for i in (ident, ident_b):
                nc.gpsimd.affine_select(out=i[:, :], in_=i[:, :], compare_op=ALU.not_equal, fill=1.0, base=0,
                                        pattern=[[-1, P]], channel_multiplier=1).then_inc(ident_ready, 1)

            def chunk_rstd(n):
                c = n % CHUNKS
                cols = slice(CT * c, CT * (c + 1))
                pool.wait_ge(aggr_done, n + 1)
                nc.gpsimd.tensor_scalar(var_eps[:, cols], mean_var[:, cols, 1], EPS, None, ALU.add).then_inc(eps_done, 1)
                pool.wait_ge(eps_done, n + 1)
                nc.gpsimd.tensor_tensor(rstd[:, cols], var_eps[:, cols], minus_half[:, :], ALU.pow).then_inc(rstd_done, 1)

            def split_low(pair, par):
                pool.wait_ge(split_hi, pair + 1)
                nc.gpsimd.tensor_tensor(w_lo[:, par, :, :], w_raw[:, :, :], w_hi[:, par, :, :], ALU.subtract).then_inc(split_lo, 1)

            pool.wait_ge(half_ready, 1)
            for c in range(CHUNKS):
                chunk_rstd(c)
            split_low(0, 0)
            nc.gpsimd.memset(mask_s[:, :], 0.0).then_inc(zeroed, 1)
            nc.gpsimd.memset(mask_t[:, :], 0.0).then_inc(zeroed, 1)
            nc.gpsimd.memset(neg_diag[:, :], 0.0).then_inc(zeroed, 1)
            nc.gpsimd.memset(k_l1[:, :, :].bitcast(F32), 0.0).then_inc(zeroed, 1)
            nc.gpsimd.memset(q_hm[:, :, :].bitcast(F32), 0.0).then_inc(zeroed, 1)
            pool.wait_ge(zeroed, 7)
            nc.gpsimd.memset(k_l1[DH:DH + QT, :, :].bitcast(F32), 1.0).then_inc(rows_ready, 1)
            pool.wait_ge(rows_ready, 1)
            split_low(1, 1)
            for s in v_stage:
                last = nc.gpsimd.memset(s[:, :, :, 2 * DH:VP], 1.0)
            last.then_inc(v_one, 1)
            nc.gpsimd.affine_select(out=mask_s[:, S - P:S], in_=mask_s[:, S - P:S], compare_op=ALU.is_ge, fill=NEG, base=0,
                                    pattern=[[-1, P]], channel_multiplier=1).then_inc(tri_ready, 1)
            nc.gpsimd.affine_select(out=mask_t[:, :], in_=mask_t[:, :], compare_op=ALU.is_ge, fill=NEG, base=0,
                                    pattern=[[1, P]], channel_multiplier=-1).then_inc(tri_ready, 1)
            nc.gpsimd.affine_select(out=neg_diag[:, :], in_=neg_diag[:, :], compare_op=ALU.not_equal, fill=-1.0, base=0,
                                    pattern=[[-1, QT]], channel_multiplier=1).then_inc(diag_ready, 1)
            for n, (lo, raw, hi) in enumerate(((wo_lo, wo_raw, wo_hi), (w1_lo, w1_raw, w1_hi), (w2_lo, w2_raw, w2_hi))):
                pool.wait_ge(wts_hi_done, n + 1)
                nc.gpsimd.tensor_tensor(lo[:], raw[:], hi[:], ALU.subtract).then_inc(wts_lo_done, 1)

            def low(u, k, r):
                i, q0, n = units[r]
                pool.wait_ge(exp_done, NU * u + (r + 1))
                pool.wait_ge(phi_done, NU * u + (r + 1))
                c0 = at[i] + q0 - P * i
                nc.gpsimd.tensor_tensor(p_hl[:, k % 2, 1, c0:c0 + n], p32[:, r % RING, 0:n], p_hl[:, k % 2, 0, c0:c0 + n], ALU.subtract)\
                    .then_inc(plo_done, 1)

            def pool_slot(t, k, split):
                u = 4 * t + k
                for i in range(QT):
                    for r in units_of[i]:
                        low(u, k, r)
                    if split and i == 1:
                        split_low(2 * t + (k + 4) // 2, ((k + 4) // 2) % 2)

            pool_slot(0, 0, True)
            with pool.Fori(0, LOOPS) as t:
                for k in range(1, 5):
                    pool_slot(t, k, k % 2 == 0)
            for k in LAST_SLOTS:
                pool_slot(LOOPS, k, False)

            pool.wait_ge(o_ready, NG * HEADS)
            for n in range(2):
                pool.wait_ge(scratch_out[n], 16 * (B + PAIRS // 2))
            nc.gpsimd.iota(bias_s[:, :], pattern=[[1, S]], base=P - S, channel_multiplier=-1,
                           allow_small_or_imprecise_dtypes=True).then_inc(bias_made, 1)
            nc.gpsimd.iota(bias_t[:, :], pattern=[[-1, S]], base=0, channel_multiplier=1,
                           allow_small_or_imprecise_dtypes=True).then_inc(bias_made, 1)
            nc.gpsimd.memset(qm_b[:, :, :].bitcast(F32), 0.0).then_inc(rows_b, 1)
            nc.gpsimd.memset(k_one[:, :].bitcast(F32), 0.0).then_inc(zeroed, 1)
            nc.gpsimd.memset(neg_diag_b[:, :], 0.0).then_inc(zeroed, 1)
            nc.gpsimd.memset(v2_sb[:, :, 2 * E:V2P], 1.0).then_inc(v2_one, 1)
            pool.wait_ge(zeroed, 9)
            nc.gpsimd.memset(k_one[0:QT, :].bitcast(F32), 1.0).then_inc(rows_b, 1)
            nc.gpsimd.affine_select(out=neg_diag_b[:, :], in_=neg_diag_b[:, :], compare_op=ALU.not_equal, fill=-1.0, base=0,
                                    pattern=[[-1, QT]], channel_multiplier=1).then_inc(rows_b, 1)
            for c in range(CHUNKS):
                chunk_rstd(CHUNKS + c)
                if c == 0:
                    pool.wait_ge(attn_b_in, 48)
            pool.wait_ge(steps_b, 2)
            nc.gpsimd.affine_select(out=bias_s[:, :], in_=bias_s[:, :], compare_op=ALU.is_ge, fill=NEG, base=S - P,
                                    pattern=[[-1, S]], channel_multiplier=1).then_inc(bias_ready, 1)
            nc.gpsimd.affine_select(out=bias_t[:, :], in_=bias_t[:, :], compare_op=ALU.is_ge, fill=NEG, base=0,
                                    pattern=[[1, S]], channel_multiplier=-1).then_inc(bias_ready, 1)
            for c in range(CHUNKS):
                chunk_rstd(2 * CHUNKS + c)
            for m in range(NU * B):
                i, q0, n = units[m % NU]
                pool.wait_ge(expb_done, m + 1)
                pool.wait_ge(phib_done, m + 1)
                c0 = at[i] + q0 - P * i
                nc.gpsimd.tensor_tensor(p_hlb[:, 1, c0:c0 + n], p32b[:, m % RING, 0:n], p_hlb[:, 0, c0:c0 + n], ALU.subtract)\
                    .then_inc(plob_done, 1)
                if m == NU + 2:
                    chunk_rstd(3 * CHUNKS)
                    chunk_rstd(3 * CHUNKS + 1)
            for c in range(2, CHUNKS):
                chunk_rstd(3 * CHUNKS + c)


_INS = ['L0_attn_a_x', 'L0_attn_a_Wq', 'L0_attn_a_Wk', 'L0_attn_a_Wv', 'L0_attn_a_bq', 'L0_attn_a_bk', 'L0_attn_a_bv',
        'L0_attn_a_Wo', 'L0_attn_a_bo', 'L0_attn_b_W_qk', 'L0_attn_b_W_v', 'L0_attn_b_alibi_slope',
        'L0_ffn_w1', 'L0_ffn_b1', 'L0_ffn_w2', 'L0_ffn_b2']
_OUT = ((2, 1024, 128), 'float32')


def kernel(**inputs):
    import numpy as _np
    import concourse.bacc as _bacc
    from concourse import mybir as _mybir
    from concourse.bass_utils import run_bass_kernel_spmd as _run

    nc = _bacc.Bacc("TRN2", target_bir_lowering=False, num_devices=1)
    arrays, args = {}, []
    for name in _INS:
        a = _np.ascontiguousarray(inputs[name])
        arrays[f"in_{name}"] = a
        args.append(nc.dram_tensor(f"in_{name}", a.shape, _mybir.dt.from_np(a.dtype), kind="ExternalInput").ap())
    shape, dtype = _OUT
    args.append(nc.dram_tensor("out_0", shape, _mybir.dt.from_np(_np.dtype(dtype)), kind="ExternalOutput").ap())
    hybrid_block(nc, *args)
    r = _run(nc, [arrays], core_ids=[0])
    return r.results[0]["out_0"]
```

```python
from contextlib import ExitStack

import concourse.bass as bass
from concourse import mybir

F32 = mybir.dt.float32
F32R = mybir.dt.float32r
F16 = mybir.dt.float16
BF16 = mybir.dt.bfloat16
ALU = mybir.AluOpType
ACT = mybir.ActivationFunctionType

P = 128
BANK = 512
NEG = -1.0e30
EPS = 1.0e-5
TINY = 1.0e-30
F16_TOP = 4096.0


def hybrid_block(nc, x, Wq, Wk, Wv, bq, bk, bv, Wo, bo, Wqk, Wv2, slope, w1, b1, w2, b2, out):
    B, S, E = x.shape
    H, _, DH = Wq.shape
    F = w1.shape[1]
    T = B * S
    TILES = T // P
    QT = S // P
    CHUNKS = T // BANK
    CT = BANK // P
    HEADS = B * H
    PAIRS = HEADS // 2
    PP = H // 2
    FW = F // P
    OB = H * DH // P
    VP = 2 * DH + 2
    VW = DH + 1
    V2P = 2 * E + 2
    V2W = E + 1
    SCALE_A = float(DH) ** -0.5
    SCALE_B = float(E) ** -0.5
    assert E == P and DH * 2 == P and QT == 8 and F % P == 0 and HEADS == 32

    units = []
    for parts in (((0, 0),), ((1, P), (3, 3 * P)), ((2, 2 * P), (6, 6 * P)), ((0, BANK),), ((1, BANK),), ((2, BANK),),
                  ((3, BANK),), ((4, BANK),), ((5, 5 * P), (7, 7 * P))):
        col, unit = 0, []
        for i, q0 in parts:
            n = BANK - q0 % BANK
            unit.append((i, q0, n, col))
            col += n
        assert col == BANK
        units.append(unit)
    NU = len(units)
    PCOLS = NU * BANK
    place = {(i, j): BANK * r + col + P * j - q0 for r, unit in enumerate(units) for i, q0, n, col in unit
             for j in range(q0 // P, (q0 + n) // P)}
    need_units = [1 + max(place[i, j] for i in range(j + 1)) // BANK for j in range(QT)]
    PV_PAIRS = [(j, kt) for j in range(QT) for kt in range(j + 1)]
    PV_STEP = len(PV_PAIRS) // NU
    assert PV_STEP * NU == len(PV_PAIRS)
    PV_GROUPS = [(0, 1, 2, 3), (4, 5, 6, 7)]
    NG = len(PV_GROUPS)
    SUMS = 2
    GROUP_OF = {j: (g, js.index(j)) for g, js in enumerate(PV_GROUPS) for j in js}
    MAX_AT = [(7,), (), (6,), (5,), (4,), (3, 2), (1, 0), (), ()]
    MAX_ORDER = [j for js in MAX_AT for j in js]
    PIECE_STEPS = (1, 4)
    MROW_STEP = 7
    RING = 4
    ST_RING = 3
    BLOCKS = 3
    BLOCK_BANKS = (0, 1, 4)

    v_dram = nc.dram_tensor("v_scratch", [HEADS, P, QT * VP], F16, kind="Internal").ap()
    o_dram = nc.dram_tensor("o_scratch", [PAIRS, P, QT, P], F32, kind="Internal").ap()
    x_tok = x.rearrange("b (t p) e -> p (b t) e", p=P)
    out_tok = out.rearrange("b (t p) e -> p (b t) e", p=P)

    start = (nc.sbuf_base + 31) // 32 * 32
    end = nc.sbuf_usable_end
    SIZE = {F32: 4, F32R: 4, F16: 2, BF16: 2}
    places = [start]

    def sb(name, shape, dt):
        n = SIZE[dt]
        for s in shape[1:]:
            n *= s
        offset = places[0]
        places[0] = offset + (n + 31) // 32 * 32
        assert places[0] <= end, (name, places[0], end)
        return nc.alloc_sbuf_tensor_at(name, shape, dt, offset=offset)

    x_sb = sb("x_sb", [P, TILES, E], F32)
    xT_hi = sb("xT_hi", [P, T], F32R)
    xT_lo = sb("xT_lo", [P, T], F32R)
    xn = sb("xn", [P, 2, CT, E], F32)
    stats = sb("stats", [P, TILES, 6], F32)
    mean_var = sb("mean_var", [P, TILES, 2], F32)
    var_eps = sb("var_eps", [P, TILES], F32)
    rstd = sb("rstd", [P, TILES], F32)
    minus_half = sb("minus_half", [P, CT], F32)
    ident = sb("ident", [P, P], F32)
    ident_b = sb("ident_b", [P, P], BF16)
    ones = sb("ones", [P, P], F32)
    wo_hi = sb("wo_hi", [P, OB, E], F32R)
    wo_lo = sb("wo_lo", [P, OB, E], F32R)
    w1_hi = sb("w1_hi", [P, F], F32R)
    w1_lo = sb("w1_lo", [P, F], F32R)
    w2_hi = sb("w2_hi", [P, FW, E], F32R)
    w2_lo = sb("w2_lo", [P, FW, E], F32R)
    b1_sb = sb("b1_sb", [P, FW], F32)
    b2_sb = sb("b2_sb", [P, 1], F32)
    bo_sb = sb("bo_sb", [P, 1], F32)
    bv_sb = sb("bv_sb", [P, OB], F32)
    bo_all = sb("bo_all", [P, 1], F32)
    l1_rows = sb("l1_rows", [P, OB], F32)
    shared = places[0]

    k_hh = sb("k_hh", [P, 4, S], F32R)
    q_hl = sb("q_hl", [P, 4, S], F32R)
    k_l1 = sb("k_l1", [P, 4, S], F32R)
    q_hm = sb("q_hm", [P, 4, S], F32R)
    staged = places[0]
    st_hi = sb("st_hi", [P, 2, S], F32R)
    st_lo = sb("st_lo", [P, 2, S], F32R)
    w_raw = sb("w_raw", [P, 2, P], F32)
    w_hi = sb("w_hi", [P, 2, 2, P], F32R)
    w_lo = sb("w_lo", [P, 2, 2, P], F32R)
    w_b = sb("w_b", [P, 2, 2], F32)
    p_hl = sb("p_hl", [P, 2, 2, PCOLS], F16)
    mask_s = sb("mask_s", [P, S], F32)
    mask_t = sb("mask_t", [P, P], BF16)
    maxima = sb("maxima", [P, 2, QT], F32)
    max_junk = sb("max_junk", [P, 2, S], BF16)
    gate = sb("gate", [P, 2], F32)
    neg_diag = sb("neg_diag", [QT, QT], F32)
    before_slots = places[0]
    p32 = sb("p32", [P, RING, BANK], F32)
    v_sb = sb("v_sb", [P, 2, QT, VP], F16)
    o_sb = sb("o_sb", [P, 2, QT, P], F32)
    o_den = sb("o_den", [P, 2, CT], F32)

    VH = H // 2
    VN = VH * QT * VP
    p_flat = p_hl[:, :, :, :].rearrange("p a b n -> p (a b n)")
    v_stage = [p_flat[:, n * VN:(n + 1) * VN].rearrange("p (h t c) -> p h t c", h=VH, t=QT) for n in range(2)]

    places[0] = before_slots
    wv_raw = sb("wv_raw", [P, H * DH], F32)
    wv_abs = sb("wv_abs", [P, H * DH], F32)
    wv_gain = sb("wv_gain", [P, H * DH], F32)
    wv_hi = sb("wv_hi", [P, H * DH], F32R)
    wv_lo = sb("wv_lo", [P, H * DH], F32R)
    wo_raw = sb("wo_raw", [P, OB, E], F32)
    w1_raw = sb("w1_raw", [P, F], F32)
    w2_raw = sb("w2_raw", [P, FW, E], F32)

    places[0] = shared
    o_in1 = sb("o_in1", [P, OB, CT, P], F32)
    oT_hi = sb("oT_hi", [P, BLOCKS, BANK], F32R)
    oT_lo = sb("oT_lo", [P, BLOCKS, BANK], F32R)
    places[0] = shared + OB * CT * P * SIZE[F32]
    p_hlb = sb("p_hlb", [P, B, 2, PCOLS], F16)
    bias_s = sb("bias_s", [P, S], F32)
    bias_t = sb("bias_t", [P, S], F32)
    yT = sb("yT", [P, 2, BANK], F32)
    assert places[0] == staged
    o_in0 = sb("o_in0", [P, OB, CT, P], F32)
    o_in = (o_in0, o_in1)
    h32 = sb("h32", [P, BLOCKS, BANK], F32)
    h_hi = sb("h_hi", [P, BLOCKS, BANK], F32R)
    h_lo = sb("h_lo", [P, BLOCKS, BANK], F32R)
    qb_hi = sb("qb_hi", [P, T], F32R)
    qb_lo = sb("qb_lo", [P, T], F32R)
    v2_sb = sb("v2_sb", [P, TILES, V2P], F16)
    qm_b = sb("qm_b", [P, B, S], F32R)
    k_one = sb("k_one", [P, P], F32R)
    s32 = sb("s32", [P, 3, BANK], F32)
    p32b = sb("p32b", [P, RING, BANK], F32)
    junk_b = sb("junk_b", [P, S], BF16)
    max_b = sb("max_b", [P, B, QT], F32)
    neg_diag_b = sb("neg_diag_b", [QT, QT], F32)
    slope_sb = sb("slope_sb", [P, 1], F32)
    wqk_raw = sb("wqk_raw", [P, E], F32)
    wqk_hi = sb("wqk_hi", [P, E], F32R)
    wqk_lo = sb("wqk_lo", [P, E], F32R)
    wv2_raw = sb("wv2_raw", [P, E], F32)
    wv2_abs = sb("wv2_abs", [P, E], F32)
    wv2_hi = sb("wv2_hi", [P, E], F32R)
    wv2_lo = sb("wv2_lo", [P, E], F32R)
    l1_b = sb("l1_b", [P, 3], F32)
    diag_b = sb("diag_b", [P, E], F32)
    l1_cols = sb("l1_cols", [P, E], F32)
    ob_den = sb("ob_den", [P, 2], F32)
    ob_out = sb("ob_out", [P, 2, E], F32)

    ctx = ExitStack()
    with ctx:
        psum = ctx.enter_context(nc.psum_tensor("psum", [P, 8 * BANK], F32))

        def bank(n, cols=BANK):
            return psum[:, n * BANK:n * BANK + cols]

        MAXB, PVB, MISC = 3, 5, 7

        def sem(name):
            return ctx.enter_context(nc.semaphore(name))

        x_in = [sem(f"x_in{g}") for g in range(CHUNKS)]
        wv_in, wo_in, ffn_in, bias_in = sem("wv_in"), sem("wo_in"), sem("ffn_in"), sem("bias_in")
        pair_in, attn_b_in = sem("pair_in"), sem("attn_b_in")
        v_in = [sem("v_in0"), sem("v_in1")]
        o_back = [sem("o_back0"), sem("o_back1")]
        scratch_out = [sem("scratch_out0"), sem("scratch_out1")]
        result_out = sem("result_out")
        zeroed, ident_ready, half_ready, ones_ready = sem("zeroed"), sem("ident_ready"), sem("half_ready"), sem("ones_ready")
        tri_ready, diag_ready, rows_ready = sem("tri_ready"), sem("diag_ready"), sem("rows_ready")
        bn_done, aggr_done, eps_done, rstd_done = sem("bn_done"), sem("aggr_done"), sem("eps_done"), sem("rstd_done")
        xn_ready, xt_full, xt_hi_done, xt_lo_done = sem("xn_ready"), sem("xt_full"), sem("xt_hi_done"), sem("xt_lo_done")
        abs_done, l1_full, gain_sum, gain_done = sem("abs_done"), sem("l1_full"), sem("gain_sum"), sem("gain_done")
        wv_scaled, wv_hi_done, wv_lo_done = sem("wv_scaled"), sem("wv_hi_done"), sem("wv_lo_done")
        l1r_full, l1r_done, wo_scaled = sem("l1r_full"), sem("l1r_done"), sem("wo_scaled")
        bo_full, wts_hi_done, wts_lo_done = sem("bo_full"), sem("wts_hi_done"), sem("wts_lo_done")
        v_full, v_hi_done, v_lo_done, v_one = sem("v_full"), sem("v_hi_done"), sem("v_lo_done"), sem("v_one")
        split_hi, split_lo = sem("split_hi"), sem("split_lo")
        piece_full, piece_hi, piece_lo = sem("piece_full"), sem("piece_hi"), sem("piece_lo")
        k_moved = [sem("k_moved0"), sem("k_moved1")]
        q_moved = [sem("q_moved0"), sem("q_moved1")]
        max_full, max_done, mt_full, mrow_done = sem("max_full"), sem("max_done"), sem("mt_full"), sem("mrow_done")
        st_full, exp_done, phi_done, plo_done = sem("st_full"), sem("exp_done"), sem("phi_done"), sem("plo_done")
        pv_done, o_inverse, o_ready = sem("pv_done"), sem("o_inverse"), sem("o_ready")
        ot_full, ot_hi_done, ot_lo_done, ot_used = sem("ot_full"), sem("ot_hi_done"), sem("ot_lo_done"), sem("ot_used")
        yT_ready, yt_full, res_done = sem("yT_ready"), sem("yt_full"), sem("res_done")
        h_full, h32_done, h_hi_done, h_lo_done, h_used = (
            sem("h_full"), sem("h32_done"), sem("h_hi_done"), sem("h_lo_done"), sem("h_used"))
        steps_b, bias_made, bias_ready, rows_b = sem("steps_b"), sem("bias_made"), sem("bias_ready"), sem("rows_b")
        wqk_hi_done, wqk_split = sem("wqk_hi_done"), sem("wqk_split")
        l1b_made, wv2_scaled, wv2_t, wv2_hi_done, wv2_split = (
            sem("l1b_made"), sem("wv2_scaled"), sem("wv2_t"), sem("wv2_hi_done"), sem("wv2_split"))
        diagb_made, l1c_full, l1c_done = sem("diagb_made"), sem("l1c_full"), sem("l1c_done")
        qb_full, qb_hi_done, qb_lo_done = sem("qb_full"), sem("qb_hi_done"), sem("qb_lo_done")
        v2_full, v2_hi_done, v2_lo_done, v2_one = sem("v2_full"), sem("v2_hi_done"), sem("v2_lo_done"), sem("v2_one")
        maxb_full, maxb_done, mtb_full, mrowb_done = sem("maxb_full"), sem("maxb_done"), sem("mtb_full"), sem("mrowb_done")
        sb_full, s32_done, expb_done, phib_done, plob_done = (
            sem("sb_full"), sem("s32_done"), sem("expb_done"), sem("phib_done"), sem("plob_done"))
        pvb_done, ob_inverse, ob_read, resb_done = sem("pvb_done"), sem("ob_inverse"), sem("ob_read"), sem("resb_done")

        LOOPS = (HEADS - 4) // 4
        LAST_SLOTS = range(1, 4)

        def pieces_after(t, k):
            if isinstance(t, int):
                return min(2 * (4 * t + k) + 8, 4 * PAIRS)
            return 8 * t + (2 * k + 8)

        def max_banks(j, c0, c1):
            first = (MAXB + (CT - 1 - j) % 2 if j < CT else MAXB) * BANK
            return psum[:, first + c0:first + c1]

        def ring_at(k, r):
            return (NU * k + r) % RING

        def set_of(k, offset=0):
            return (k + offset) % 4

        block = ctx.enter_context(nc.Block())

        @block.sync
        def _(sp):
            wk_pair = Wk.rearrange("(q a) e d -> q e a d", a=2)
            wq_pair = Wq.rearrange("(q a) e d -> q e a d", a=2)
            bk_pair = bk.rearrange("(q a) d -> q (a d)", a=2)
            bq_pair = bq.rearrange("(q a) d -> q (a d)", a=2)

            def load_biases(q, par):
                for which, b in enumerate((bk_pair, bq_pair)):
                    sp.dma_start(w_b[:, par, which:which + 1], b[q].unsqueeze(1)).then_inc(pair_in, 16)

            def load_weights(q):
                for which, w in enumerate((wk_pair, wq_pair)):
                    sp.dma_start(w_raw[:, which, :].rearrange("p (a d) -> p a d", a=2), w[q]).then_inc(pair_in, 16)

            def move_k(par, s):
                rows = slice(DH * par, DH * par + DH)
                hi, lo = st_hi[rows, 0, :].bitcast(F32), st_lo[rows, 0, :].bitcast(F32)
                sp.dma_start(k_hh[0:DH, s, :].bitcast(F32), hi).then_inc(k_moved[par], 16)
                sp.dma_start(k_hh[DH:P, s, :].bitcast(F32), hi).then_inc(k_moved[par], 16)
                sp.dma_start(k_l1[0:DH, s, :].bitcast(F32), lo).then_inc(k_moved[par], 16)

            def move_q(par, s):
                rows = slice(DH * par, DH * par + DH)
                hi, lo = st_hi[rows, 1, :].bitcast(F32), st_lo[rows, 1, :].bitcast(F32)
                sp.dma_start(q_hl[0:DH, s, :].bitcast(F32), hi).then_inc(q_moved[par], 16)
                sp.dma_start(q_hl[DH:P, s, :].bitcast(F32), lo).then_inc(q_moved[par], 16)
                sp.dma_start(q_hm[0:DH, s, :].bitcast(F32), hi).then_inc(q_moved[par], 16)

            for g in range(CHUNKS):
                sp.dma_start(x_sb[:, CT * g:CT * (g + 1), :], x_tok[:, CT * g:CT * (g + 1), :]).then_inc(x_in[g], 16)
                if g == 0:
                    load_weights(0)
                    load_biases(0, 0)
            sp.wait_ge(rows_ready, 1)
            for pair in range(2):
                sp.wait_ge(split_lo, pair + 1)
                if pair == 1:
                    sp.wait_ge(piece_lo, 4)
                load_biases(pair + 1, (pair + 1) % 2)
                load_weights(pair + 1)
                sp.wait_ge(piece_lo, 4 * pair + 2)
                for par in range(2):
                    move_k(par, 2 * pair + par)
                sp.wait_ge(piece_lo, 4 * pair + 4)
                for par in range(2):
                    move_q(par, 2 * pair + par)
            sp.wait_ge(v_one, 1)
            for n in range(2 * B):
                sp.wait_ge(v_lo_done, QT * (n + 1))
                h0 = (n % B) * H + (n // B) * VH
                sp.dma_start(v_dram[h0:h0 + VH].rearrange("h p n -> p h n"),
                             v_stage[n % 2].rearrange("p h t c -> p h (t c)")).then_inc(scratch_out[n % 2], 16)
            for n in range(2):
                sp.wait_ge(scratch_out[n], 16 * B)
            sp.wait_ge(wts_lo_done, 3)

            def fixed(value):
                return value if isinstance(value, int) else sp.snap(value)

            def sp_slot(t, k, project):
                u = fixed(4 * t + k)
                scored, pair = fixed(NU * u), fixed(2 * t + (k + 5) // 2)
                earlier, index, projected = fixed(4 * (pair - 1)), fixed(pair % PP), fixed(pieces_after(t, k))
                stored, pair_out = fixed(NG * (4 * t + k) + SUMS), fixed(2 * t + (k // 2 - 1))
                if k or not isinstance(t, int):
                    sp.wait_ge(st_full, scored)
                sp.dma_start(v_sb[:, k % 2, :, :].rearrange("p t c -> p (t c)"), v_dram[u]).then_inc(v_in[k % 2], 16)
                if project and k % 2 == 1:
                    sp.wait_ge(piece_lo, earlier)
                    load_biases(index, ((k + 5) // 2) % 2)
                    sp.wait_ge(split_lo, pair)
                    load_weights(index)
                    sp.wait_ge(piece_lo, projected)
                    move_k(0, set_of(k, 3))
                if project and k % 2 == 0 and k:
                    move_k(1, set_of(k, 3))
                    sp.wait_ge(piece_lo, projected)
                    move_q(0, set_of(k, 2))
                    move_q(1, set_of(k, 3))
                if k % 2 == 0 and k:
                    store_pair(k, stored, pair_out)

            def store_pair(k, stored, index):
                sp.wait_ge(o_ready, stored)
                par = (k // 2 - 1) % 2
                sp.dma_start(o_dram[index], o_sb[:, par, :, :]).then_inc(scratch_out[par], 16)

            sp_slot(0, 0, True)
            with sp.Fori(0, LOOPS) as t:
                for k in range(1, 5):
                    sp_slot(t, k, True)
            def load_outputs(c):
                b, t0 = c * CT // QT, c * CT % QT
                sp.dma_start(o_in[c % 2][:, :, :, :], o_dram[PP * b:PP * (b + 1), :, t0:t0 + CT, :].rearrange("h p t n -> p h t n"))\
                    .then_inc(o_back[c % 2], 16)

            for k in LAST_SLOTS:
                sp_slot(LOOPS, k, False)
                if k == 2:
                    for n in range(2):
                        sp.wait_ge(scratch_out[n], 16 * (B + PP // 2))
                        sp.wait_ge(k_moved[n], 48 * PAIRS)
                        sp.wait_ge(q_moved[n], 48 * PAIRS)
                    load_outputs(0)
            sp.wait_ge(st_full, NU * HEADS)
            load_outputs(1)
            store_pair(4, SUMS + NG * HEADS, PAIRS - 1)

            for n in range(2):
                sp.wait_ge(scratch_out[n], 16 * (B + PAIRS // 2))
            sp.wait_ge(plo_done, NU * HEADS)
            sp.dma_start(wqk_raw[:, :], Wqk).then_inc(attn_b_in, 16)
            sp.dma_start(wv2_raw[:, :], Wv2).then_inc(attn_b_in, 16)
            sp.dma_start(slope_sb[:, :], slope.partition_broadcast(P)).then_inc(attn_b_in, 16)
            for c in range(2, CHUNKS):
                sp.wait_ge(ot_full, OB * (c - 1))
                load_outputs(c)
            for c in range(CHUNKS):
                sp.wait_ge(res_done, 2 * CHUNKS + c + 1)
                sp.dma_start(out_tok[:, CT * c:CT * (c + 1), :], x_sb[:, CT * c:CT * (c + 1), :]).then_inc(result_out, 16)
            sp.wait_ge(result_out, 16 * CHUNKS)

        @block.tensor
        def _(pe):
            def three(dst, hi, lo, m_hi, m_lo, start=True, stop=True):
                nc.tensor.matmul(dst, hi, m_hi, start=start, stop=False)
                nc.tensor.matmul(dst, lo, m_hi, start=False, stop=False)
                return nc.tensor.matmul(dst, hi, m_lo, start=False, stop=stop)

            def turn_chunk(n):
                pe.wait_ge(xn_ready, n + 1)
                if n >= 2:
                    pe.wait_ge(xt_lo_done, n - 1)
                for j in range(CT):
                    last = nc.tensor.transpose(bank(6 + n % 2)[:, P * j:P * (j + 1)], xn[:, n % 2, j, :], ident[:, :])
                last.then_inc(xt_full, 1)

            pe.wait_ge(ident_ready, 2)
            for c in range(CHUNKS):
                turn_chunk(c)
            pe.wait_ge(abs_done, 1)
            pe.wait_ge(ones_ready, 1)
            for n in range(2):
                last = nc.tensor.matmul(bank(MAXB + n), ones[:, :], wv_abs[:, BANK * n:BANK * (n + 1)], start=True, stop=True)
            last.then_inc(l1_full, 1)
            for k in range(OB):
                last = nc.tensor.matmul(bank(PVB)[:, k:k + 1], wv_abs[:, P * k:P * (k + 1)], ones[:, 0:1], start=True, stop=True)
            last.then_inc(l1r_full, 1)
            pe.wait_ge(wo_in, 16)
            pe.wait_ge(bias_in, 64)
            pe.wait_ge(xt_lo_done, CHUNKS)
            for k in range(OB):
                last = nc.tensor.matmul(bank(PVB + 1)[:, 0:1], wo_raw[:, k, :], bv_sb[:, k:k + 1], start=(k == 0), stop=(k == OB - 1))
            last.then_inc(bo_full, 1)

            def piece(n, pair, par, which, half, b):
                pe.wait_ge(piece_lo, n)
                pe.wait_ge(split_lo, pair + 1)
                cols = slice(S * b + BANK * half, S * b + BANK * (half + 1)) if isinstance(b, int) else bass.ds(b * S + BANK * half, BANK)
                three(bank(MISC), w_hi[:, par, which, :], w_lo[:, par, which, :], xT_hi[:, cols], xT_lo[:, cols]).then_inc(piece_full, 1)

            for n in range(8):
                if n == 0:
                    pe.wait_ge(split_lo, 1)
                    three(bank(MISC), w_hi[:, 0, 0, :], w_lo[:, 0, 0, :], xT_hi[:, 0:BANK], xT_lo[:, 0:BANK]).then_inc(piece_full, 1)
                else:
                    piece(n, n // 4, n // 4, n % 4 // 2, n % 2, 0)

            pe.wait_ge(wv_lo_done, 1)
            n = 0
            for half in range(2):
                cols = slice(BANK * half, BANK * (half + 1))
                for tile in range(TILES):
                    if n >= ST_RING:
                        pe.wait_ge(v_lo_done, n - ST_RING + 1)
                    rows = slice(P * tile, P * (tile + 1))
                    three(bank(n % ST_RING), xT_hi[:, rows], xT_lo[:, rows], wv_hi[:, cols], wv_lo[:, cols]).then_inc(v_full, 1)
                    n += 1

            def max_tile(v, n, s):
                j = MAX_ORDER[n]
                if not (isinstance(v, int) and v == 0 and n == 0):
                    pe.wait_ge(max_done, QT * v + (n - max_alone(j)))
                cols = P * (j + 1)
                for c0 in range(0, cols, BANK):
                    c1 = min(c0 + BANK, cols)
                    last = nc.tensor.matmul(max_banks(j, c0, c1), q_hl[:, s, P * j:P * (j + 1)], k_hh[:, s, c0:c1],
                                            start=True, stop=True)
                last.then_inc(max_full, 1)

            def max_alone(j):
                return int(j < CT - 1)

            def turn_maxima(v, par, pieces):
                pe.wait_ge(max_done, QT * (v + 1))
                pe.wait_ge(piece_lo, pieces)
                nc.tensor.transpose(bank(MISC)[0:QT, 0:P], maxima[:, par, :], ident[:, :]).then_inc(mt_full, 1)

            def outputs(w, k, step, uses):
                par = (k - 1) % 2
                for j, kt in PV_PAIRS[PV_STEP * step:PV_STEP * (step + 1)]:
                    g, r = GROUP_OF[j]
                    if kt == 0:
                        if j == 0:
                            pe.wait_ge(v_in[par], 16 * (uses + 1))
                        if j == 0 or need_units[j] > need_units[j - 1]:
                            pe.wait_ge(plo_done, NU * w + need_units[j])
                        if r == 0:
                            pe.wait_ge(o_ready, NG * w + (g + (SUMS - 1)))
                    dst = bank(PVB + g)[:, VW * r:VW * (r + 1)]
                    cols = slice(place[kt, j], place[kt, j] + P)
                    v_hi_one, v_lo = v_sb[:, par, kt, DH:DH + VW], v_sb[:, par, kt, 0:DH]
                    nc.tensor.matmul(dst, p_hl[:, par, 0, cols], v_hi_one, start=(kt == 0), stop=False)
                    nc.tensor.matmul(dst[:, 0:DH], p_hl[:, par, 0, cols], v_lo, start=False, stop=False)
                    last = nc.tensor.matmul(dst, p_hl[:, par, 1, cols], v_hi_one, start=False, stop=(kt == j))
                    if kt == j:
                        last.then_inc(pv_done, 1)

            def scores(u, k, r):
                s = set_of(k)
                if r >= ST_RING or not (isinstance(u, int) and u == 0):
                    pe.wait_ge(phi_done, NU * u + (r - ST_RING + 1))
                if r == 0:
                    pe.wait_ge(mrow_done, u + 1)
                for i, q0, n, col in units[r]:
                    keys = slice(P * i, P * (i + 1))
                    dst = bank(r % ST_RING)[:, col:col + n]
                    diagonal = q0 == P * i
                    nc.tensor.matmul(dst, k_hh[:, s, keys], q_hl[:, s, q0:q0 + n], start=True, stop=False)
                    last = nc.tensor.matmul(dst, k_l1[:, s, keys], q_hm[:, s, q0:q0 + n], start=False, stop=not diagonal)
                    if diagonal:
                        last = nc.tensor.matmul(dst[:, 0:P], ident_b[:, :], mask_t[:, :], start=False, stop=True)
                last.then_inc(st_full, 1)

            def pe_slot(t, k, projects, takes_maxima):
                u = 4 * t + k

                def maximum(v, n):
                    if takes_maxima:
                        if n == 0:
                            par, count = (k + 1) % 2, 2 * t + (k + 1) // 2 + 1
                            pe.wait_ge(k_moved[par], 48 * count)
                            pe.wait_ge(q_moved[par], 48 * count)
                        max_tile(v, n, set_of(k, 1))

                def products(step):
                    if not (isinstance(u, int) and u == 0):
                        outputs(u - 1, k, step, 2 * t + (k - 1) // 2)

                def project(half):
                    if projects:
                        if half == 0:
                            pe.wait_ge(mrow_done, u + 1)
                        piece(2 * u + (6 + half), 2 * t + (k + 3) // 2, ((k + 3) // 2) % 2, (k + 1) % 2, half, (t + 1) // (PP // 2))

                def rows():
                    if takes_maxima:
                        turn_maxima(u + 1, (k + 1) % 2, pieces_after(t, k))

                maximum(u + 1, 0)
                products(0)
                products(1)
                project(0)
                scores(u, k, 0)
                maximum(u + 1, 1)
                scores(u, k, 1)
                scores(u, k, 2)
                project(1)
                maximum(u + 1, 2)
                products(2)
                products(3)
                products(4)
                products(5)
                maximum(u + 1, 3)
                scores(u, k, 3)
                scores(u, k, 4)
                products(6)
                maximum(u + 1, 4)
                scores(u, k, 5)
                maximum(u + 1, 5)
                scores(u, k, 6)
                maximum(u + 1, 6)
                products(7)
                maximum(u + 1, 7)
                products(8)
                scores(u, k, 7)
                rows()
                scores(u, k, 8)

            pe.wait_ge(gain_sum, 2)
            pe.wait_ge(k_moved[0], 48)
            pe.wait_ge(q_moved[0], 48)
            for n in range(QT):
                max_tile(0, n, 0)
            turn_maxima(0, 0, 8)
            pe.wait_ge(rows_ready, 1)
            pe.wait_ge(tri_ready, 2)
            pe.wait_ge(v_lo_done, 2 * TILES)

            pe_slot(0, 0, False, True)
            with pe.Fori(0, LOOPS) as t:
                for k in range(1, 5):
                    pe_slot(t, k, True, True)
            for k in LAST_SLOTS:
                pe_slot(LOOPS, k, False, k < 3)
            for step in range(NU):
                outputs(HEADS - 1, 4, step, PAIRS - 1)

            def turn_result(n):
                pe.wait_ge(yT_ready, n + 1)
                if n >= 1:
                    pe.wait_ge(res_done, n)
                else:
                    pe.wait_ge(o_ready, SUMS + NG * HEADS)
                for j in range(CT):
                    last = nc.tensor.transpose(bank(5)[:, P * j:P * (j + 1)], yT[:, n % 2, P * j:P * (j + 1)], ident[:, :])
                last.then_inc(yt_full, 1)

            pe.wait_ge(phi_done, NU * HEADS)
            for n in range(OB * CHUNKS + 2):
                if n < OB * CHUNKS:
                    c, blk = divmod(n, OB)
                    if blk == 0:
                        pe.wait_ge(o_back[c % 2], 16 * (c // 2 + 1))
                    if n >= BLOCKS:
                        pe.wait_ge(ot_lo_done, n - BLOCKS + 1)
                    for j in range(CT):
                        last = nc.tensor.transpose(bank(BLOCK_BANKS[n % BLOCKS])[:, P * j:P * (j + 1)], o_in[c % 2][:, blk, j, :], ident[:, :])
                    last.then_inc(ot_full, 1)
                if n >= 2:
                    c, blk = divmod(n - 2, OB)
                    m = (n - 2) % BLOCKS
                    pe.wait_ge(ot_lo_done, n - 1)
                    if blk == 0 and c >= 2:
                        pe.wait_ge(yT_ready, c - 1)
                    three(bank(2 + c % 2), wo_hi[:, blk, :], wo_lo[:, blk, :], oT_hi[:, m, :], oT_lo[:, m, :],
                          start=(blk == 0), stop=(blk == OB - 1)).then_inc(ot_used, 1)
                    if blk == 3 and c >= 1:
                        turn_result(c - 1)
                    if blk == 2 and c == 2:
                        pe.wait_ge(wv2_scaled, 1)
                        nc.tensor.transpose(bank(6)[:, 0:P], wv2_abs[:, :], ident[:, :]).then_inc(wv2_t, 1)
                        pe.wait_ge(diagb_made, 1)
                        nc.tensor.matmul(bank(7)[:, 0:P], ones[:, :], diag_b[:, :], start=True, stop=True).then_inc(l1c_full, 1)
                    if blk == 5 and c == CHUNKS - 1:
                        pe.wait_ge(wv2_split, 1)
                        pe.wait_ge(l1c_done, 1)
                        turn_chunk(CHUNKS)

            def feed_forward(layer):
                f0 = FW * CHUNKS * layer
                for n in range(FW * CHUNKS + 2):
                    if n < FW * CHUNKS:
                        c, m = divmod(n, FW)
                        if m == 0:
                            pe.wait_ge(xt_lo_done, CHUNKS * (1 + 2 * layer) + c + 1)
                        if f0 + n >= BLOCKS:
                            pe.wait_ge(h_hi_done, f0 + n - BLOCKS + 1)
                        blk, cols = slice(P * m, P * (m + 1)), slice(BANK * c, BANK * (c + 1))
                        three(bank(BLOCK_BANKS[n % BLOCKS]), w1_hi[:, blk], w1_lo[:, blk], xT_hi[:, cols], xT_lo[:, cols]).then_inc(h_full, 1)
                    if n >= 2:
                        c, m = divmod(n - 2, FW)
                        y = CHUNKS * (1 + layer) + c
                        r = (n - 2) % BLOCKS
                        pe.wait_ge(h_lo_done, f0 + n - 1)
                        if m == 0:
                            pe.wait_ge(yT_ready, y - 1)
                        three(bank(2 + y % 2), w2_hi[:, m, :], w2_lo[:, m, :], h_hi[:, r, :], h_lo[:, r, :],
                              start=(m == 0), stop=(m == FW - 1)).then_inc(h_used, 1)
                        if m == 0 and (layer == 0 or c + 1 < CHUNKS):
                            turn_chunk(CHUNKS * (1 + 2 * layer) + c + 1)
                        if m == 1 and not (layer == 1 and c == 0):
                            turn_result(y - 1)

            feed_forward(0)

            def max_tile_b(b, n):
                j = QT - 1 - n
                if b or n:
                    pe.wait_ge(maxb_done, QT * b + n)
                cols = P * (j + 1)
                for c0 in range(0, cols, BANK):
                    c1 = min(c0 + BANK, cols)
                    last = nc.tensor.matmul(psum[:, 2 * BANK + c0:2 * BANK + c1], qb_hi[:, S * b + P * j:S * b + P * (j + 1)],
                                            xT_hi[:, S * b + c0:S * b + c1], start=True, stop=True)
                last.then_inc(maxb_full, 1)

            def turn_maxima_b(b):
                pe.wait_ge(maxb_done, QT * (b + 1))
                if b == 0:
                    pe.wait_ge(v2_lo_done, CHUNKS)
                else:
                    pe.wait_ge(mrowb_done, 1)
                nc.tensor.transpose(bank(1)[0:QT, 0:P], max_b[:, b, :], ident[:, :]).then_inc(mtb_full, 1)

            pe.wait_ge(wqk_split, 1)
            pe.wait_ge(h_lo_done, FW * CHUNKS)
            for c in range(CHUNKS):
                cols = slice(BANK * c, BANK * (c + 1))
                pe.wait_ge(xt_lo_done, 2 * CHUNKS + c + 1)
                if c:
                    pe.wait_ge(qb_lo_done, c)
                three(bank(0), wqk_hi[:, :], wqk_lo[:, :], xT_hi[:, cols], xT_lo[:, cols]).then_inc(qb_full, 1)
                if c == 0:
                    turn_result(2 * CHUNKS - 1)
                if c + 1 < CHUNKS:
                    turn_chunk(2 * CHUNKS + c + 1)
                if c:
                    pe.wait_ge(v2_lo_done, c)
                for j in range(CT):
                    rows = slice(BANK * c + P * j, BANK * c + P * (j + 1))
                    last = three(bank(1)[:, P * j:P * (j + 1)], xT_hi[:, rows], xT_lo[:, rows], wv2_hi[:, :], wv2_lo[:, :])
                last.then_inc(v2_full, 1)
                if c == 2:
                    pe.wait_ge(yT_ready, 2 * CHUNKS)
                    pe.wait_ge(qb_lo_done, 2)
                if c >= 2:
                    for n in range(4 * (c - 2), 4 * (c - 1)):
                        max_tile_b(0, n)
            turn_maxima_b(0)
            pe.wait_ge(rows_b, 3)
            pe.wait_ge(res_done, 2 * CHUNKS)
            pe.wait_ge(xt_lo_done, 3 * CHUNKS)

            st_bank = (4, 5, 0)

            def scores_b(b, r):
                m = NU * b + r
                if m >= ST_RING:
                    pe.wait_ge(s32_done, m - ST_RING + 1)
                if r == 0:
                    pe.wait_ge(mrowb_done, b + 1)
                    pe.wait_ge(qb_lo_done, CHUNKS)
                for i, q0, n, col in units[r]:
                    keys = slice(S * b + P * i, S * b + P * (i + 1))
                    qs = slice(S * b + q0, S * b + q0 + n)
                    dst = bank(st_bank[m % ST_RING])[:, col:col + n]
                    three(dst, xT_hi[:, keys], xT_lo[:, keys], qb_hi[:, qs], qb_lo[:, qs], stop=False)
                    last = nc.tensor.matmul(dst, k_one[:, :], qm_b[:, b, q0:q0 + n], start=False, stop=True)
                last.then_inc(sb_full, 1)

            def outputs_b(b, step):
                for j, kt in PV_PAIRS[PV_STEP * step:PV_STEP * (step + 1)]:
                    m = QT * b + j
                    if kt == 0:
                        pe.wait_ge(plob_done, NU * b + need_units[j])
                        if m >= 2:
                            pe.wait_ge(ob_read, m - 1)
                        if m == 0:
                            pe.wait_ge(v2_one, 1)
                    dst = bank(6 + m % 2, V2W)
                    cols = slice(place[kt, j], place[kt, j] + P)
                    tile = QT * b + kt
                    v_hi_one, v_lo = v2_sb[:, tile, E:E + V2W], v2_sb[:, tile, 0:E]
                    nc.tensor.matmul(dst, p_hlb[:, b, 0, cols], v_hi_one, start=(kt == 0), stop=False)
                    nc.tensor.matmul(dst[:, 0:E], p_hlb[:, b, 0, cols], v_lo, start=False, stop=False)
                    last = nc.tensor.matmul(dst, p_hlb[:, b, 1, cols], v_hi_one, start=False, stop=(kt == j))
                    if kt == j:
                        last.then_inc(pvb_done, 1)

            for b in range(B + 1):
                for step in range(NU):
                    if b < B:
                        scores_b(b, step)
                    if b + 1 < B and step < QT:
                        max_tile_b(b + 1, step)
                    if b >= 1:
                        outputs_b(b - 1, step)
                if b + 1 < B:
                    turn_maxima_b(b + 1)

            pe.wait_ge(s32_done, NU * B)
            pe.wait_ge(mrowb_done, B)
            pe.wait_ge(ob_read, QT * B)
            turn_chunk(3 * CHUNKS)
            feed_forward(1)
            turn_result(3 * CHUNKS - 1)

        @block.scalar
        def _(act):
            act.dma_start(wv_raw[:, :].rearrange("p (h d) -> p h d", h=H), Wv.rearrange("h e d -> e h d")).then_inc(wv_in, 16)
            act.dma_start(bv_sb[:, :], bv.rearrange("(q a) d -> (a d) q", a=2), allow_slow_non_contiguous=True).then_inc(bias_in, 16)
            act.dma_start(bo_sb[:, :], bo.unsqueeze(1)).then_inc(bias_in, 16)
            act.dma_start(b1_sb[:, :], b1.rearrange("(m p) -> p m", p=P), allow_slow_non_contiguous=True).then_inc(bias_in, 16)
            act.dma_start(b2_sb[:, :], b2.unsqueeze(1)).then_inc(bias_in, 16)
            act.dma_start(wo_raw[:, :, :], Wo.rearrange("(k p) e -> p k e", p=P)).then_inc(wo_in, 16)
            act.dma_start(w1_raw[:, :], w1).then_inc(ffn_in, 16)
            act.dma_start(w2_raw[:, :, :], w2.rearrange("(m p) e -> p m e", p=P)).then_inc(ffn_in, 16)

            def split_high(pair, par):
                act.wait_ge(pair_in, 64 * (pair + 1))
                nc.scalar.copy(w_hi[:, par, :, :], w_raw[:, :, :]).then_inc(split_hi, 1)

            def chunk_high(n):
                act.wait_ge(xt_full, n + 1)
                c = n % CHUNKS
                nc.scalar.copy(xT_hi[:, BANK * c:BANK * (c + 1)], bank(6 + n % 2)).then_inc(xt_hi_done, 1)

            def piece_high(n, pair, par, which, half):
                act.wait_ge(piece_full, n + 1)
                if half == 0 and not (isinstance(pair, int) and pair == 0):
                    moved = (k_moved, q_moved)[which]
                    act.wait_ge(moved[0], 48 * pair)
                    act.wait_ge(moved[1], 48 * pair)
                nc.scalar.activation(st_hi[:, which, BANK * half:BANK * (half + 1)], bank(MISC), ACT.Identity,
                                     bias=w_b[:, par, which:which + 1]).then_inc(piece_hi, 1)

            split_high(0, 0)
            act.wait_ge(wv_in, 16)
            nc.scalar.activation(wv_abs[:, :], wv_raw[:, :], ACT.Abs).then_inc(abs_done, 1)
            for c in range(CHUNKS):
                chunk_high(c)
            for n in range(8):
                if n == 2:
                    split_high(1, 1)
                piece_high(n, n // 4, n // 4, n % 4 // 2, n % 2)
            act.wait_ge(wv_scaled, 1)
            nc.scalar.copy(wv_hi[:, :], wv_raw[:, :]).then_inc(wv_hi_done, 1)
            act.wait_ge(wo_scaled, 1)
            nc.scalar.copy(wo_hi[:, :, :], wo_raw[:, :, :]).then_inc(wts_hi_done, 1)
            act.wait_ge(ffn_in, 32)
            nc.scalar.copy(w1_hi[:, :], w1_raw[:, :]).then_inc(wts_hi_done, 1)
            nc.scalar.copy(w2_hi[:, :, :], w2_raw[:, :, :]).then_inc(wts_hi_done, 1)
            for n in range(2 * TILES):
                act.wait_ge(v_full, n + 1)
                stage = n // QT
                if n % QT == 0 and stage >= 2:
                    act.wait_ge(scratch_out[stage % 2], 16)
                nc.scalar.copy(v_stage[stage % 2][:, :, n % QT, DH:2 * DH],
                               bank(n % ST_RING).rearrange("p (h d) -> p h d", d=DH)).then_inc(v_hi_done, 1)
            for n in range(2):
                act.wait_ge(scratch_out[n], 16 * B)
            act.wait_ge(wts_lo_done, 3)
            act.wait_ge(v_lo_done, 2 * TILES)

            def exponentials(u, k, r):
                act.wait_ge(st_full, NU * u + (r + 1))
                if r >= RING or not (isinstance(u, int) and u == 0):
                    act.wait_ge(plo_done, NU * u + (r - RING + 1))
                src = bank(r % ST_RING)
                nc.scalar.activation(p32[:, ring_at(k, r), :], src, ACT.Exp, scale=SCALE_A).then_inc(exp_done, 1)
                nc.scalar.activation(p_hl[:, k % 2, 0, BANK * r:BANK * (r + 1)], src, ACT.Exp, scale=SCALE_A).then_inc(phi_done, 1)

            def act_slot(t, k, projects, split):
                u = 4 * t + k

                def project(half):
                    if projects:
                        piece_high(2 * u + (6 + half), 2 * t + (k + 3) // 2, ((k + 3) // 2) % 2, (k + 1) % 2, half)

                project(0)
                exponentials(u, k, 0)
                if split:
                    split_high(2 * t + (k + 4) // 2, ((k + 4) // 2) % 2)
                exponentials(u, k, 1)
                project(1)
                exponentials(u, k, 2)
                exponentials(u, k, 3)
                exponentials(u, k, 4)
                exponentials(u, k, 5)
                exponentials(u, k, 6)
                exponentials(u, k, 7)
                exponentials(u, k, 8)

            act_slot(0, 0, False, True)
            with act.Fori(0, LOOPS) as t:
                for k in range(1, 5):
                    act_slot(t, k, True, k % 2 == 0)
            for k in LAST_SLOTS:
                act_slot(LOOPS, k, False, False)

            def result_high(n, bias):
                if n >= 2:
                    act.wait_ge(yt_full, n - 1)
                nc.scalar.activation(yT[:, n % 2, :], bank(2 + n % 2), ACT.Identity, bias=bias).then_inc(yT_ready, 1)

            for n in range(OB * CHUNKS):
                c, blk = divmod(n, OB)
                act.wait_ge(ot_full, n + 1)
                if n >= BLOCKS:
                    act.wait_ge(ot_used, n - BLOCKS + 1)
                nc.scalar.copy(oT_hi[:, n % BLOCKS, :], bank(BLOCK_BANKS[n % BLOCKS])).then_inc(ot_hi_done, 1)
                if blk == 2 and c >= 1:
                    act.wait_ge(ot_used, OB * c)
                    result_high(c - 1, bo_all[:, 0:1])
                if blk == 5 and c == 0:
                    act.wait_ge(attn_b_in, 48)
                    nc.scalar.activation(wv2_abs[:, :], wv2_raw[:, :], ACT.Abs, accum_out=l1_b[:, 0:1]).then_inc(l1b_made, 1)
                if blk == 5 and c == 2:
                    nc.scalar.copy(wqk_hi[:, :], wqk_raw[:, :]).then_inc(wqk_hi_done, 1)
                    act.wait_ge(wv2_t, 1)
                    nc.scalar.copy(wv2_hi[:, :], bank(6)[:, 0:P]).then_inc(wv2_hi_done, 1)
            chunk_high(CHUNKS)
            act.wait_ge(ot_used, OB * CHUNKS)
            result_high(CHUNKS - 1, bo_all[:, 0:1])

            def feed_forward(layer):
                f0 = FW * CHUNKS * layer
                for n in range(FW * CHUNKS):
                    c, m = divmod(n, FW)
                    act.wait_ge(h_full, f0 + n + 1)
                    r = n % BLOCKS
                    if f0 + n >= BLOCKS:
                        before = f0 + n - BLOCKS + 1 if n >= BLOCKS else f0
                        act.wait_ge(h_lo_done, before)
                        act.wait_ge(h_used, before)
                    nc.scalar.activation(h32[:, r, :], bank(BLOCK_BANKS[r]), ACT.Relu, bias=b1_sb[:, m:m + 1]).then_inc(h32_done, 1)
                    nc.scalar.activation(h_hi[:, r, :], bank(BLOCK_BANKS[r]), ACT.Relu, bias=b1_sb[:, m:m + 1]).then_inc(h_hi_done, 1)
                    if m == 1 and c >= 1:
                        act.wait_ge(h_used, f0 + FW * c)
                        result_high(CHUNKS * (1 + layer) + c - 1, b2_sb[:, 0:1])
                    if m == 2 and (layer == 0 or c + 1 < CHUNKS):
                        chunk_high(CHUNKS * (1 + 2 * layer) + c + 1)
                act.wait_ge(h_used, f0 + FW * CHUNKS)
                result_high(CHUNKS * (2 + layer) - 1, b2_sb[:, 0:1])

            feed_forward(0)
            for c in range(CHUNKS):
                act.wait_ge(qb_full, c + 1)
                nc.scalar.mul(qb_hi[:, BANK * c:BANK * (c + 1)], bank(0), SCALE_B).then_inc(qb_hi_done, 1)
                if c + 1 < CHUNKS:
                    chunk_high(2 * CHUNKS + c + 1)
                act.wait_ge(v2_full, c + 1)
                nc.scalar.copy(v2_sb[:, CT * c:CT * (c + 1), E:2 * E], bank(1).rearrange("p (t e) -> p t e", e=E)).then_inc(v2_hi_done, 1)
            for m in range(NU * B):
                b, r = m // NU, m % NU
                act.wait_ge(s32_done, m + 1)
                if m >= RING:
                    act.wait_ge(plob_done, m - RING + 1)
                src = s32[:, m % 3, :]
                nc.scalar.activation(p32b[:, m % RING, :], src, ACT.Exp).then_inc(expb_done, 1)
                nc.scalar.activation(p_hlb[:, b, 0, BANK * r:BANK * (r + 1)], src, ACT.Exp).then_inc(phib_done, 1)
            chunk_high(3 * CHUNKS)
            feed_forward(1)

        @block.vector
        def _(dve):
            def chunk_stats(n):
                c = n % CHUNKS
                for j in range(CT * c, CT * (c + 1)):
                    last = nc.vector.bn_stats(stats[:, j, :], x_sb[:, j, :])
                last.then_inc(bn_done, 1)
                dve.wait_ge(bn_done, n + 1)
                for j in range(CT * c, CT * (c + 1)):
                    last = nc.vector.bn_aggr(mean_var[:, j, :], stats[:, j, :])
                last.then_inc(aggr_done, 1)

            def chunk_norm(n):
                c = n % CHUNKS
                dve.wait_ge(rstd_done, n + 1)
                if n >= 2:
                    dve.wait_ge(xt_full, n - 1)
                for j in range(CT):
                    tile = CT * c + j
                    last = nc.vector.tensor_scalar(xn[:, n % 2, j, :], x_sb[:, tile, :], mean_var[:, tile, 0:1], rstd[:, tile:tile + 1],
                                                   ALU.subtract, ALU.mult)
                last.then_inc(xn_ready, 1)

            def chunk_low(n):
                dve.wait_ge(xt_hi_done, n + 1)
                c = n % CHUNKS
                cols = slice(BANK * c, BANK * (c + 1))
                nc.vector.tensor_tensor(xT_lo[:, cols], bank(6 + n % 2), xT_hi[:, cols], ALU.subtract).then_inc(xt_lo_done, 1)

            def piece_low(n, par, which, half):
                dve.wait_ge(piece_hi, n + 1)
                cols = slice(BANK * half, BANK * (half + 1))
                nc.vector.scalar_tensor_tensor(out=st_lo[:, which, cols], in0=bank(MISC), scalar=w_b[:, par, which:which + 1],
                                               in1=st_hi[:, which, cols], op0=ALU.add, op1=ALU.subtract).then_inc(piece_lo, 1)

            nc.vector.memset(minus_half[:, :], -0.5).then_inc(half_ready, 1)
            nc.vector.memset(ones[:, :], 1.0).then_inc(ones_ready, 1)
            for c in range(CHUNKS):
                dve.wait_ge(x_in[c], 16)
                chunk_stats(c)
            chunk_norm(0)
            chunk_norm(1)
            for c in range(CHUNKS):
                chunk_low(c)
                if c + 2 < CHUNKS:
                    chunk_norm(c + 2)
            dve.wait_ge(l1r_full, 1)
            nc.vector.tensor_scalar(l1_rows[:, :], bank(PVB)[:, 0:OB], TINY, 1.0 / F16_TOP, ALU.add, ALU.mult).then_inc(o_ready, 1)
            dve.wait_ge(bo_full, 1)
            nc.vector.tensor_tensor(bo_all[:, :], bank(PVB + 1)[:, 0:1], bo_sb[:, :], ALU.add).then_inc(o_ready, 1)
            dve.wait_ge(o_ready, SUMS)
            nc.vector.tensor_tensor(wo_raw[:, :, :], wo_raw[:, :, :], l1_rows[:, :].unsqueeze(2).to_broadcast([P, OB, E]), ALU.mult)\
                .then_inc(wo_scaled, 1)
            for n in range(4):
                piece_low(n, 0, n // 2, n % 2)
            dve.wait_ge(l1_full, 1)
            for n in range(2):
                nc.vector.tensor_scalar(wv_gain[:, BANK * n:BANK * (n + 1)], bank(MAXB + n), TINY, None, ALU.add).then_inc(gain_sum, 1)
            dve.wait_ge(gain_sum, 2)
            nc.vector.reciprocal(wv_abs[:, :], wv_gain[:, :]).then_inc(gain_done, 1)
            dve.wait_ge(gain_done, 1)
            nc.vector.scalar_tensor_tensor(out=wv_raw[:, :], in0=wv_abs[:, :], scalar=F16_TOP, in1=wv_raw[:, :],
                                           op0=ALU.mult, op1=ALU.mult).then_inc(wv_scaled, 1)
            for n in range(4, 8):
                piece_low(n, 1, n % 4 // 2, n % 2)
            dve.wait_ge(wv_hi_done, 1)
            nc.vector.tensor_tensor(wv_lo[:, :], wv_raw[:, :], wv_hi[:, :], ALU.subtract).then_inc(wv_lo_done, 1)
            for n in range(2 * TILES):
                dve.wait_ge(v_hi_done, n + 1)
                stage = v_stage[n // QT % 2]
                nc.vector.tensor_tensor(stage[:, :, n % QT, 0:DH], bank(n % ST_RING).rearrange("p (h d) -> p h d", d=DH),
                                        stage[:, :, n % QT, DH:2 * DH], ALU.subtract).then_inc(v_lo_done, 1)

            def take_max(v, par, n):
                j = MAX_ORDER[n]
                cols = P * (j + 1)
                dve.wait_ge(max_full, QT * v + (n + 1))
                nc.vector.memset(gate[:, n % 2:n % 2 + 1], 0.0)
                nc.vector.tensor_tensor_reduce(out=max_junk[:, n % 2, 0:cols], in0=max_banks(j, 0, cols),
                                               in1=mask_s[:, S - cols:S], scale=1.0, scalar=-3.0e38, op0=ALU.add, op1=ALU.max,
                                               accum_out=maxima[:, par, j:j + 1]).then_inc(max_done, 1)

            def max_rows(v, s):
                dve.wait_ge(mt_full, v + 1)
                nc.vector.tensor_tensor(q_hm[DH:DH + QT, s, :].rearrange("p (j q) -> p j q", j=QT),
                                        bank(MISC)[0:QT, 0:P].unsqueeze(1).to_broadcast([QT, QT, P]),
                                        neg_diag[:, :].unsqueeze(2).to_broadcast([QT, QT, P]), ALU.mult).then_inc(mrow_done, 1)

            def outputs_out(w, k, g, pairs_before):
                js = PV_GROUPS[g]
                n = len(js)
                par = (k - 1) // 2 % 2
                src = bank(PVB + g, VW * n).rearrange("p (j c) -> p j c", c=VW)
                dve.wait_ge(pv_done, QT * w + js[-1] + 1)
                nc.vector.reciprocal(o_den[:, g, :], src[:, :, DH]).then_inc(o_inverse, 1)
                if g == 0 and (k - 1) % 2 == 0:
                    dve.wait_ge(scratch_out[par], 16 * (B + pairs_before))
                dve.wait_ge(o_inverse, NG * w + (g + 1))
                c0 = DH * ((k - 1) % 2)
                nc.vector.tensor_tensor(o_sb[:, par, js[0]:js[-1] + 1, c0:c0 + DH], src[:, :, 0:DH],
                                        o_den[:, g, :].unsqueeze(2).to_broadcast([P, n, DH]), ALU.mult).then_inc(o_ready, 1)

            def dve_slot(t, k, projects, takes_maxima):
                u = 4 * t + k

                def maximum(n):
                    if takes_maxima:
                        take_max(u + 1, (k + 1) % 2, n)

                def project(half):
                    if projects:
                        piece_low(2 * u + (6 + half), ((k + 3) // 2) % 2, (k + 1) % 2, half)

                def outputs(g):
                    if not (isinstance(u, int) and u == 0):
                        outputs_out(u - 1, k, g, t + (k - 1) // 4)

                maximum(0)
                project(0)
                maximum(1)
                maximum(2)
                project(1)
                maximum(3)
                outputs(0)
                maximum(4)
                maximum(5)
                maximum(6)
                maximum(7)
                outputs(1)
                if takes_maxima:
                    max_rows(u + 1, set_of(k, 1))

            dve.wait_ge(tri_ready, 2)
            for n in range(QT):
                take_max(0, 0, n)
            dve.wait_ge(diag_ready, 1)
            dve.wait_ge(rows_ready, 1)
            max_rows(0, 0)
            dve_slot(0, 0, False, True)
            with dve.Fori(0, LOOPS) as t:
                for k in range(1, 5):
                    dve_slot(t, k, True, True)
            for k in LAST_SLOTS:
                dve_slot(LOOPS, k, False, k < 3)
            for g in range(NG):
                outputs_out(HEADS - 1, 4, g, LOOPS)

            def add_result(n):
                c = n % CHUNKS
                dve.wait_ge(yt_full, n + 1)
                tiles = slice(CT * c, CT * (c + 1))
                nc.vector.tensor_tensor(x_sb[:, tiles, :], bank(5).rearrange("p (t e) -> p t e", e=E), x_sb[:, tiles, :], ALU.add)\
                    .then_inc(res_done, 1)

            for n in range(OB * CHUNKS):
                c, blk = divmod(n, OB)
                r = n % BLOCKS
                dve.wait_ge(ot_hi_done, n + 1)
                nc.vector.tensor_tensor(oT_lo[:, r, :], bank(BLOCK_BANKS[r]), oT_hi[:, r, :], ALU.subtract).then_inc(ot_lo_done, 1)
                if blk == 2 and c == 1:
                    dve.wait_ge(attn_b_in, 48)
                    dve.wait_ge(l1b_made, 1)
                    nc.vector.tensor_scalar(l1_b[:, 1:2], l1_b[:, 0:1], TINY, 1.0 / F16_TOP, ALU.add, ALU.mult).then_inc(l1b_made, 1)
                    dve.wait_ge(l1b_made, 2)
                    nc.vector.reciprocal(l1_b[:, 2:3], l1_b[:, 1:2]).then_inc(l1b_made, 1)
                    nc.vector.tensor_scalar(diag_b[:, :], ident[:, :], l1_b[:, 1:2], None, ALU.mult).then_inc(diagb_made, 1)
                    dve.wait_ge(l1b_made, 3)
                    nc.vector.tensor_scalar(wv2_abs[:, :], wv2_raw[:, :], l1_b[:, 2:3], None, ALU.mult).then_inc(wv2_scaled, 1)
                if blk == 2 and c == 2:
                    dve.wait_ge(bias_made, 2)
                    nc.vector.tensor_scalar(bias_s[:, :], bias_s[:, :], slope_sb[:, 0:1], None, ALU.mult).then_inc(steps_b, 1)
                    nc.vector.tensor_scalar(bias_t[:, :], bias_t[:, :], slope_sb[:, 0:1], None, ALU.mult).then_inc(steps_b, 1)
                if blk == 5 and c == 2:
                    dve.wait_ge(wqk_hi_done, 1)
                    nc.vector.tensor_tensor(wqk_lo[:, :], wqk_raw[:, :], wqk_hi[:, :], ALU.subtract).then_inc(wqk_split, 1)
                    dve.wait_ge(wv2_hi_done, 1)
                    nc.vector.tensor_tensor(wv2_lo[:, :], bank(6)[:, 0:P], wv2_hi[:, :], ALU.subtract).then_inc(wv2_split, 1)
                    dve.wait_ge(l1c_full, 1)
                    nc.vector.tensor_copy(l1_cols[:, :], bank(7)[:, 0:P]).then_inc(l1c_done, 1)
                if blk == 5 and c >= 1:
                    add_result(c - 1)
                    dve.wait_ge(res_done, c)
                    chunk_stats(CHUNKS + c - 1)
                if c == CHUNKS - 1 and blk in (3, 4):
                    chunk_norm(CHUNKS + blk - 3)
            chunk_low(CHUNKS)

            def feed_forward(layer):
                f0 = FW * CHUNKS * layer
                ln = CHUNKS * (1 + 2 * layer)
                for n in range(FW * CHUNKS):
                    c, m = divmod(n, FW)
                    r = n % BLOCKS
                    dve.wait_ge(h32_done, f0 + n + 1)
                    dve.wait_ge(h_hi_done, f0 + n + 1)
                    nc.vector.tensor_tensor(h_lo[:, r, :], h32[:, r, :], h_hi[:, r, :], ALU.subtract).then_inc(h_lo_done, 1)
                    if m == 2 and (layer == 0 or c + 1 < CHUNKS):
                        chunk_low(ln + c + 1)
                    if m == 3:
                        if layer == 0 or c + 2 < CHUNKS:
                            chunk_norm(ln + c + 2)
                        if not (layer == 1 and c == 0):
                            y = CHUNKS * (1 + layer) + c
                            add_result(y - 1)
                            if layer == 0:
                                dve.wait_ge(res_done, y)
                                chunk_stats(CHUNKS + y - 1)

            feed_forward(0)

            def take_max_b(b, n):
                j = QT - 1 - n
                cols = P * (j + 1)
                dve.wait_ge(maxb_full, QT * b + n + 1)
                nc.vector.tensor_tensor_reduce(out=junk_b[:, 0:cols], in0=psum[:, 2 * BANK:2 * BANK + cols], in1=bias_s[:, S - cols:S],
                                               scale=1.0, scalar=-3.0e38, op0=ALU.add, op1=ALU.max,
                                               accum_out=max_b[:, b, j:j + 1]).then_inc(maxb_done, 1)

            def max_rows_b(b):
                dve.wait_ge(mtb_full, b + 1)
                nc.vector.tensor_tensor(qm_b[0:QT, b, :].rearrange("p (j q) -> p j q", j=QT),
                                        bank(1)[0:QT, 0:P].unsqueeze(1).to_broadcast([QT, QT, P]),
                                        neg_diag_b[:, :].unsqueeze(2).to_broadcast([QT, QT, P]), ALU.mult).then_inc(mrowb_done, 1)

            for c in range(CHUNKS):
                if c == 0:
                    add_result(2 * CHUNKS - 1)
                    dve.wait_ge(res_done, 2 * CHUNKS)
                    chunk_stats(3 * CHUNKS - 1)
                cols = slice(BANK * c, BANK * (c + 1))
                dve.wait_ge(qb_hi_done, c + 1)
                nc.vector.scalar_tensor_tensor(out=qb_lo[:, cols], in0=bank(0), scalar=SCALE_B, in1=qb_hi[:, cols],
                                               op0=ALU.mult, op1=ALU.subtract).then_inc(qb_lo_done, 1)
                if c + 1 < CHUNKS:
                    chunk_low(2 * CHUNKS + c + 1)
                if c + 2 < CHUNKS:
                    chunk_norm(2 * CHUNKS + c + 2)
                dve.wait_ge(v2_hi_done, c + 1)
                tiles = slice(CT * c, CT * (c + 1))
                nc.vector.tensor_tensor(v2_sb[:, tiles, 0:E], bank(1).rearrange("p (t e) -> p t e", e=E), v2_sb[:, tiles, E:2 * E], ALU.subtract)\
                    .then_inc(v2_lo_done, 1)
                if c == 2:
                    dve.wait_ge(bias_ready, 2)
                if c >= 2:
                    for n in range(4 * (c - 2), 4 * (c - 1)):
                        take_max_b(0, n)
            dve.wait_ge(rows_b, 3)
            max_rows_b(0)

            def biased(b, r):
                m = NU * b + r
                dve.wait_ge(sb_full, m + 1)
                if m >= 3:
                    dve.wait_ge(phib_done, m - 2)
                for i, q0, n, col in units[r]:
                    c0 = q0 - P * i
                    last = nc.vector.tensor_tensor(s32[:, m % 3, col:col + n], bank(st_bank[m % ST_RING])[:, col:col + n], bias_t[:, c0:c0 + n], ALU.add)
                last.then_inc(s32_done, 1)

            st_bank = (4, 5, 0)

            def output_b(b, j):
                m = QT * b + j
                src = bank(6 + m % 2, V2W)
                dve.wait_ge(pvb_done, m + 1)
                nc.vector.reciprocal(ob_den[:, m % 2:m % 2 + 1], src[:, E:V2W]).then_inc(ob_inverse, 1)
                dve.wait_ge(ob_inverse, m + 1)
                nc.vector.scalar_tensor_tensor(out=ob_out[:, m % 2, :], in0=src[:, 0:E], scalar=ob_den[:, m % 2:m % 2 + 1],
                                               in1=l1_cols[:, :], op0=ALU.mult, op1=ALU.mult).then_inc(ob_read, 1)
                dve.wait_ge(ob_read, m + 1)
                nc.vector.tensor_tensor(x_sb[:, m, :], ob_out[:, m % 2, :], x_sb[:, m, :], ALU.add).then_inc(resb_done, 1)
                if m % CT == CT - 1:
                    dve.wait_ge(resb_done, m + 1)
                    chunk_stats(3 * CHUNKS + m // CT)

            for b in range(B + 1):
                for step in range(NU):
                    if b < B:
                        biased(b, step)
                    if b + 1 < B and step < QT:
                        take_max_b(b + 1, step)
                    if b >= 1:
                        for j, kt in PV_PAIRS[PV_STEP * step:PV_STEP * (step + 1)]:
                            if kt == j:
                                output_b(b - 1, j)
                if b + 1 < B:
                    max_rows_b(b + 1)
            chunk_norm(3 * CHUNKS)
            chunk_norm(3 * CHUNKS + 1)
            chunk_low(3 * CHUNKS)
            feed_forward(1)
            add_result(3 * CHUNKS - 1)

        @block.gpsimd
        def _(pool):
            nc.gpsimd.memset(ident[:, :], 0.0).then_inc(zeroed, 1)
            nc.gpsimd.memset(ident_b[:, :], 0.0).then_inc(zeroed, 1)
            pool.wait_ge(zeroed, 2)
            for i in (ident, ident_b):
                nc.gpsimd.affine_select(out=i[:, :], in_=i[:, :], compare_op=ALU.not_equal, fill=1.0, base=0,
                                        pattern=[[-1, P]], channel_multiplier=1).then_inc(ident_ready, 1)

            def chunk_rstd(n):
                c = n % CHUNKS
                cols = slice(CT * c, CT * (c + 1))
                pool.wait_ge(aggr_done, n + 1)
                nc.gpsimd.tensor_scalar(var_eps[:, cols], mean_var[:, cols, 1], EPS, None, ALU.add).then_inc(eps_done, 1)
                pool.wait_ge(eps_done, n + 1)
                nc.gpsimd.tensor_tensor(rstd[:, cols], var_eps[:, cols], minus_half[:, :], ALU.pow).then_inc(rstd_done, 1)

            def split_low(pair, par):
                pool.wait_ge(split_hi, pair + 1)
                nc.gpsimd.tensor_tensor(w_lo[:, par, :, :], w_raw[:, :, :], w_hi[:, par, :, :], ALU.subtract).then_inc(split_lo, 1)

            pool.wait_ge(half_ready, 1)
            for c in range(CHUNKS):
                chunk_rstd(c)
            split_low(0, 0)
            nc.gpsimd.memset(mask_s[:, :], 0.0).then_inc(zeroed, 1)
            nc.gpsimd.memset(mask_t[:, :], 0.0).then_inc(zeroed, 1)
            nc.gpsimd.memset(neg_diag[:, :], 0.0).then_inc(zeroed, 1)
            nc.gpsimd.memset(k_l1[:, :, :].bitcast(F32), 0.0).then_inc(zeroed, 1)
            nc.gpsimd.memset(q_hm[:, :, :].bitcast(F32), 0.0).then_inc(zeroed, 1)
            pool.wait_ge(zeroed, 7)
            nc.gpsimd.memset(k_l1[DH:DH + QT, :, :].bitcast(F32), 1.0).then_inc(rows_ready, 1)
            pool.wait_ge(rows_ready, 1)
            split_low(1, 1)
            for s in v_stage:
                last = nc.gpsimd.memset(s[:, :, :, 2 * DH:VP], 1.0)
            last.then_inc(v_one, 1)
            nc.gpsimd.affine_select(out=mask_s[:, S - P:S], in_=mask_s[:, S - P:S], compare_op=ALU.is_ge, fill=NEG, base=0,
                                    pattern=[[-1, P]], channel_multiplier=1).then_inc(tri_ready, 1)
            nc.gpsimd.affine_select(out=mask_t[:, :], in_=mask_t[:, :], compare_op=ALU.is_ge, fill=NEG, base=0,
                                    pattern=[[1, P]], channel_multiplier=-1).then_inc(tri_ready, 1)
            nc.gpsimd.affine_select(out=neg_diag[:, :], in_=neg_diag[:, :], compare_op=ALU.not_equal, fill=-1.0, base=0,
                                    pattern=[[-1, QT]], channel_multiplier=1).then_inc(diag_ready, 1)
            for n, (lo, raw, hi) in enumerate(((wo_lo, wo_raw, wo_hi), (w1_lo, w1_raw, w1_hi), (w2_lo, w2_raw, w2_hi))):
                pool.wait_ge(wts_hi_done, n + 1)
                nc.gpsimd.tensor_tensor(lo[:], raw[:], hi[:], ALU.subtract).then_inc(wts_lo_done, 1)

            def low(u, k, r):
                pool.wait_ge(exp_done, NU * u + (r + 1))
                pool.wait_ge(phi_done, NU * u + (r + 1))
                cols = slice(BANK * r, BANK * (r + 1))
                nc.gpsimd.tensor_tensor(p_hl[:, k % 2, 1, cols], p32[:, ring_at(k, r), :], p_hl[:, k % 2, 0, cols], ALU.subtract)\
                    .then_inc(plo_done, 1)

            def pool_slot(t, k, split):
                u = 4 * t + k
                for r in range(NU):
                    low(u, k, r)
                    if split and r == 2:
                        split_low(2 * t + (k + 4) // 2, ((k + 4) // 2) % 2)

            pool_slot(0, 0, True)
            with pool.Fori(0, LOOPS) as t:
                for k in range(1, 5):
                    pool_slot(t, k, k % 2 == 0)
            for k in LAST_SLOTS:
                pool_slot(LOOPS, k, False)

            pool.wait_ge(o_ready, SUMS + NG * HEADS)
            for n in range(2):
                pool.wait_ge(scratch_out[n], 16 * (B + PAIRS // 2))
            nc.gpsimd.iota(bias_s[:, :], pattern=[[1, S]], base=P - S, channel_multiplier=-1,
                           allow_small_or_imprecise_dtypes=True).then_inc(bias_made, 1)
            nc.gpsimd.iota(bias_t[:, :], pattern=[[-1, S]], base=0, channel_multiplier=1,
                           allow_small_or_imprecise_dtypes=True).then_inc(bias_made, 1)
            nc.gpsimd.memset(qm_b[:, :, :].bitcast(F32), 0.0).then_inc(rows_b, 1)
            nc.gpsimd.memset(k_one[:, :].bitcast(F32), 0.0).then_inc(zeroed, 1)
            nc.gpsimd.memset(neg_diag_b[:, :], 0.0).then_inc(zeroed, 1)
            nc.gpsimd.memset(v2_sb[:, :, 2 * E:V2P], 1.0).then_inc(v2_one, 1)
            pool.wait_ge(zeroed, 9)
            nc.gpsimd.memset(k_one[0:QT, :].bitcast(F32), 1.0).then_inc(rows_b, 1)
            nc.gpsimd.affine_select(out=neg_diag_b[:, :], in_=neg_diag_b[:, :], compare_op=ALU.not_equal, fill=-1.0, base=0,
                                    pattern=[[-1, QT]], channel_multiplier=1).then_inc(rows_b, 1)
            for c in range(CHUNKS):
                chunk_rstd(CHUNKS + c)
                if c == 0:
                    pool.wait_ge(attn_b_in, 48)
            pool.wait_ge(steps_b, 2)
            nc.gpsimd.affine_select(out=bias_s[:, :], in_=bias_s[:, :], compare_op=ALU.is_ge, fill=NEG, base=S - P,
                                    pattern=[[-1, S]], channel_multiplier=1).then_inc(bias_ready, 1)
            nc.gpsimd.affine_select(out=bias_t[:, :], in_=bias_t[:, :], compare_op=ALU.is_ge, fill=NEG, base=0,
                                    pattern=[[1, S]], channel_multiplier=-1).then_inc(bias_ready, 1)
            for c in range(CHUNKS):
                chunk_rstd(2 * CHUNKS + c)
            for m in range(NU * B):
                b, cols = m // NU, slice(BANK * (m % NU), BANK * (m % NU + 1))
                pool.wait_ge(expb_done, m + 1)
                pool.wait_ge(phib_done, m + 1)
                nc.gpsimd.tensor_tensor(p_hlb[:, b, 1, cols], p32b[:, m % RING, :], p_hlb[:, b, 0, cols], ALU.subtract)\
                    .then_inc(plob_done, 1)
            for c in range(CHUNKS):
                chunk_rstd(3 * CHUNKS + c)


_INS = ['L0_attn_a_x', 'L0_attn_a_Wq', 'L0_attn_a_Wk', 'L0_attn_a_Wv', 'L0_attn_a_bq', 'L0_attn_a_bk', 'L0_attn_a_bv',
        'L0_attn_a_Wo', 'L0_attn_a_bo', 'L0_attn_b_W_qk', 'L0_attn_b_W_v', 'L0_attn_b_alibi_slope',
        'L0_ffn_w1', 'L0_ffn_b1', 'L0_ffn_w2', 'L0_ffn_b2']
_OUT = ((2, 1024, 128), 'float32')


def kernel(**inputs):
    import numpy as _np
    import concourse.bacc as _bacc
    from concourse import mybir as _mybir
    from concourse.bass_utils import run_bass_kernel_spmd as _run

    nc = _bacc.Bacc("TRN2", target_bir_lowering=False, num_devices=1)
    arrays, args = {}, []
    for name in _INS:
        a = _np.ascontiguousarray(inputs[name])
        arrays[f"in_{name}"] = a
        args.append(nc.dram_tensor(f"in_{name}", a.shape, _mybir.dt.from_np(a.dtype), kind="ExternalInput").ap())
    shape, dtype = _OUT
    args.append(nc.dram_tensor("out_0", shape, _mybir.dt.from_np(_np.dtype(dtype)), kind="ExternalOutput").ap())
    hybrid_block(nc, *args)
    r = _run(nc, [arrays], core_ids=[0])
    return r.results[0]["out_0"]
```

```python
from contextlib import ExitStack

import concourse.bass as bass
from concourse import mybir

F32 = mybir.dt.float32
F32R = mybir.dt.float32r
F16 = mybir.dt.float16
BF16 = mybir.dt.bfloat16
ALU = mybir.AluOpType
ACT = mybir.ActivationFunctionType

P = 128
BANK = 512
NEG = -1.0e30
EPS = 1.0e-5
TINY = 1.0e-30
F16_TOP = 4096.0


def hybrid_block(nc, x, Wq, Wk, Wv, bq, bk, bv, Wo, bo, Wqk, Wv2, slope, w1, b1, w2, b2, out):
    B, S, E = x.shape
    H, _, DH = Wq.shape
    F = w1.shape[1]
    T = B * S
    TILES = T // P
    QT = S // P
    CHUNKS = T // BANK
    CT = BANK // P
    HEADS = B * H
    PAIRS = HEADS // 2
    PP = H // 2
    FW = F // P
    OB = H * DH // P
    VP = 2 * DH + 2
    VW = DH + 1
    V2P = 2 * E + 2
    V2W = E + 1
    SCALE_A = float(DH) ** -0.5
    SCALE_B = float(E) ** -0.5
    assert E == P and DH * 2 == P and QT == 8 and F % P == 0 and HEADS == 32

    units = []
    for parts in (((0, 0),), ((1, P), (3, 3 * P)), ((2, 2 * P), (6, 6 * P)), ((0, BANK),), ((1, BANK),), ((2, BANK),),
                  ((3, BANK),), ((4, BANK),), ((5, 5 * P), (7, 7 * P))):
        col, unit = 0, []
        for i, q0 in parts:
            n = BANK - q0 % BANK
            unit.append((i, q0, n, col))
            col += n
        assert col == BANK
        units.append(unit)
    NU = len(units)
    PCOLS = NU * BANK
    place = {(i, j): BANK * r + col + P * j - q0 for r, unit in enumerate(units) for i, q0, n, col in unit
             for j in range(q0 // P, (q0 + n) // P)}
    need_units = [1 + max(place[i, j] for i in range(j + 1)) // BANK for j in range(QT)]
    PV_PAIRS = [(j, kt) for j in range(QT) for kt in range(j + 1)]
    PV_STEP = len(PV_PAIRS) // NU
    assert PV_STEP * NU == len(PV_PAIRS)
    PV_GROUPS = [(0, 1, 2, 3), (4, 5, 6, 7)]
    NG = len(PV_GROUPS)
    SUMS = 2
    GROUP_OF = {j: (g, js.index(j)) for g, js in enumerate(PV_GROUPS) for j in js}
    MAX_ORDER = list(range(QT - 1, -1, -1))
    QB_BANKS, V2_BANKS, OB_BANKS = (0, 5), (1, 4), ((7, 1), (3, 5))
    MAX_B_AT = (((), (), ()), ((), (0,), (1,)), ((2,), (3,), (4,)), ((5, 6, 7), (), ()))
    MAX_B_NEXT = ((0,), (1,), (2,), (3,), (4,), (5,), (6, 7), (), ())
    OB_FIRST = (0, 1)
    OB_AT = [tuple(r for r in (2 * n + 2, 2 * n + 3) if r < NU) for n in range(FW * CHUNKS + 2)]
    NORM_STEP = 6
    FIRST_BANKS = (7, 0, 1, 2)
    PIECE_AT = (2, 4, 6, 8)
    FIRST_MAX_AT = tuple(range(11, 27, 2))
    FIRST_ROWS_AT = 27
    BIAS_AT = 10
    WEIGHTS_AT = (16, 20)
    RING = 4
    ST_RING = 3
    BLOCKS = 3
    BLOCK_BANKS = (0, 1, 4)

    v_dram = nc.dram_tensor("v_scratch", [HEADS, P, QT * VP], F16, kind="Internal").ap()
    o_dram = nc.dram_tensor("o_scratch", [PAIRS, P, QT, P], F32, kind="Internal").ap()
    x_tok = x.rearrange("b (t p) e -> p (b t) e", p=P)
    out_tok = out.rearrange("b (t p) e -> p (b t) e", p=P)

    start = (nc.sbuf_base + 31) // 32 * 32
    end = nc.sbuf_usable_end
    SIZE = {F32: 4, F32R: 4, F16: 2, BF16: 2}
    places = [start]

    def sb(name, shape, dt):
        n = SIZE[dt]
        for s in shape[1:]:
            n *= s
        offset = places[0]
        places[0] = offset + (n + 31) // 32 * 32
        assert places[0] <= end, (name, places[0], end)
        return nc.alloc_sbuf_tensor_at(name, shape, dt, offset=offset)

    x_sb = sb("x_sb", [P, TILES, E], F32)
    xT_hi = sb("xT_hi", [P, T], F32R)
    xT_lo = sb("xT_lo", [P, T], F32R)
    xn = sb("xn", [P, 2, CT, E], F32)
    stats = sb("stats", [P, TILES, 6], F32)
    mean_var = sb("mean_var", [P, TILES, 2], F32)
    var_eps = sb("var_eps", [P, TILES], F32)
    rstd = sb("rstd", [P, TILES], F32)
    gain_rows = sb("gain_rows", [P, OB], F32)
    minus_half = sb("minus_half", [P, CT], F32)
    ident = sb("ident", [P, P], F32)
    ident_b = sb("ident_b", [P, P], BF16)
    ones = sb("ones", [P, P], F32)
    wo_hi = sb("wo_hi", [P, OB, E], F32R)
    wo_lo = sb("wo_lo", [P, OB, E], F32R)
    w1_hi = sb("w1_hi", [P, F], F32R)
    w1_lo = sb("w1_lo", [P, F], F32R)
    w2_hi = sb("w2_hi", [P, FW, E], F32R)
    w2_lo = sb("w2_lo", [P, FW, E], F32R)
    b1_sb = sb("b1_sb", [P, FW], F32)
    b2_sb = sb("b2_sb", [P, 1], F32)
    bo_sb = sb("bo_sb", [P, 1], F32)
    bv_sb = sb("bv_sb", [P, OB], F32)
    bo_all = sb("bo_all", [P, 1], F32)
    l1_rows = sb("l1_rows", [P, OB], F32)
    shared = places[0]

    k_hh = sb("k_hh", [P, 4, S], F32R)
    q_hl = sb("q_hl", [P, 4, S], F32R)
    k_l1 = sb("k_l1", [P, 4, S], F32R)
    q_hm = sb("q_hm", [P, 4, S], F32R)
    staged = places[0]
    st_hi = sb("st_hi", [P, 2, S], F32R)
    st_lo = sb("st_lo", [P, 2, S], F32R)
    w_raw = sb("w_raw", [P, 2, P], F32)
    w_hi = sb("w_hi", [P, 2, 2, P], F32R)
    w_lo = sb("w_lo", [P, 2, 2, P], F32R)
    w_b = sb("w_b", [P, 2, 2], F32)
    p_hl = sb("p_hl", [P, 2, 2, PCOLS], F16)
    mask_s = sb("mask_s", [P, S], F32)
    mask_t = sb("mask_t", [P, P], BF16)
    maxima = sb("maxima", [P, 2, QT], F32)
    max_junk = sb("max_junk", [P, 2, S], BF16)
    gate = sb("gate", [P, 2], F32)
    neg_diag = sb("neg_diag", [QT, QT], F32)
    before_slots = places[0]
    p32 = sb("p32", [P, RING, BANK], F32)
    v_sb = sb("v_sb", [P, 2, QT, VP], F16)
    o_sb = sb("o_sb", [P, 2, QT, P], F32)
    o_den = sb("o_den", [P, 2, CT], F32)

    VH = H // 2
    VN = VH * QT * VP
    V_STORES = 2 * B
    p_flat = p_hl[:, :, :, :].rearrange("p a b n -> p (a b n)")
    v_stage = [p_flat[:, 2 * n * PCOLS:2 * n * PCOLS + VN].rearrange("p (h t c) -> p h t c", h=VH, t=QT) for n in range(2)]

    places[0] = before_slots
    wv_raw = sb("wv_raw", [P, H * DH], F32)
    wv_abs = sb("wv_abs", [P, H * DH], F32)
    wv_hi = sb("wv_hi", [P, H * DH], F32R)
    wv_lo = sb("wv_lo", [P, H * DH], F32R)
    wo_raw = sb("wo_raw", [P, OB, E], F32)
    w1_raw = sb("w1_raw", [P, F], F32)
    w2_raw = sb("w2_raw", [P, FW, E], F32)

    places[0] = shared
    o_in1 = sb("o_in1", [P, OB, CT, P], F32)
    oT_hi = sb("oT_hi", [P, BLOCKS, BANK], F32R)
    oT_lo = sb("oT_lo", [P, BLOCKS, BANK], F32R)
    places[0] = shared + OB * CT * P * SIZE[F32]
    p_hlb = sb("p_hlb", [P, B, 2, PCOLS], F16)
    bias_s = sb("bias_s", [P, S], F32)
    bias_t = sb("bias_t", [P, S], F32)
    yT = sb("yT", [P, 2, BANK], F32)
    assert places[0] == staged
    o_in0 = sb("o_in0", [P, OB, CT, P], F32)
    o_in = (o_in0, o_in1)
    h32 = sb("h32", [P, BLOCKS, BANK], F32)
    h_hi = sb("h_hi", [P, BLOCKS, BANK], F32R)
    h_lo = sb("h_lo", [P, BLOCKS, BANK], F32R)
    qb_hi = sb("qb_hi", [P, T], F32R)
    qb_lo = sb("qb_lo", [P, T], F32R)
    v2_sb = sb("v2_sb", [P, TILES, V2P], F16)
    qm_b = sb("qm_b", [P, B, S], F32R)
    k_one = sb("k_one", [P, P], F32R)
    s32 = sb("s32", [P, 3, BANK], F32)
    p32b = sb("p32b", [P, RING, BANK], F32)
    junk_b = sb("junk_b", [P, S], BF16)
    max_b = sb("max_b", [P, B, QT], F32)
    neg_diag_b = sb("neg_diag_b", [QT, QT], F32)
    slope_sb = sb("slope_sb", [P, 1], F32)
    wqk_raw = sb("wqk_raw", [P, E], F32)
    wqk_hi = sb("wqk_hi", [P, E], F32R)
    wqk_lo = sb("wqk_lo", [P, E], F32R)
    wv2_raw = sb("wv2_raw", [P, E], F32)
    wv2_abs = sb("wv2_abs", [P, E], F32)
    wv2_hi = sb("wv2_hi", [P, E], F32R)
    wv2_lo = sb("wv2_lo", [P, E], F32R)
    l1_b = sb("l1_b", [P, 3], F32)
    diag_b = sb("diag_b", [P, E], F32)
    l1_cols = sb("l1_cols", [P, E], F32)
    ob_den = sb("ob_den", [P, 2], F32)
    ob_out = sb("ob_out", [P, 2, E], F32)

    ctx = ExitStack()
    with ctx:
        psum = ctx.enter_context(nc.psum_tensor("psum", [P, 8 * BANK], F32))

        def bank(n, cols=BANK):
            return psum[:, n * BANK:n * BANK + cols]

        MAXB, PVB, MISC = 3, 5, 7

        def sem(name):
            return ctx.enter_context(nc.semaphore(name))

        x_in = [sem(f"x_in{g}") for g in range(CHUNKS)]
        wv_in, wo_in, ffn_in, bias_in = sem("wv_in"), sem("wo_in"), sem("ffn_in"), sem("bias_in")
        pair_in, attn_b_in = sem("pair_in"), sem("attn_b_in")
        v_in = [sem("v_in0"), sem("v_in1")]
        o_back = [sem("o_back0"), sem("o_back1")]
        scratch_out = [sem("scratch_out0"), sem("scratch_out1")]
        result_out = sem("result_out")
        zeroed, ident_ready, half_ready, ones_ready = sem("zeroed"), sem("ident_ready"), sem("half_ready"), sem("ones_ready")
        tri_ready, diag_ready, rows_ready = sem("tri_ready"), sem("diag_ready"), sem("rows_ready")
        bn_done, aggr_done, eps_done, rstd_done = sem("bn_done"), sem("aggr_done"), sem("eps_done"), sem("rstd_done")
        xn_ready, xt_full, xt_hi_done, xt_lo_done = sem("xn_ready"), sem("xt_full"), sem("xt_hi_done"), sem("xt_lo_done")
        abs_done, gain_made, gain_diag, gain_full = sem("abs_done"), sem("gain_made"), sem("gain_diag"), sem("gain_full")
        wv_scaled, wv_hi_done, wv_lo_done = sem("wv_scaled"), sem("wv_hi_done"), sem("wv_lo_done")
        l1r_full, wo_scaled = sem("l1r_full"), sem("wo_scaled")
        bo_full, wts_hi_done, wts_lo_done = sem("bo_full"), sem("wts_hi_done"), sem("wts_lo_done")
        v_full, v_hi_done, v_lo_done, v_one = sem("v_full"), sem("v_hi_done"), sem("v_lo_done"), sem("v_one")
        split_hi, split_lo = sem("split_hi"), sem("split_lo")
        piece_full, piece_hi, piece_lo = sem("piece_full"), sem("piece_hi"), sem("piece_lo")
        k_moved = [sem("k_moved0"), sem("k_moved1")]
        q_moved = [sem("q_moved0"), sem("q_moved1")]
        max_full, max_done, mt_full, mrow_done = sem("max_full"), sem("max_done"), sem("mt_full"), sem("mrow_done")
        st_full, exp_done, phi_done, plo_done = sem("st_full"), sem("exp_done"), sem("phi_done"), sem("plo_done")
        pv_done, o_inverse, o_ready = sem("pv_done"), sem("o_inverse"), sem("o_ready")
        ot_full, ot_hi_done, ot_lo_done, ot_used = sem("ot_full"), sem("ot_hi_done"), sem("ot_lo_done"), sem("ot_used")
        yT_ready, yt_full, res_done = sem("yT_ready"), sem("yt_full"), sem("res_done")
        h_full, h32_done, h_hi_done, h_lo_done, h_used = (
            sem("h_full"), sem("h32_done"), sem("h_hi_done"), sem("h_lo_done"), sem("h_used"))
        steps_b, bias_made, bias_ready, rows_b = sem("steps_b"), sem("bias_made"), sem("bias_ready"), sem("rows_b")
        wqk_hi_done, wqk_split = sem("wqk_hi_done"), sem("wqk_split")
        l1b_made, wv2_scaled, wv2_t, wv2_hi_done, wv2_split = (
            sem("l1b_made"), sem("wv2_scaled"), sem("wv2_t"), sem("wv2_hi_done"), sem("wv2_split"))
        diagb_made, l1c_full, l1c_done = sem("diagb_made"), sem("l1c_full"), sem("l1c_done")
        qb_full, qb_hi_done, qb_lo_done = sem("qb_full"), sem("qb_hi_done"), sem("qb_lo_done")
        v2_full, v2_hi_done, v2_lo_done, v2_one = sem("v2_full"), sem("v2_hi_done"), sem("v2_lo_done"), sem("v2_one")
        maxb_full, maxb_done, mtb_full, mrowb_done = sem("maxb_full"), sem("maxb_done"), sem("mtb_full"), sem("mrowb_done")
        sb_full, s32_done, expb_done, phib_done, plob_done = (
            sem("sb_full"), sem("s32_done"), sem("expb_done"), sem("phib_done"), sem("plob_done"))
        pvb_done, ob_inverse, ob_read, resb_done = sem("pvb_done"), sem("ob_inverse"), sem("ob_read"), sem("resb_done")

        LOOPS = (HEADS - 4) // 4
        LAST_SLOTS = range(1, 4)

        def pieces_after(t, k):
            if isinstance(t, int):
                return min(2 * (4 * t + k) + 8, 4 * PAIRS)
            return 8 * t + (2 * k + 8)

        def max_banks(j, c0, c1):
            first = (MAXB + (CT - 1 - j) % 2 if j < CT else MAXB) * BANK
            return psum[:, first + c0:first + c1]

        def ring_at(k, r):
            return (NU * k + r) % RING

        def set_of(k, offset=0):
            return (k + offset) % 4

        block = ctx.enter_context(nc.Block())

        @block.sync
        def _(sp):
            wk_pair = Wk.rearrange("(q a) e d -> q e a d", a=2)
            wq_pair = Wq.rearrange("(q a) e d -> q e a d", a=2)
            bk_pair = bk.rearrange("(q a) d -> q (a d)", a=2)
            bq_pair = bq.rearrange("(q a) d -> q (a d)", a=2)

            def load_biases(q, par):
                for which, b in enumerate((bk_pair, bq_pair)):
                    sp.dma_start(w_b[:, par, which:which + 1], b[q].unsqueeze(1)).then_inc(pair_in, 16)

            def load_weights(q):
                for which, w in enumerate((wk_pair, wq_pair)):
                    sp.dma_start(w_raw[:, which, :].rearrange("p (a d) -> p a d", a=2), w[q]).then_inc(pair_in, 16)

            def move_k(par, s):
                rows = slice(DH * par, DH * par + DH)
                hi, lo = st_hi[rows, 0, :].bitcast(F32), st_lo[rows, 0, :].bitcast(F32)
                sp.dma_start(k_hh[0:DH, s, :].bitcast(F32), hi).then_inc(k_moved[par], 16)
                sp.dma_start(k_hh[DH:P, s, :].bitcast(F32), hi).then_inc(k_moved[par], 16)
                sp.dma_start(k_l1[0:DH, s, :].bitcast(F32), lo).then_inc(k_moved[par], 16)

            def move_q(par, s):
                rows = slice(DH * par, DH * par + DH)
                hi, lo = st_hi[rows, 1, :].bitcast(F32), st_lo[rows, 1, :].bitcast(F32)
                sp.dma_start(q_hl[0:DH, s, :].bitcast(F32), hi).then_inc(q_moved[par], 16)
                sp.dma_start(q_hl[DH:P, s, :].bitcast(F32), lo).then_inc(q_moved[par], 16)
                sp.dma_start(q_hm[0:DH, s, :].bitcast(F32), hi).then_inc(q_moved[par], 16)

            for g in range(CHUNKS):
                sp.dma_start(x_sb[:, CT * g:CT * (g + 1), :], x_tok[:, CT * g:CT * (g + 1), :]).then_inc(x_in[g], 16)
                if g == 1:
                    load_weights(0)
            load_biases(0, 0)
            sp.dma_start(wo_raw[:, :, :], Wo.rearrange("(k p) e -> p k e", p=P)).then_inc(wo_in, 16)
            sp.dma_start(bv_sb[:, :], bv.rearrange("(q a) d -> (a d) q", a=2), allow_slow_non_contiguous=True).then_inc(bias_in, 16)
            sp.dma_start(bo_sb[:, :], bo.unsqueeze(1)).then_inc(bias_in, 16)
            sp.wait_ge(split_lo, 1)
            load_biases(1, 1)
            load_weights(1)
            sp.dma_start(b1_sb[:, :], b1.rearrange("(m p) -> p m", p=P), allow_slow_non_contiguous=True).then_inc(ffn_in, 16)
            sp.dma_start(b2_sb[:, :], b2.unsqueeze(1)).then_inc(ffn_in, 16)
            sp.dma_start(w1_raw[:, :], w1).then_inc(ffn_in, 16)
            sp.dma_start(w2_raw[:, :, :], w2.rearrange("(m p) e -> p m e", p=P)).then_inc(ffn_in, 16)
            sp.wait_ge(rows_ready, 1)

            def move_pair(pair, move, pieces):
                sp.wait_ge(piece_lo, pieces)
                for par in range(2):
                    move(par, 2 * pair + par)

            def store_v(n, half):
                sp.wait_ge(v_lo_done, QT * n + QT // 2 * (half + 1))
                h0 = (n % B) * H + (n // B) * VH
                cols = slice(QT * VP // 2 * half, QT * VP // 2 * (half + 1))
                sp.dma_start(v_dram[h0:h0 + VH].rearrange("h p n -> p h n")[:, :, cols],
                             v_stage[n % 2].rearrange("p h t c -> p h (t c)")[:, :, cols]).then_inc(scratch_out[n % 2], 16)

            move_pair(0, move_k, 2)
            move_pair(0, move_q, 4)
            sp.wait_ge(split_lo, 2)
            load_biases(2, 0)
            load_weights(2)
            sp.wait_ge(v_one, 1)
            store_v(0, 0)
            move_pair(1, move_k, 6)
            store_v(0, 1)
            move_pair(1, move_q, 8)
            for n in range(1, 2 * B):
                for half in range(2):
                    store_v(n, half)
            for n in range(2):
                sp.wait_ge(scratch_out[n], 16 * V_STORES)
            sp.wait_ge(wts_lo_done, 3)

            def fixed(value):
                return value if isinstance(value, int) else sp.snap(value)

            def sp_slot(t, k, project):
                u = fixed(4 * t + k)
                scored, pair = fixed(NU * u), fixed(2 * t + (k + 5) // 2)
                earlier, index, projected = fixed(4 * (pair - 1)), fixed(pair % PP), fixed(pieces_after(t, k))
                stored, pair_out = fixed(NG * (4 * t + k) + SUMS), fixed(2 * t + (k // 2 - 1))
                if k or not isinstance(t, int):
                    sp.wait_ge(st_full, scored)
                sp.dma_start(v_sb[:, k % 2, :, :].rearrange("p t c -> p (t c)"), v_dram[u]).then_inc(v_in[k % 2], 16)
                if project and k % 2 == 1:
                    sp.wait_ge(piece_lo, earlier)
                    load_biases(index, ((k + 5) // 2) % 2)
                    sp.wait_ge(split_lo, pair)
                    load_weights(index)
                    sp.wait_ge(piece_lo, projected)
                    move_k(0, set_of(k, 3))
                if project and k % 2 == 0 and k:
                    move_k(1, set_of(k, 3))
                    sp.wait_ge(piece_lo, projected)
                    move_q(0, set_of(k, 2))
                    move_q(1, set_of(k, 3))
                if k % 2 == 0 and k:
                    store_pair(k, stored, pair_out)

            def store_pair(k, stored, index):
                sp.wait_ge(o_ready, stored)
                par = (k // 2 - 1) % 2
                sp.dma_start(o_dram[index], o_sb[:, par, :, :]).then_inc(scratch_out[par], 16)

            sp_slot(0, 0, True)
            with sp.Fori(0, LOOPS) as t:
                for k in range(1, 5):
                    sp_slot(t, k, True)
            def load_outputs(c):
                b, t0 = c * CT // QT, c * CT % QT
                sp.dma_start(o_in[c % 2][:, :, :, :], o_dram[PP * b:PP * (b + 1), :, t0:t0 + CT, :].rearrange("h p t n -> p h t n"))\
                    .then_inc(o_back[c % 2], 16)

            for k in LAST_SLOTS:
                sp_slot(LOOPS, k, False)
                if k == 2:
                    for n in range(2):
                        sp.wait_ge(scratch_out[n], 16 * (V_STORES + PP // 2))
                        sp.wait_ge(k_moved[n], 48 * PAIRS)
                        sp.wait_ge(q_moved[n], 48 * PAIRS)
                    load_outputs(0)
            sp.wait_ge(st_full, NU * HEADS)
            load_outputs(1)
            store_pair(4, SUMS + NG * HEADS, PAIRS - 1)

            for n in range(2):
                sp.wait_ge(scratch_out[n], 16 * (V_STORES + PAIRS // 2))
            sp.wait_ge(plo_done, NU * HEADS)
            sp.dma_start(wqk_raw[:, :], Wqk).then_inc(attn_b_in, 16)
            sp.dma_start(wv2_raw[:, :], Wv2).then_inc(attn_b_in, 16)
            sp.dma_start(slope_sb[:, :], slope.partition_broadcast(P)).then_inc(attn_b_in, 16)
            for c in range(2, CHUNKS):
                sp.wait_ge(ot_full, OB * (c - 1))
                load_outputs(c)
            for c in range(CHUNKS):
                sp.wait_ge(res_done, 2 * CHUNKS + c + 1)
                sp.dma_start(out_tok[:, CT * c:CT * (c + 1), :], x_sb[:, CT * c:CT * (c + 1), :]).then_inc(result_out, 16)
            sp.wait_ge(result_out, 16 * CHUNKS)

        @block.tensor
        def _(pe):
            def three(dst, hi, lo, m_hi, m_lo, start=True, stop=True):
                nc.tensor.matmul(dst, hi, m_hi, start=start, stop=False)
                nc.tensor.matmul(dst, lo, m_hi, start=False, stop=False)
                return nc.tensor.matmul(dst, hi, m_lo, start=False, stop=stop)

            def turn_chunk(n):
                pe.wait_ge(xn_ready, n + 1)
                if n >= 2:
                    pe.wait_ge(xt_lo_done, n - 1)
                for j in range(CT):
                    last = nc.tensor.transpose(bank(6 + n % 2)[:, P * j:P * (j + 1)], xn[:, n % 2, j, :], ident[:, :])
                last.then_inc(xt_full, 1)

            def piece(n, pair, par, which, half, b):
                pe.wait_ge(piece_lo, n)
                pe.wait_ge(split_lo, pair + 1)
                cols = slice(S * b + BANK * half, S * b + BANK * (half + 1)) if isinstance(b, int) else bass.ds(b * S + BANK * half, BANK)
                three(bank(MISC), w_hi[:, par, which, :], w_lo[:, par, which, :], xT_hi[:, cols], xT_lo[:, cols]).then_inc(piece_full, 1)

            def max_tile(v, n, s):
                j = MAX_ORDER[n]
                if not (isinstance(v, int) and v == 0 and n == 0):
                    pe.wait_ge(max_done, QT * v + (n - max_alone(j)))
                cols = P * (j + 1)
                for c0 in range(0, cols, BANK):
                    c1 = min(c0 + BANK, cols)
                    last = nc.tensor.matmul(max_banks(j, c0, c1), q_hl[:, s, P * j:P * (j + 1)], k_hh[:, s, c0:c1],
                                            start=True, stop=True)
                last.then_inc(max_full, 1)

            def max_alone(j):
                return int(j < CT - 1)

            def turn_maxima(v, par, pieces):
                pe.wait_ge(max_done, QT * (v + 1))
                pe.wait_ge(piece_lo, pieces)
                nc.tensor.transpose(bank(MISC)[0:QT, 0:P], maxima[:, par, :], ident[:, :]).then_inc(mt_full, 1)

            def outputs(w, k, step, uses):
                par = (k - 1) % 2
                for j, kt in PV_PAIRS[PV_STEP * step:PV_STEP * (step + 1)]:
                    g, r = GROUP_OF[j]
                    if kt == 0:
                        if j == 0:
                            pe.wait_ge(v_in[par], 16 * (uses + 1))
                        if j == 0 or need_units[j] > need_units[j - 1]:
                            pe.wait_ge(plo_done, NU * w + need_units[j])
                        if r == 0:
                            pe.wait_ge(o_ready, NG * w + (g + (SUMS - 1)))
                    dst = bank(PVB + g)[:, VW * r:VW * (r + 1)]
                    cols = slice(place[kt, j], place[kt, j] + P)
                    v_hi_one, v_lo = v_sb[:, par, kt, DH:DH + VW], v_sb[:, par, kt, 0:DH]
                    nc.tensor.matmul(dst, p_hl[:, par, 0, cols], v_hi_one, start=(kt == 0), stop=False)
                    nc.tensor.matmul(dst[:, 0:DH], p_hl[:, par, 0, cols], v_lo, start=False, stop=False)
                    last = nc.tensor.matmul(dst, p_hl[:, par, 1, cols], v_hi_one, start=False, stop=(kt == j))
                    if kt == j:
                        last.then_inc(pv_done, 1)

            def scores(u, k, r):
                s = set_of(k)
                if r >= ST_RING or not (isinstance(u, int) and u == 0):
                    pe.wait_ge(phi_done, NU * u + (r - ST_RING + 1))
                if r == 0:
                    pe.wait_ge(mrow_done, u + 1)
                for i, q0, n, col in units[r]:
                    keys = slice(P * i, P * (i + 1))
                    dst = bank(r % ST_RING)[:, col:col + n]
                    diagonal = q0 == P * i
                    nc.tensor.matmul(dst, k_hh[:, s, keys], q_hl[:, s, q0:q0 + n], start=True, stop=False)
                    last = nc.tensor.matmul(dst, k_l1[:, s, keys], q_hm[:, s, q0:q0 + n], start=False, stop=not diagonal)
                    if diagonal:
                        last = nc.tensor.matmul(dst[:, 0:P], ident_b[:, :], mask_t[:, :], start=False, stop=True)
                last.then_inc(st_full, 1)

            def pe_slot(t, k, projects, takes_maxima):
                u = 4 * t + k

                def maximum(v, n):
                    if takes_maxima:
                        if n == 0:
                            par, count = (k + 1) % 2, 2 * t + (k + 1) // 2 + 1
                            pe.wait_ge(k_moved[par], 48 * count)
                            pe.wait_ge(q_moved[par], 48 * count)
                        max_tile(v, n, set_of(k, 1))

                def products(step):
                    if not (isinstance(u, int) and u == 0):
                        outputs(u - 1, k, step, 2 * t + (k - 1) // 2)

                def project(half):
                    if projects:
                        if half == 0:
                            pe.wait_ge(mrow_done, u + 1)
                        piece(2 * u + (6 + half), 2 * t + (k + 3) // 2, ((k + 3) // 2) % 2, (k + 1) % 2, half, (t + 1) // (PP // 2))

                def rows():
                    if takes_maxima:
                        turn_maxima(u + 1, (k + 1) % 2, pieces_after(t, k))

                products(0)
                maximum(u + 1, 0)
                products(1)
                project(0)
                scores(u, k, 0)
                maximum(u + 1, 1)
                scores(u, k, 1)
                scores(u, k, 2)
                project(1)
                maximum(u + 1, 2)
                products(2)
                products(3)
                products(4)
                products(5)
                maximum(u + 1, 3)
                scores(u, k, 3)
                scores(u, k, 4)
                scores(u, k, 5)
                maximum(u + 1, 4)
                products(6)
                maximum(u + 1, 5)
                scores(u, k, 6)
                maximum(u + 1, 6)
                products(7)
                maximum(u + 1, 7)
                products(8)
                scores(u, k, 7)
                rows()
                scores(u, k, 8)

            turn_chunk(0)
            pe.wait_ge(abs_done, 1)
            pe.wait_ge(ones_ready, 1)
            for k in range(OB):
                last = nc.tensor.matmul(bank(PVB)[:, k:k + 1], wv_abs[:, P * k:P * (k + 1)], ones[:, 0:1], start=True, stop=True)
            last.then_inc(l1r_full, 1)
            turn_chunk(1)
            turn_chunk(2)
            pe.wait_ge(split_lo, 1)
            pe.wait_ge(xt_lo_done, 2)
            for n in range(4):
                cols = slice(BANK * (n % 2), BANK * (n % 2 + 1))
                three(bank(FIRST_BANKS[n]), w_hi[:, 0, n // 2, :], w_lo[:, 0, n // 2, :], xT_hi[:, cols], xT_lo[:, cols]).then_inc(piece_full, 1)
                if n == 1:
                    pe.wait_ge(gain_diag, 1)
                    for m in range(2):
                        last = nc.tensor.matmul(bank(MAXB + m), ones[:, :], wv_abs[:, BANK * m:BANK * (m + 1)], start=True, stop=True)
                    last.then_inc(gain_full, 1)

            pe.wait_ge(wv_lo_done, 1)
            for n in range(2 * TILES):
                half, tile = divmod(n, TILES)
                if n < ST_RING:
                    pe.wait_ge(piece_lo, n + 2)
                else:
                    pe.wait_ge(v_lo_done, n - ST_RING + 1)
                rows, cols = slice(P * tile, P * (tile + 1)), slice(BANK * half, BANK * (half + 1))
                three(bank(n % ST_RING), xT_hi[:, rows], xT_lo[:, rows], wv_hi[:, cols], wv_lo[:, cols]).then_inc(v_full, 1)
                if n == 0:
                    turn_chunk(CHUNKS - 1)
                if n == BIAS_AT:
                    pe.wait_ge(wo_in, 16)
                    pe.wait_ge(bias_in, 32)
                    pe.wait_ge(xt_lo_done, 3)
                    for k in range(OB):
                        last = nc.tensor.matmul(bank(PVB + 1)[:, 0:1], wo_raw[:, k, :], bv_sb[:, k:k + 1], start=(k == 0), stop=(k == OB - 1))
                    last.then_inc(bo_full, 1)
                if n in PIECE_AT:
                    if n == PIECE_AT[0]:
                        pe.wait_ge(xt_lo_done, CHUNKS)
                    m = 4 + PIECE_AT.index(n)
                    piece(m, 1, 1, m % 4 // 2, m % 2, 0)
                if n in FIRST_MAX_AT:
                    m = FIRST_MAX_AT.index(n)
                    if m == 0:
                        pe.wait_ge(wv_scaled, 1)
                        pe.wait_ge(k_moved[0], 48)
                        pe.wait_ge(q_moved[0], 48)
                    max_tile(0, m, 0)
                if n == FIRST_ROWS_AT:
                    turn_maxima(0, 0, 8)
            pe.wait_ge(rows_ready, 1)
            pe.wait_ge(tri_ready, 2)
            pe.wait_ge(v_lo_done, 2 * TILES)

            pe_slot(0, 0, False, True)
            with pe.Fori(0, LOOPS) as t:
                for k in range(1, 5):
                    pe_slot(t, k, True, True)
            for k in LAST_SLOTS:
                pe_slot(LOOPS, k, False, k < 3)
            for step in range(NU):
                outputs(HEADS - 1, 4, step, PAIRS - 1)

            def turn_result(n):
                pe.wait_ge(yT_ready, n + 1)
                if n >= 1:
                    pe.wait_ge(res_done, n)
                else:
                    pe.wait_ge(o_ready, SUMS + NG * HEADS)
                for j in range(CT):
                    last = nc.tensor.transpose(bank(5)[:, P * j:P * (j + 1)], yT[:, n % 2, P * j:P * (j + 1)], ident[:, :])
                last.then_inc(yt_full, 1)

            pe.wait_ge(phi_done, NU * HEADS)
            for n in range(OB * CHUNKS + 2):
                if n < OB * CHUNKS:
                    c, blk = divmod(n, OB)
                    if blk == 0:
                        pe.wait_ge(o_back[c % 2], 16 * (c // 2 + 1))
                    if n >= BLOCKS:
                        pe.wait_ge(ot_lo_done, n - BLOCKS + 1)
                    for j in range(CT):
                        last = nc.tensor.transpose(bank(BLOCK_BANKS[n % BLOCKS])[:, P * j:P * (j + 1)], o_in[c % 2][:, blk, j, :], ident[:, :])
                    last.then_inc(ot_full, 1)
                if n >= 2:
                    c, blk = divmod(n - 2, OB)
                    m = (n - 2) % BLOCKS
                    pe.wait_ge(ot_lo_done, n - 1)
                    if blk == 0 and c >= 2:
                        pe.wait_ge(yT_ready, c - 1)
                    three(bank(2 + c % 2), wo_hi[:, blk, :], wo_lo[:, blk, :], oT_hi[:, m, :], oT_lo[:, m, :],
                          start=(blk == 0), stop=(blk == OB - 1)).then_inc(ot_used, 1)
                    if blk == 3 and c >= 1:
                        turn_result(c - 1)
                    if blk == 2 and c == 2:
                        pe.wait_ge(wv2_scaled, 1)
                        nc.tensor.transpose(bank(6)[:, 0:P], wv2_abs[:, :], ident[:, :]).then_inc(wv2_t, 1)
                        pe.wait_ge(diagb_made, 1)
                        nc.tensor.matmul(bank(7)[:, 0:P], ones[:, :], diag_b[:, :], start=True, stop=True).then_inc(l1c_full, 1)
                    if blk == 5 and c == CHUNKS - 1:
                        pe.wait_ge(wv2_split, 1)
                        pe.wait_ge(l1c_done, 1)
                        turn_chunk(CHUNKS)

            def feed_forward(layer):
                f0 = FW * CHUNKS * layer
                for n in range(FW * CHUNKS + 2):
                    if n < FW * CHUNKS:
                        c, m = divmod(n, FW)
                        if m == 0:
                            pe.wait_ge(xt_lo_done, CHUNKS * (1 + 2 * layer) + c + 1)
                        if f0 + n >= BLOCKS:
                            pe.wait_ge(h_hi_done, f0 + n - BLOCKS + 1)
                        blk, cols = slice(P * m, P * (m + 1)), slice(BANK * c, BANK * (c + 1))
                        three(bank(BLOCK_BANKS[n % BLOCKS]), w1_hi[:, blk], w1_lo[:, blk], xT_hi[:, cols], xT_lo[:, cols]).then_inc(h_full, 1)
                    if layer == 1:
                        for step in OB_AT[n]:
                            outputs_b(B - 1, step)
                    if n >= 2:
                        c, m = divmod(n - 2, FW)
                        y = CHUNKS * (1 + layer) + c
                        r = (n - 2) % BLOCKS
                        pe.wait_ge(h_lo_done, f0 + n - 1)
                        if m == 0:
                            pe.wait_ge(yT_ready, y - 1)
                        three(bank(2 + y % 2), w2_hi[:, m, :], w2_lo[:, m, :], h_hi[:, r, :], h_lo[:, r, :],
                              start=(m == 0), stop=(m == FW - 1)).then_inc(h_used, 1)
                        if m == 0 and (layer == 0 or c + 1 < CHUNKS):
                            turn_chunk(CHUNKS * (1 + 2 * layer) + c + 1)
                        if m == 1 and not (layer == 1 and c == 0):
                            turn_result(y - 1)

            feed_forward(0)

            def max_tile_b(b, n):
                j = QT - 1 - n
                if b or n:
                    pe.wait_ge(maxb_done, QT * b + n)
                cols = P * (j + 1)
                for c0 in range(0, cols, BANK):
                    c1 = min(c0 + BANK, cols)
                    last = nc.tensor.matmul(psum[:, 2 * BANK + c0:2 * BANK + c1], qb_hi[:, S * b + P * j:S * b + P * (j + 1)],
                                            xT_hi[:, S * b + c0:S * b + c1], start=True, stop=True)
                last.then_inc(maxb_full, 1)

            def turn_maxima_b(b):
                pe.wait_ge(maxb_done, QT * (b + 1))
                if b == 0:
                    pe.wait_ge(v2_lo_done, CHUNKS - 1)
                else:
                    pe.wait_ge(mrowb_done, 1)
                nc.tensor.transpose(bank(1)[0:QT, 0:P], max_b[:, b, :], ident[:, :]).then_inc(mtb_full, 1)

            pe.wait_ge(wqk_split, 1)
            pe.wait_ge(h_lo_done, FW * CHUNKS)
            for c in range(CHUNKS):
                cols = slice(BANK * c, BANK * (c + 1))
                pe.wait_ge(xt_lo_done, 2 * CHUNKS + c + 1)
                if c == 1:
                    pe.wait_ge(res_done, 2 * CHUNKS)
                if c >= 2:
                    pe.wait_ge(qb_lo_done, c - 1)
                three(bank(QB_BANKS[c % 2]), wqk_hi[:, :], wqk_lo[:, :], xT_hi[:, cols], xT_lo[:, cols]).then_inc(qb_full, 1)
                if c == 0:
                    turn_result(2 * CHUNKS - 1)
                for n in MAX_B_AT[c][0]:
                    max_tile_b(0, n)
                if c + 1 < CHUNKS:
                    turn_chunk(2 * CHUNKS + c + 1)
                for n in MAX_B_AT[c][1]:
                    if n == 0:
                        pe.wait_ge(yT_ready, 2 * CHUNKS)
                        pe.wait_ge(qb_hi_done, 2)
                    max_tile_b(0, n)
                if c >= 2:
                    pe.wait_ge(v2_lo_done, c - 1)
                if c == CHUNKS - 1:
                    turn_maxima_b(0)
                for j in range(CT):
                    rows = slice(BANK * c + P * j, BANK * c + P * (j + 1))
                    last = three(bank(V2_BANKS[c % 2])[:, P * j:P * (j + 1)], xT_hi[:, rows], xT_lo[:, rows], wv2_hi[:, :], wv2_lo[:, :])
                last.then_inc(v2_full, 1)
                for n in MAX_B_AT[c][2]:
                    max_tile_b(0, n)
            pe.wait_ge(rows_b, 3)
            pe.wait_ge(res_done, 2 * CHUNKS)
            pe.wait_ge(xt_lo_done, 3 * CHUNKS)

            st_bank = (0, 5, 4)

            def scores_b(b, r):
                m = NU * b + r
                if m >= ST_RING:
                    pe.wait_ge(s32_done, m - ST_RING + 1)
                if r == 0:
                    pe.wait_ge(mrowb_done, b + 1)
                    pe.wait_ge(qb_lo_done, CHUNKS)
                if m == ST_RING - 1:
                    pe.wait_ge(v2_lo_done, CHUNKS)
                for i, q0, n, col in units[r]:
                    keys = slice(S * b + P * i, S * b + P * (i + 1))
                    qs = slice(S * b + q0, S * b + q0 + n)
                    dst = bank(st_bank[m % ST_RING])[:, col:col + n]
                    three(dst, xT_hi[:, keys], xT_lo[:, keys], qb_hi[:, qs], qb_lo[:, qs], stop=False)
                    last = nc.tensor.matmul(dst, k_one[:, :], qm_b[:, b, q0:q0 + n], start=False, stop=True)
                last.then_inc(sb_full, 1)

            def outputs_b(b, step):
                for j, kt in PV_PAIRS[PV_STEP * step:PV_STEP * (step + 1)]:
                    m = QT * b + j
                    if kt == 0:
                        pe.wait_ge(plob_done, NU * b + need_units[j])
                        if j >= 2:
                            pe.wait_ge(ob_read, m - 1)
                        if m == 0:
                            pe.wait_ge(v2_one, 1)
                    dst = bank(OB_BANKS[b][j % 2], V2W)
                    cols = slice(place[kt, j], place[kt, j] + P)
                    tile = QT * b + kt
                    v_hi_one, v_lo = v2_sb[:, tile, E:E + V2W], v2_sb[:, tile, 0:E]
                    nc.tensor.matmul(dst, p_hlb[:, b, 0, cols], v_hi_one, start=(kt == 0), stop=False)
                    nc.tensor.matmul(dst[:, 0:E], p_hlb[:, b, 0, cols], v_lo, start=False, stop=False)
                    last = nc.tensor.matmul(dst, p_hlb[:, b, 1, cols], v_hi_one, start=False, stop=(kt == j))
                    if kt == j:
                        last.then_inc(pvb_done, 1)

            for b in range(B):
                for step in range(NU):
                    scores_b(b, step)
                    if b + 1 < B:
                        for n in MAX_B_NEXT[step]:
                            max_tile_b(b + 1, n)
                        if step == NU - 2:
                            turn_maxima_b(b + 1)
                    if b >= 1:
                        outputs_b(b - 1, step)

            turn_chunk(3 * CHUNKS)
            pe.wait_ge(s32_done, NU * B)
            for step in OB_FIRST:
                outputs_b(B - 1, step)
            pe.wait_ge(ob_read, QT * (B - 1))
            feed_forward(1)
            turn_result(3 * CHUNKS - 1)

        @block.scalar
        def _(act):
            act.dma_start(wv_raw[:, :].rearrange("p (h d) -> p h d", h=H), Wv.rearrange("h e d -> e h d")).then_inc(wv_in, 16)

            def split_high(pair, par):
                act.wait_ge(pair_in, 64 * (pair + 1))
                nc.scalar.copy(w_hi[:, par, :, :], w_raw[:, :, :]).then_inc(split_hi, 1)

            def chunk_high(n):
                act.wait_ge(xt_full, n + 1)
                c = n % CHUNKS
                nc.scalar.copy(xT_hi[:, BANK * c:BANK * (c + 1)], bank(6 + n % 2)).then_inc(xt_hi_done, 1)

            def piece_high(n, pair, par, which, half, src=MISC):
                act.wait_ge(piece_full, n + 1)
                if half == 0 and not (isinstance(pair, int) and pair == 0):
                    moved = (k_moved, q_moved)[which]
                    act.wait_ge(moved[0], 48 * pair)
                    act.wait_ge(moved[1], 48 * pair)
                nc.scalar.activation(st_hi[:, which, BANK * half:BANK * (half + 1)], bank(src), ACT.Identity,
                                     bias=w_b[:, par, which:which + 1]).then_inc(piece_hi, 1)

            act.wait_ge(wv_in, 16)
            nc.scalar.activation(wv_abs[:, :], wv_raw[:, :], ACT.Abs).then_inc(abs_done, 1)
            split_high(0, 0)
            for c in range(CHUNKS - 1):
                chunk_high(c)
            for n in range(4):
                piece_high(n, 0, 0, n // 2, n % 2, FIRST_BANKS[n])
                if n == 1:
                    split_high(1, 1)
                    act.wait_ge(wv_scaled, 1)
                    nc.scalar.copy(wv_hi[:, :], wv_raw[:, :]).then_inc(wv_hi_done, 1)
            for n in range(2 * TILES):
                act.wait_ge(v_full, n + 1)
                stage = n // QT
                if n % QT == 0 and stage >= 2:
                    act.wait_ge(scratch_out[stage % 2], 16 * 2)
                nc.scalar.copy(v_stage[stage % 2][:, :, n % QT, DH:2 * DH],
                               bank(n % ST_RING).rearrange("p (h d) -> p h d", d=DH)).then_inc(v_hi_done, 1)
                if n == 0:
                    chunk_high(CHUNKS - 1)
                if n in PIECE_AT:
                    m = 4 + PIECE_AT.index(n)
                    piece_high(m, 1, 1, m % 4 // 2, m % 2)
                if n == WEIGHTS_AT[0]:
                    act.wait_ge(wo_scaled, 1)
                    nc.scalar.copy(wo_hi[:, :, :], wo_raw[:, :, :]).then_inc(wts_hi_done, 1)
                if n == WEIGHTS_AT[1]:
                    act.wait_ge(ffn_in, 64)
                    nc.scalar.copy(w1_hi[:, :], w1_raw[:, :]).then_inc(wts_hi_done, 1)
                    nc.scalar.copy(w2_hi[:, :, :], w2_raw[:, :, :]).then_inc(wts_hi_done, 1)
            act.wait_ge(scratch_out[0], 16 * V_STORES)
            act.wait_ge(wts_lo_done, 3)
            act.wait_ge(v_lo_done, 2 * TILES)

            def exponentials(u, k, r):
                act.wait_ge(st_full, NU * u + (r + 1))
                if r >= RING or not (isinstance(u, int) and u == 0):
                    act.wait_ge(plo_done, NU * u + (r - RING + 1))
                src = bank(r % ST_RING)
                nc.scalar.activation(p32[:, ring_at(k, r), :], src, ACT.Exp, scale=SCALE_A).then_inc(exp_done, 1)
                nc.scalar.activation(p_hl[:, k % 2, 0, BANK * r:BANK * (r + 1)], src, ACT.Exp, scale=SCALE_A).then_inc(phi_done, 1)

            def act_slot(t, k, projects, split):
                u = 4 * t + k

                def project(half):
                    if projects:
                        piece_high(2 * u + (6 + half), 2 * t + (k + 3) // 2, ((k + 3) // 2) % 2, (k + 1) % 2, half)

                project(0)
                exponentials(u, k, 0)
                if split:
                    split_high(2 * t + (k + 4) // 2, ((k + 4) // 2) % 2)
                project(1)
                exponentials(u, k, 1)
                exponentials(u, k, 2)
                exponentials(u, k, 3)
                exponentials(u, k, 4)
                exponentials(u, k, 5)
                exponentials(u, k, 6)
                exponentials(u, k, 7)
                exponentials(u, k, 8)

            act_slot(0, 0, False, True)
            act.wait_ge(scratch_out[1], 16 * V_STORES)
            with act.Fori(0, LOOPS) as t:
                for k in range(1, 5):
                    act_slot(t, k, True, k % 2 == 0)
            for k in LAST_SLOTS:
                act_slot(LOOPS, k, False, False)

            def result_high(n, bias):
                if n >= 2:
                    act.wait_ge(yt_full, n - 1)
                nc.scalar.activation(yT[:, n % 2, :], bank(2 + n % 2), ACT.Identity, bias=bias).then_inc(yT_ready, 1)

            for n in range(OB * CHUNKS):
                c, blk = divmod(n, OB)
                act.wait_ge(ot_full, n + 1)
                if n >= BLOCKS:
                    act.wait_ge(ot_used, n - BLOCKS + 1)
                nc.scalar.copy(oT_hi[:, n % BLOCKS, :], bank(BLOCK_BANKS[n % BLOCKS])).then_inc(ot_hi_done, 1)
                if blk == 2 and c >= 1:
                    act.wait_ge(ot_used, OB * c)
                    result_high(c - 1, bo_all[:, 0:1])
                if blk == 5 and c == 0:
                    act.wait_ge(attn_b_in, 48)
                    nc.scalar.activation(wv2_abs[:, :], wv2_raw[:, :], ACT.Abs, accum_out=l1_b[:, 0:1]).then_inc(l1b_made, 1)
                if blk == 5 and c == 2:
                    nc.scalar.copy(wqk_hi[:, :], wqk_raw[:, :]).then_inc(wqk_hi_done, 1)
                    act.wait_ge(wv2_t, 1)
                    nc.scalar.copy(wv2_hi[:, :], bank(6)[:, 0:P]).then_inc(wv2_hi_done, 1)
            chunk_high(CHUNKS)
            act.wait_ge(ot_used, OB * CHUNKS)
            result_high(CHUNKS - 1, bo_all[:, 0:1])

            def feed_forward(layer):
                f0 = FW * CHUNKS * layer
                for n in range(FW * CHUNKS):
                    c, m = divmod(n, FW)
                    act.wait_ge(h_full, f0 + n + 1)
                    r = n % BLOCKS
                    if f0 + n >= BLOCKS:
                        before = f0 + n - BLOCKS + 1 if n >= BLOCKS else f0
                        act.wait_ge(h_lo_done, before)
                        act.wait_ge(h_used, before)
                    nc.scalar.activation(h32[:, r, :], bank(BLOCK_BANKS[r]), ACT.Relu, bias=b1_sb[:, m:m + 1]).then_inc(h32_done, 1)
                    nc.scalar.activation(h_hi[:, r, :], bank(BLOCK_BANKS[r]), ACT.Relu, bias=b1_sb[:, m:m + 1]).then_inc(h_hi_done, 1)
                    if m == 1 and c >= 1:
                        act.wait_ge(h_used, f0 + FW * c)
                        result_high(CHUNKS * (1 + layer) + c - 1, b2_sb[:, 0:1])
                    if m == 2 and (layer == 0 or c + 1 < CHUNKS):
                        chunk_high(CHUNKS * (1 + 2 * layer) + c + 1)
                act.wait_ge(h_used, f0 + FW * CHUNKS)
                result_high(CHUNKS * (2 + layer) - 1, b2_sb[:, 0:1])

            feed_forward(0)
            for c in range(CHUNKS):
                act.wait_ge(qb_full, c + 1)
                nc.scalar.mul(qb_hi[:, BANK * c:BANK * (c + 1)], bank(QB_BANKS[c % 2]), SCALE_B).then_inc(qb_hi_done, 1)
                if c + 1 < CHUNKS:
                    chunk_high(2 * CHUNKS + c + 1)
                act.wait_ge(v2_full, c + 1)
                nc.scalar.copy(v2_sb[:, CT * c:CT * (c + 1), E:2 * E], bank(V2_BANKS[c % 2]).rearrange("p (t e) -> p t e", e=E)).then_inc(v2_hi_done, 1)
            for m in range(NU * B):
                b, r = m // NU, m % NU
                act.wait_ge(s32_done, m + 1)
                if m >= RING:
                    act.wait_ge(plob_done, m - RING + 1)
                src = s32[:, m % 3, :]
                nc.scalar.activation(p32b[:, m % RING, :], src, ACT.Exp).then_inc(expb_done, 1)
                nc.scalar.activation(p_hlb[:, b, 0, BANK * r:BANK * (r + 1)], src, ACT.Exp).then_inc(phib_done, 1)
            chunk_high(3 * CHUNKS)
            feed_forward(1)

        @block.vector
        def _(dve):
            def chunk_stats(n):
                c = n % CHUNKS
                for j in range(CT * c, CT * (c + 1)):
                    last = nc.vector.bn_stats(stats[:, j, :], x_sb[:, j, :])
                last.then_inc(bn_done, 1)
                dve.wait_ge(bn_done, n + 1)
                for j in range(CT * c, CT * (c + 1)):
                    last = nc.vector.bn_aggr(mean_var[:, j, :], stats[:, j, :])
                last.then_inc(aggr_done, 1)

            def chunk_norm(n):
                c = n % CHUNKS
                dve.wait_ge(rstd_done, n + 1)
                if n >= 2:
                    dve.wait_ge(xt_full, n - 1)
                for j in range(CT):
                    tile = CT * c + j
                    last = nc.vector.tensor_scalar(xn[:, n % 2, j, :], x_sb[:, tile, :], mean_var[:, tile, 0:1], rstd[:, tile:tile + 1],
                                                   ALU.subtract, ALU.mult)
                last.then_inc(xn_ready, 1)

            def chunk_low(n):
                dve.wait_ge(xt_hi_done, n + 1)
                c = n % CHUNKS
                cols = slice(BANK * c, BANK * (c + 1))
                nc.vector.tensor_tensor(xT_lo[:, cols], bank(6 + n % 2), xT_hi[:, cols], ALU.subtract).then_inc(xt_lo_done, 1)

            def piece_low(n, par, which, half, src=MISC):
                dve.wait_ge(piece_hi, n + 1)
                cols = slice(BANK * half, BANK * (half + 1))
                nc.vector.scalar_tensor_tensor(out=st_lo[:, which, cols], in0=bank(src), scalar=w_b[:, par, which:which + 1],
                                               in1=st_hi[:, which, cols], op0=ALU.add, op1=ALU.subtract).then_inc(piece_lo, 1)

            def take_max(v, par, n):
                j = MAX_ORDER[n]
                cols = P * (j + 1)
                dve.wait_ge(max_full, QT * v + (n + 1))
                nc.vector.memset(gate[:, n % 2:n % 2 + 1], 0.0)
                nc.vector.tensor_tensor_reduce(out=max_junk[:, n % 2, 0:cols], in0=max_banks(j, 0, cols),
                                               in1=mask_s[:, S - cols:S], scale=1.0, scalar=-3.0e38, op0=ALU.add, op1=ALU.max,
                                               accum_out=maxima[:, par, j:j + 1]).then_inc(max_done, 1)

            def max_rows(v, s):
                dve.wait_ge(mt_full, v + 1)
                nc.vector.tensor_tensor(q_hm[DH:DH + QT, s, :].rearrange("p (j q) -> p j q", j=QT),
                                        bank(MISC)[0:QT, 0:P].unsqueeze(1).to_broadcast([QT, QT, P]),
                                        neg_diag[:, :].unsqueeze(2).to_broadcast([QT, QT, P]), ALU.mult).then_inc(mrow_done, 1)

            def outputs_out(w, k, g, pairs_before):
                js = PV_GROUPS[g]
                n = len(js)
                par = (k - 1) // 2 % 2
                src = bank(PVB + g, VW * n).rearrange("p (j c) -> p j c", c=VW)
                dve.wait_ge(pv_done, QT * w + js[-1] + 1)
                nc.vector.reciprocal(o_den[:, g, :], src[:, :, DH]).then_inc(o_inverse, 1)
                if g == 0 and (k - 1) % 2 == 0:
                    dve.wait_ge(scratch_out[par], 16 * (V_STORES + pairs_before))
                dve.wait_ge(o_inverse, NG * w + (g + 1))
                c0 = DH * ((k - 1) % 2)
                nc.vector.tensor_tensor(o_sb[:, par, js[0]:js[-1] + 1, c0:c0 + DH], src[:, :, 0:DH],
                                        o_den[:, g, :].unsqueeze(2).to_broadcast([P, n, DH]), ALU.mult).then_inc(o_ready, 1)

            def dve_slot(t, k, projects, takes_maxima):
                u = 4 * t + k

                def maximum(n):
                    if takes_maxima:
                        take_max(u + 1, (k + 1) % 2, n)

                def project(half):
                    if projects:
                        piece_low(2 * u + (6 + half), ((k + 3) // 2) % 2, (k + 1) % 2, half)

                def outputs(g):
                    if not (isinstance(u, int) and u == 0):
                        outputs_out(u - 1, k, g, t + (k - 1) // 4)

                maximum(0)
                project(0)
                maximum(1)
                maximum(2)
                project(1)
                maximum(3)
                outputs(0)
                maximum(4)
                maximum(5)
                maximum(6)
                maximum(7)
                outputs(1)
                if takes_maxima:
                    max_rows(u + 1, set_of(k, 1))

            nc.vector.memset(minus_half[:, :], -0.5).then_inc(half_ready, 1)
            nc.vector.memset(ones[:, :], 1.0).then_inc(ones_ready, 1)
            def first_stats(c):
                dve.wait_ge(x_in[c], 16)
                chunk_stats(c)

            first_stats(0)
            first_stats(1)
            chunk_norm(0)
            first_stats(2)
            chunk_norm(1)
            first_stats(3)
            chunk_low(0)
            dve.wait_ge(l1r_full, 1)
            nc.vector.tensor_scalar(l1_rows[:, :], bank(PVB)[:, 0:OB], TINY, 1.0 / F16_TOP, ALU.add, ALU.mult).then_inc(o_ready, 1)
            dve.wait_ge(o_ready, 1)
            nc.vector.reciprocal(gain_rows[:, :], l1_rows[:, :]).then_inc(gain_made, 1)
            chunk_norm(2)
            chunk_low(1)
            dve.wait_ge(gain_made, 1)
            nc.vector.tensor_tensor(wv_abs[:, :].rearrange("p (k q) -> p k q", k=OB), ident[:, :].unsqueeze(1).to_broadcast([P, OB, P]),
                                    gain_rows[:, :].unsqueeze(2).to_broadcast([P, OB, P]), ALU.mult).then_inc(gain_diag, 1)
            chunk_norm(3)
            chunk_low(2)
            for n in range(4):
                piece_low(n, 0, n // 2, n % 2, FIRST_BANKS[n])
                if n == 1:
                    dve.wait_ge(gain_full, 1)
                    nc.vector.tensor_tensor(wv_raw[:, :], psum[:, MAXB * BANK:(MAXB + 2) * BANK], wv_raw[:, :], ALU.mult).then_inc(wv_scaled, 1)
                if n == 2:
                    dve.wait_ge(wv_hi_done, 1)
                    nc.vector.tensor_tensor(wv_lo[:, :], wv_raw[:, :], wv_hi[:, :], ALU.subtract).then_inc(wv_lo_done, 1)
            for n in range(2 * TILES):
                dve.wait_ge(v_hi_done, n + 1)
                stage = v_stage[n // QT % 2]
                nc.vector.tensor_tensor(stage[:, :, n % QT, 0:DH], bank(n % ST_RING).rearrange("p (h d) -> p h d", d=DH),
                                        stage[:, :, n % QT, DH:2 * DH], ALU.subtract).then_inc(v_lo_done, 1)
                if n == 0:
                    chunk_low(CHUNKS - 1)
                if n == BIAS_AT:
                    dve.wait_ge(bo_full, 1)
                    nc.vector.tensor_tensor(bo_all[:, :], bank(PVB + 1)[:, 0:1], bo_sb[:, :], ALU.add).then_inc(o_ready, 1)
                if n in PIECE_AT:
                    m = 4 + PIECE_AT.index(n)
                    piece_low(m, 1, m % 4 // 2, m % 2)
                if n in FIRST_MAX_AT:
                    m = FIRST_MAX_AT.index(n)
                    if m == 0:
                        dve.wait_ge(tri_ready, 2)
                    take_max(0, 0, m)
                if n == FIRST_ROWS_AT:
                    dve.wait_ge(diag_ready, 1)
                    dve.wait_ge(rows_ready, 1)
                    max_rows(0, 0)
            dve_slot(0, 0, False, True)
            with dve.Fori(0, LOOPS) as t:
                for k in range(1, 5):
                    dve_slot(t, k, True, True)
            for k in LAST_SLOTS:
                dve_slot(LOOPS, k, False, k < 3)
            for g in range(NG):
                outputs_out(HEADS - 1, 4, g, LOOPS)

            def add_result(n):
                c = n % CHUNKS
                dve.wait_ge(yt_full, n + 1)
                tiles = slice(CT * c, CT * (c + 1))
                nc.vector.tensor_tensor(x_sb[:, tiles, :], bank(5).rearrange("p (t e) -> p t e", e=E), x_sb[:, tiles, :], ALU.add)\
                    .then_inc(res_done, 1)

            for n in range(OB * CHUNKS):
                c, blk = divmod(n, OB)
                r = n % BLOCKS
                dve.wait_ge(ot_hi_done, n + 1)
                nc.vector.tensor_tensor(oT_lo[:, r, :], bank(BLOCK_BANKS[r]), oT_hi[:, r, :], ALU.subtract).then_inc(ot_lo_done, 1)
                if blk == 2 and c == 1:
                    dve.wait_ge(attn_b_in, 48)
                    dve.wait_ge(l1b_made, 1)
                    nc.vector.tensor_scalar(l1_b[:, 1:2], l1_b[:, 0:1], TINY, 1.0 / F16_TOP, ALU.add, ALU.mult).then_inc(l1b_made, 1)
                    dve.wait_ge(l1b_made, 2)
                    nc.vector.reciprocal(l1_b[:, 2:3], l1_b[:, 1:2]).then_inc(l1b_made, 1)
                    nc.vector.tensor_scalar(diag_b[:, :], ident[:, :], l1_b[:, 1:2], None, ALU.mult).then_inc(diagb_made, 1)
                    dve.wait_ge(l1b_made, 3)
                    nc.vector.tensor_scalar(wv2_abs[:, :], wv2_raw[:, :], l1_b[:, 2:3], None, ALU.mult).then_inc(wv2_scaled, 1)
                if blk == 2 and c == 2:
                    dve.wait_ge(bias_made, 2)
                    nc.vector.tensor_scalar(bias_s[:, :], bias_s[:, :], slope_sb[:, 0:1], None, ALU.mult).then_inc(steps_b, 1)
                    nc.vector.tensor_scalar(bias_t[:, :], bias_t[:, :], slope_sb[:, 0:1], None, ALU.mult).then_inc(steps_b, 1)
                if blk == 5 and c == 2:
                    dve.wait_ge(wqk_hi_done, 1)
                    nc.vector.tensor_tensor(wqk_lo[:, :], wqk_raw[:, :], wqk_hi[:, :], ALU.subtract).then_inc(wqk_split, 1)
                    dve.wait_ge(wv2_hi_done, 1)
                    nc.vector.tensor_tensor(wv2_lo[:, :], bank(6)[:, 0:P], wv2_hi[:, :], ALU.subtract).then_inc(wv2_split, 1)
                    dve.wait_ge(l1c_full, 1)
                    nc.vector.tensor_copy(l1_cols[:, :], bank(7)[:, 0:P]).then_inc(l1c_done, 1)
                if blk == 5 and c >= 1:
                    add_result(c - 1)
                if blk == 6 and c >= 1 and c < CHUNKS - 1:
                    dve.wait_ge(res_done, c)
                    chunk_stats(CHUNKS + c - 1)
                if c == CHUNKS - 1 and blk in (3, 4):
                    chunk_norm(CHUNKS + blk - 3)
            chunk_low(CHUNKS)

            def feed_forward(layer):
                f0 = FW * CHUNKS * layer
                ln = CHUNKS * (1 + 2 * layer)
                for n in range(FW * CHUNKS):
                    c, m = divmod(n, FW)
                    r = n % BLOCKS
                    dve.wait_ge(h32_done, f0 + n + 1)
                    dve.wait_ge(h_hi_done, f0 + n + 1)
                    nc.vector.tensor_tensor(h_lo[:, r, :], h32[:, r, :], h_hi[:, r, :], ALU.subtract).then_inc(h_lo_done, 1)
                    if layer == 1:
                        outputs_of(B - 1, OB_AT[n])
                    y = CHUNKS * (1 + layer) + c
                    if m == 0 and layer == 0:
                        dve.wait_ge(res_done, y - 1)
                        chunk_stats(CHUNKS + y - 2)
                    if m == 2:
                        if layer == 0 or c + 1 < CHUNKS:
                            chunk_low(ln + c + 1)
                        if layer == 0 or c + 2 < CHUNKS:
                            chunk_norm(ln + c + 2)
                    if m == 3 and not (layer == 1 and c == 0):
                        add_result(y - 1)

            feed_forward(0)

            def take_max_b(b, n):
                j = QT - 1 - n
                cols = P * (j + 1)
                dve.wait_ge(maxb_full, QT * b + n + 1)
                nc.vector.tensor_tensor_reduce(out=junk_b[:, 0:cols], in0=psum[:, 2 * BANK:2 * BANK + cols], in1=bias_s[:, S - cols:S],
                                               scale=1.0, scalar=-3.0e38, op0=ALU.add, op1=ALU.max,
                                               accum_out=max_b[:, b, j:j + 1]).then_inc(maxb_done, 1)

            def max_rows_b(b):
                dve.wait_ge(mtb_full, b + 1)
                nc.vector.tensor_tensor(qm_b[0:QT, b, :].rearrange("p (j q) -> p j q", j=QT),
                                        bank(1)[0:QT, 0:P].unsqueeze(1).to_broadcast([QT, QT, P]),
                                        neg_diag_b[:, :].unsqueeze(2).to_broadcast([QT, QT, P]), ALU.mult).then_inc(mrowb_done, 1)

            for c in range(CHUNKS):
                if c == 0:
                    dve.wait_ge(res_done, 2 * CHUNKS - 1)
                    chunk_stats(3 * CHUNKS - 2)
                    add_result(2 * CHUNKS - 1)
                cols = slice(BANK * c, BANK * (c + 1))
                dve.wait_ge(qb_hi_done, c + 1)
                nc.vector.scalar_tensor_tensor(out=qb_lo[:, cols], in0=bank(QB_BANKS[c % 2]), scalar=SCALE_B, in1=qb_hi[:, cols],
                                               op0=ALU.mult, op1=ALU.subtract).then_inc(qb_lo_done, 1)
                for n in MAX_B_AT[c][0]:
                    take_max_b(0, n)
                if c + 1 < CHUNKS:
                    chunk_low(2 * CHUNKS + c + 1)
                if c == 0:
                    dve.wait_ge(res_done, 2 * CHUNKS)
                    chunk_stats(3 * CHUNKS - 1)
                if c == 1:
                    dve.wait_ge(bias_ready, 2)
                for n in MAX_B_AT[c][1]:
                    take_max_b(0, n)
                if c == CHUNKS - 1:
                    dve.wait_ge(rows_b, 3)
                    max_rows_b(0)
                if c + 2 < CHUNKS:
                    chunk_norm(2 * CHUNKS + c + 2)
                dve.wait_ge(v2_hi_done, c + 1)
                tiles = slice(CT * c, CT * (c + 1))
                nc.vector.tensor_tensor(v2_sb[:, tiles, 0:E], bank(V2_BANKS[c % 2]).rearrange("p (t e) -> p t e", e=E),
                                        v2_sb[:, tiles, E:2 * E], ALU.subtract).then_inc(v2_lo_done, 1)
                for n in MAX_B_AT[c][2]:
                    take_max_b(0, n)

            def biased(b, r):
                m = NU * b + r
                dve.wait_ge(sb_full, m + 1)
                if m >= 3:
                    dve.wait_ge(phib_done, m - 2)
                for i, q0, n, col in units[r]:
                    c0 = q0 - P * i
                    last = nc.vector.tensor_tensor(s32[:, m % 3, col:col + n], bank(st_bank[m % ST_RING])[:, col:col + n], bias_t[:, c0:c0 + n], ALU.add)
                last.then_inc(s32_done, 1)

            st_bank = (0, 5, 4)

            def output_b(b, j):
                m = QT * b + j
                src = bank(OB_BANKS[b][j % 2], V2W)
                dve.wait_ge(pvb_done, m + 1)
                nc.vector.reciprocal(ob_den[:, m % 2:m % 2 + 1], src[:, E:V2W]).then_inc(ob_inverse, 1)
                if m % CT:
                    add_output(m - 1)
                dve.wait_ge(ob_inverse, m + 1)
                nc.vector.scalar_tensor_tensor(out=ob_out[:, m % 2, :], in0=src[:, 0:E], scalar=ob_den[:, m % 2:m % 2 + 1],
                                               in1=l1_cols[:, :], op0=ALU.mult, op1=ALU.mult).then_inc(ob_read, 1)
                if m % CT == CT - 1:
                    add_output(m)
                    dve.wait_ge(resb_done, m + 1)
                    chunk_stats(3 * CHUNKS + m // CT)

            def add_output(m):
                dve.wait_ge(ob_read, m + 1)
                nc.vector.tensor_tensor(x_sb[:, m, :], ob_out[:, m % 2, :], x_sb[:, m, :], ALU.add).then_inc(resb_done, 1)

            def outputs_of(b, steps):
                for step in steps:
                    for j, kt in PV_PAIRS[PV_STEP * step:PV_STEP * (step + 1)]:
                        if kt == j:
                            output_b(b, j)

            for b in range(B):
                for step in range(NU):
                    biased(b, step)
                    if b + 1 < B:
                        for n in MAX_B_NEXT[step]:
                            take_max_b(b + 1, n)
                        if step == NU - 2:
                            max_rows_b(b + 1)
                    if b >= 1:
                        outputs_of(b - 1, (step,))
                    if b == B - 1 and step == NORM_STEP:
                        chunk_norm(3 * CHUNKS)
            chunk_low(3 * CHUNKS)
            outputs_of(B - 1, OB_FIRST)
            chunk_norm(3 * CHUNKS + 1)
            feed_forward(1)
            add_result(3 * CHUNKS - 1)

        @block.gpsimd
        def _(pool):
            nc.gpsimd.memset(ident[:, :], 0.0).then_inc(zeroed, 1)
            nc.gpsimd.memset(ident_b[:, :], 0.0).then_inc(zeroed, 1)
            pool.wait_ge(zeroed, 2)
            for i in (ident, ident_b):
                nc.gpsimd.affine_select(out=i[:, :], in_=i[:, :], compare_op=ALU.not_equal, fill=1.0, base=0,
                                        pattern=[[-1, P]], channel_multiplier=1).then_inc(ident_ready, 1)

            nc.gpsimd.memset(k_l1[:, :, :].bitcast(F32), 0.0).then_inc(zeroed, 1)

            def chunk_rstd(n):
                c = n % CHUNKS
                cols = slice(CT * c, CT * (c + 1))
                pool.wait_ge(aggr_done, n + 1)
                nc.gpsimd.tensor_scalar(var_eps[:, cols], mean_var[:, cols, 1], EPS, None, ALU.add).then_inc(eps_done, 1)
                pool.wait_ge(eps_done, n + 1)
                nc.gpsimd.tensor_tensor(rstd[:, cols], var_eps[:, cols], minus_half[:, :], ALU.pow).then_inc(rstd_done, 1)

            def split_low(pair, par):
                pool.wait_ge(split_hi, pair + 1)
                nc.gpsimd.tensor_tensor(w_lo[:, par, :, :], w_raw[:, :, :], w_hi[:, par, :, :], ALU.subtract).then_inc(split_lo, 1)

            pool.wait_ge(half_ready, 1)
            for c in range(CHUNKS):
                chunk_rstd(c)
                if c == 1:
                    split_low(0, 0)
            nc.gpsimd.memset(q_hm[:, :, :].bitcast(F32), 0.0).then_inc(zeroed, 1)
            pool.wait_ge(zeroed, 4)
            pool.wait_ge(rstd_done, CHUNKS)
            nc.gpsimd.memset(k_l1[DH:DH + QT, :, :].bitcast(F32), 1.0).then_inc(rows_ready, 1)
            pool.wait_ge(rows_ready, 1)
            nc.gpsimd.memset(mask_s[:, :], 0.0).then_inc(zeroed, 1)
            nc.gpsimd.memset(mask_t[:, :], 0.0).then_inc(zeroed, 1)
            nc.gpsimd.memset(neg_diag[:, :], 0.0).then_inc(zeroed, 1)
            pool.wait_ge(zeroed, 7)
            split_low(1, 1)
            for s in v_stage:
                last = nc.gpsimd.memset(s[:, :, :, 2 * DH:VP], 1.0)
            last.then_inc(v_one, 1)
            nc.gpsimd.affine_select(out=mask_s[:, S - P:S], in_=mask_s[:, S - P:S], compare_op=ALU.is_ge, fill=NEG, base=0,
                                    pattern=[[-1, P]], channel_multiplier=1).then_inc(tri_ready, 1)
            nc.gpsimd.affine_select(out=mask_t[:, :], in_=mask_t[:, :], compare_op=ALU.is_ge, fill=NEG, base=0,
                                    pattern=[[1, P]], channel_multiplier=-1).then_inc(tri_ready, 1)
            nc.gpsimd.affine_select(out=neg_diag[:, :], in_=neg_diag[:, :], compare_op=ALU.not_equal, fill=-1.0, base=0,
                                    pattern=[[-1, QT]], channel_multiplier=1).then_inc(diag_ready, 1)
            pool.wait_ge(bo_full, 1)
            pool.wait_ge(o_ready, 1)
            nc.gpsimd.tensor_tensor(wo_raw[:, :, :], wo_raw[:, :, :], l1_rows[:, :].unsqueeze(2).to_broadcast([P, OB, E]), ALU.mult)\
                .then_inc(wo_scaled, 1)
            for n, (lo, raw, hi) in enumerate(((wo_lo, wo_raw, wo_hi), (w1_lo, w1_raw, w1_hi), (w2_lo, w2_raw, w2_hi))):
                pool.wait_ge(wts_hi_done, n + 1)
                nc.gpsimd.tensor_tensor(lo[:], raw[:], hi[:], ALU.subtract).then_inc(wts_lo_done, 1)

            def low(u, k, r):
                pool.wait_ge(exp_done, NU * u + (r + 1))
                pool.wait_ge(phi_done, NU * u + (r + 1))
                cols = slice(BANK * r, BANK * (r + 1))
                nc.gpsimd.tensor_tensor(p_hl[:, k % 2, 1, cols], p32[:, ring_at(k, r), :], p_hl[:, k % 2, 0, cols], ALU.subtract)\
                    .then_inc(plo_done, 1)

            def pool_slot(t, k, split):
                u = 4 * t + k
                for r in range(NU):
                    low(u, k, r)
                    if split and r == 2:
                        split_low(2 * t + (k + 4) // 2, ((k + 4) // 2) % 2)

            pool_slot(0, 0, True)
            with pool.Fori(0, LOOPS) as t:
                for k in range(1, 5):
                    pool_slot(t, k, k % 2 == 0)
            for k in LAST_SLOTS:
                pool_slot(LOOPS, k, False)

            pool.wait_ge(o_ready, SUMS + NG * HEADS)
            for n in range(2):
                pool.wait_ge(scratch_out[n], 16 * (V_STORES + PAIRS // 2))
            nc.gpsimd.iota(bias_s[:, :], pattern=[[1, S]], base=P - S, channel_multiplier=-1,
                           allow_small_or_imprecise_dtypes=True).then_inc(bias_made, 1)
            nc.gpsimd.iota(bias_t[:, :], pattern=[[-1, S]], base=0, channel_multiplier=1,
                           allow_small_or_imprecise_dtypes=True).then_inc(bias_made, 1)
            nc.gpsimd.memset(qm_b[:, :, :].bitcast(F32), 0.0).then_inc(rows_b, 1)
            nc.gpsimd.memset(k_one[:, :].bitcast(F32), 0.0).then_inc(zeroed, 1)
            nc.gpsimd.memset(neg_diag_b[:, :], 0.0).then_inc(zeroed, 1)
            nc.gpsimd.memset(v2_sb[:, :, 2 * E:V2P], 1.0).then_inc(v2_one, 1)
            pool.wait_ge(zeroed, 9)
            nc.gpsimd.memset(k_one[0:QT, :].bitcast(F32), 1.0).then_inc(rows_b, 1)
            nc.gpsimd.affine_select(out=neg_diag_b[:, :], in_=neg_diag_b[:, :], compare_op=ALU.not_equal, fill=-1.0, base=0,
                                    pattern=[[-1, QT]], channel_multiplier=1).then_inc(rows_b, 1)
            for c in range(CHUNKS):
                chunk_rstd(CHUNKS + c)
                if c == 0:
                    pool.wait_ge(attn_b_in, 48)
            pool.wait_ge(steps_b, 2)
            nc.gpsimd.affine_select(out=bias_s[:, :], in_=bias_s[:, :], compare_op=ALU.is_ge, fill=NEG, base=S - P,
                                    pattern=[[-1, S]], channel_multiplier=1).then_inc(bias_ready, 1)
            nc.gpsimd.affine_select(out=bias_t[:, :], in_=bias_t[:, :], compare_op=ALU.is_ge, fill=NEG, base=0,
                                    pattern=[[1, S]], channel_multiplier=-1).then_inc(bias_ready, 1)
            for c in range(CHUNKS):
                chunk_rstd(2 * CHUNKS + c)
            for m in range(NU * B):
                b, cols = m // NU, slice(BANK * (m % NU), BANK * (m % NU + 1))
                pool.wait_ge(expb_done, m + 1)
                pool.wait_ge(phib_done, m + 1)
                nc.gpsimd.tensor_tensor(p_hlb[:, b, 1, cols], p32b[:, m % RING, :], p_hlb[:, b, 0, cols], ALU.subtract)\
                    .then_inc(plob_done, 1)
                if m == NU + NORM_STEP - 2:
                    chunk_rstd(3 * CHUNKS)
            for c in range(1, CHUNKS):
                chunk_rstd(3 * CHUNKS + c)


_INS = ['L0_attn_a_x', 'L0_attn_a_Wq', 'L0_attn_a_Wk', 'L0_attn_a_Wv', 'L0_attn_a_bq', 'L0_attn_a_bk', 'L0_attn_a_bv',
        'L0_attn_a_Wo', 'L0_attn_a_bo', 'L0_attn_b_W_qk', 'L0_attn_b_W_v', 'L0_attn_b_alibi_slope',
        'L0_ffn_w1', 'L0_ffn_b1', 'L0_ffn_w2', 'L0_ffn_b2']
_OUT = ((2, 1024, 128), 'float32')


def kernel(**inputs):
    import numpy as _np
    import concourse.bacc as _bacc
    from concourse import mybir as _mybir
    from concourse.bass_utils import run_bass_kernel_spmd as _run

    nc = _bacc.Bacc("TRN2", target_bir_lowering=False, num_devices=1)
    arrays, args = {}, []
    for name in _INS:
        a = _np.ascontiguousarray(inputs[name])
        arrays[f"in_{name}"] = a
        args.append(nc.dram_tensor(f"in_{name}", a.shape, _mybir.dt.from_np(a.dtype), kind="ExternalInput").ap())
    shape, dtype = _OUT
    args.append(nc.dram_tensor("out_0", shape, _mybir.dt.from_np(_np.dtype(dtype)), kind="ExternalOutput").ap())
    hybrid_block(nc, *args)
    r = _run(nc, [arrays], core_ids=[0])
    return r.results[0]["out_0"]
```
